# Optimizing a Trainium2 kernel written in Bass

```python
import numpy as np
import jax
import jax.numpy as jnp

def _softmax(x, axis=-1):
    return jax.nn.softmax(x, axis=axis)

def _gelu(x):
    return jax.nn.gelu(x, approximate=True)

def _silu(x):
    return jax.nn.silu(x)

def _sigmoid(x):
    return jax.nn.sigmoid(x)

def _layernorm(x, axis=-1, eps=1e-05):
    m = jnp.mean(x, axis=axis, keepdims=True)
    v = jnp.var(x, axis=axis, keepdims=True)
    return (x - m) / jnp.sqrt(v + eps)

def _scatter_add(tgt, idx, src, axis=0):
    return tgt.at[idx].add(src)

def _segment_sum(src, seg, n):
    return jax.ops.segment_sum(src, seg, n)
kernel_name = 'mk_macaron_d2_jaxref_r8_38493a'

def setup_inputs(seed: int=0):
    np.random.seed(seed)
    _w = jnp.asarray

    def _L0_attn_setup():
        import jax, jax.numpy as jnp
        import numpy as np
        N_HEADS = 16

        def _alibi_causal_mask(T, n_heads, dtype):
            slopes = (1.0 / jnp.power(2.0, jnp.arange(1, n_heads + 1, dtype=dtype)))[:, None, None]
            idx = jnp.arange(T)
            rel = (idx[None, :] - idx[:, None]).astype(dtype)
            alibi = jnp.tril(rel)
            causal = jnp.where(idx[None, :] > idx[:, None], -jnp.inf, 0.0).astype(dtype)
            return (alibi + causal)[None, :, :] * slopes
        key = jax.random.key(seed)
        ks = jax.random.split(key, 5)
        B, T, C = (2, 256, 128)
        scale = 0.02
        return {'x': jax.random.normal(ks[0], (B, T, C), dtype=jnp.float32), 'W_attn': jax.random.normal(ks[1], (C, 3 * C), dtype=jnp.float32) * scale, 'b_attn': jax.random.normal(ks[2], (3 * C,), dtype=jnp.float32) * scale, 'W_proj': jax.random.normal(ks[3], (C, C), dtype=jnp.float32) * scale, 'b_proj': jax.random.normal(ks[4], (C,), dtype=jnp.float32) * scale}
    _L0_attn_in = _L0_attn_setup()

    def _L0_ffn_setup():
        import jax, jax.numpy as jnp
        import numpy as np
        D_MODEL = 128
        FFN = 128
        N_EXPERTS = 8
        N_SHARED = 1
        TOP_K = 2
        B, S = (2, 256)

        def _swiglu(h):
            a, b = jnp.split(h, 2, axis=-1)
            return jax.nn.silu(a) * b
        key = jax.random.key(seed)
        ks = jax.random.split(key, 12)
        sc = 0.02
        return {'x': jax.random.normal(ks[0], (B, S, D_MODEL), dtype=jnp.float32), 'gate_w': jax.random.normal(ks[1], (D_MODEL, N_EXPERTS), dtype=jnp.float32) * sc, 'gate_b': jnp.zeros((N_EXPERTS,), dtype=jnp.float32), 'sw1': jax.random.normal(ks[2], (N_SHARED, D_MODEL, 2 * FFN), dtype=jnp.float32) * sc, 'sb1': jnp.zeros((N_SHARED, 2 * FFN), dtype=jnp.float32), 'sw2': jax.random.normal(ks[3], (N_SHARED, FFN, D_MODEL), dtype=jnp.float32) * sc, 'sb2': jnp.zeros((N_SHARED, D_MODEL), dtype=jnp.float32), 'rw1': jax.random.normal(ks[4], (N_EXPERTS, D_MODEL, 2 * FFN), dtype=jnp.float32) * sc, 'rb1': jnp.zeros((N_EXPERTS, 2 * FFN), dtype=jnp.float32), 'rw2': jax.random.normal(ks[5], (N_EXPERTS, FFN, D_MODEL), dtype=jnp.float32) * sc, 'rb2': jnp.zeros((N_EXPERTS, D_MODEL), dtype=jnp.float32)}
    _L0_ffn_in = _L0_ffn_setup()

    def _L1_attn_setup():
        import jax, jax.numpy as jnp
        import numpy as np
        H = 16
        WIN = 64
        key = jax.random.key(seed)
        ks = jax.random.split(key, 4)
        B, S, D = (1, 512, 128)
        s = 1.0 / np.sqrt(D)
        x = jax.random.normal(ks[0], (B, S, D), jnp.float32)
        Wqkv = jax.random.normal(ks[1], (3 * D, D), jnp.float32) * s
        bqkv = jnp.zeros((3 * D,), jnp.float32)
        Wout = jax.random.normal(ks[2], (D, D), jnp.float32) * s
        bout = jnp.zeros((D,), jnp.float32)
        return {'x': x, 'Wqkv': Wqkv, 'bqkv': bqkv, 'Wout': Wout, 'bout': bout}
    _L1_attn_in = _L1_attn_setup()

    def _L1_ffn_setup():
        import jax, jax.numpy as jnp
        import numpy as np
        DIM = 128
        HIDDEN = 512
        E = 8
        B, S = (2, 512)
        key = jax.random.key(seed)
        ks = jax.random.split(key, 8)
        sd = 1.0 / np.sqrt(DIM)
        sh = 1.0 / np.sqrt(HIDDEN)
        return {'x': jax.random.normal(ks[0], (B, S, DIM), dtype=jnp.float32), 'router_w': jax.random.uniform(ks[1], (DIM, E), jnp.float32, -sd, sd), 'router_b': jax.random.uniform(ks[2], (E,), jnp.float32, -sd, sd), 'w1': jax.random.uniform(ks[3], (E, DIM, 2 * HIDDEN), jnp.float32, -sd, sd), 'b1': jax.random.uniform(ks[4], (E, 2 * HIDDEN), jnp.float32, -sd, sd), 'w2': jax.random.uniform(ks[5], (E, HIDDEN, DIM), jnp.float32, -sh, sh), 'b2': jax.random.uniform(ks[6], (E, DIM), jnp.float32, -sh, sh)}
    _L1_ffn_in = _L1_ffn_setup()
    _d = {'L0_attn_x': _L0_attn_in['x'], 'L0_attn_W_attn': _L0_attn_in['W_attn'], 'L0_attn_b_attn': _L0_attn_in['b_attn'], 'L0_attn_W_proj': _L0_attn_in['W_proj'], 'L0_attn_b_proj': _L0_attn_in['b_proj'], 'L0_ffn_gate_w': _L0_ffn_in['gate_w'], 'L0_ffn_gate_b': _L0_ffn_in['gate_b'], 'L0_ffn_sw1': _L0_ffn_in['sw1'], 'L0_ffn_sb1': _L0_ffn_in['sb1'], 'L0_ffn_sw2': _L0_ffn_in['sw2'], 'L0_ffn_sb2': _L0_ffn_in['sb2'], 'L0_ffn_rw1': _L0_ffn_in['rw1'], 'L0_ffn_rb1': _L0_ffn_in['rb1'], 'L0_ffn_rw2': _L0_ffn_in['rw2'], 'L0_ffn_rb2': _L0_ffn_in['rb2'], 'L1_attn_Wqkv': _L1_attn_in['Wqkv'], 'L1_attn_bqkv': _L1_attn_in['bqkv'], 'L1_attn_Wout': _L1_attn_in['Wout'], 'L1_attn_bout': _L1_attn_in['bout'], 'L1_ffn_router_w': _L1_ffn_in['router_w'], 'L1_ffn_router_b': _L1_ffn_in['router_b'], 'L1_ffn_w1': _L1_ffn_in['w1'], 'L1_ffn_b1': _L1_ffn_in['b1'], 'L1_ffn_w2': _L1_ffn_in['w2'], 'L1_ffn_b2': _L1_ffn_in['b2']}
    _x0 = _d['L0_attn_x']
    _d['L0_attn_x'] = jax.random.normal(jax.random.fold_in(jax.random.key(seed), 1), (8, 256, 128), dtype=_x0.dtype)
    del _x0
    return _d

def reference(L0_attn_x, L0_attn_W_attn, L0_attn_b_attn, L0_attn_W_proj, L0_attn_b_proj, L0_ffn_gate_w, L0_ffn_gate_b, L0_ffn_sw1, L0_ffn_sb1, L0_ffn_sw2, L0_ffn_sb2, L0_ffn_rw1, L0_ffn_rb1, L0_ffn_rw2, L0_ffn_rb2, L1_attn_Wqkv, L1_attn_bqkv, L1_attn_Wout, L1_attn_bout, L1_ffn_router_w, L1_ffn_router_b, L1_ffn_w1, L1_ffn_b1, L1_ffn_w2, L1_ffn_b2):

    def _L0_attn_ref(x, W_attn, b_attn, W_proj, b_proj):
        import jax, jax.numpy as jnp
        import numpy as np
        N_HEADS = 16

        def _alibi_causal_mask(T, n_heads, dtype):
            slopes = (1.0 / jnp.power(2.0, jnp.arange(1, n_heads + 1, dtype=dtype)))[:, None, None]
            idx = jnp.arange(T)
            rel = (idx[None, :] - idx[:, None]).astype(dtype)
            alibi = jnp.tril(rel)
            causal = jnp.where(idx[None, :] > idx[:, None], -jnp.inf, 0.0).astype(dtype)
            return (alibi + causal)[None, :, :] * slopes
        B, T, C = x.shape
        H = N_HEADS
        D = C // H
        qkv = x @ W_attn + b_attn
        q, k, v = jnp.split(qkv, 3, axis=-1)
        q = q.reshape(B, T, H, D).transpose(0, 2, 1, 3)
        k = k.reshape(B, T, H, D).transpose(0, 2, 1, 3)
        v = v.reshape(B, T, H, D).transpose(0, 2, 1, 3)
        att = jnp.einsum('bhtd,bhsd->bhts', q, k) / jnp.sqrt(jnp.asarray(D, x.dtype))
        att = att + _alibi_causal_mask(T, H, x.dtype)[None]
        att = jax.nn.softmax(att, axis=-1)
        y = jnp.einsum('bhts,bhsd->bhtd', att, v)
        y = y.transpose(0, 2, 1, 3).reshape(B, T, C)
        return y @ W_proj + b_proj

    def _L0_ffn_ref(x, gate_w, gate_b, sw1, sb1, sw2, sb2, rw1, rb1, rw2, rb2):
        import jax, jax.numpy as jnp
        import numpy as np
        D_MODEL = 128
        FFN = 128
        N_EXPERTS = 8
        N_SHARED = 1
        TOP_K = 2
        B, S = (2, 256)

        def _swiglu(h):
            a, b = jnp.split(h, 2, axis=-1)
            return jax.nn.silu(a) * b
        hs = jnp.einsum('bsd,ndf->nbsf', x, sw1) + sb1[:, None, None, :]
        shared_out = jnp.einsum('nbsf,nfd->bsd', _swiglu(hs), sw2) + sb2.sum(0)
        probs = jax.nn.softmax(x @ gate_w + gate_b, axis=-1)
        topk_probs, topk_idx = jax.lax.top_k(probs, TOP_K)
        cw = jnp.sum(jax.nn.one_hot(topk_idx, N_EXPERTS, dtype=x.dtype) * topk_probs[..., None], axis=2)
        hr = jnp.einsum('bsd,edf->ebsf', x, rw1) + rb1[:, None, None, :]
        out_e = jnp.einsum('ebsf,efd->ebsd', _swiglu(hr), rw2) + rb2[:, None, None, :]
        routed_out = jnp.einsum('ebsd,bse->bsd', out_e, cw)
        return shared_out + routed_out

    def _L1_attn_ref(x, Wqkv, bqkv, Wout, bout):
        import jax, jax.numpy as jnp
        import numpy as np
        H = 16
        WIN = 64
        B, S, D = x.shape
        d = D // H
        pads = WIN // 2
        C = WIN
        N = S // C
        L = C + WIN - 1
        qkv = (x @ Wqkv.T + bqkv).reshape(B, S, 3, H, d).transpose(2, 0, 3, 1, 4)
        q, k, v = (qkv[0], qkv[1], qkv[2])
        kp = jnp.pad(k, ((0, 0), (0, 0), (pads, pads), (0, 0)))
        vp = jnp.pad(v, ((0, 0), (0, 0), (pads, pads), (0, 0)))
        idx = jnp.arange(N)[:, None] * C + jnp.arange(L)[None, :]
        kb = kp[:, :, idx, :]
        vb = vp[:, :, idx, :]
        qc = q.reshape(B, H, N, C, d)
        scores = jnp.einsum('bhncd,bhnld->bhncl', qc, kb) / np.sqrt(d).astype(np.float32)
        c = jnp.arange(C)[:, None]
        j = jnp.arange(L)[None, :]
        band = (j >= c) & (j < c + WIN)
        scores = jnp.where(band, scores, -jnp.inf)
        attn = jax.nn.softmax(scores, axis=-1)
        o = jnp.einsum('bhncl,bhnld->bhncd', attn, vb).reshape(B, H, S, d)
        o = o.transpose(0, 2, 1, 3).reshape(B, S, D)
        return o @ Wout.T + bout

    def _L1_ffn_ref(x, router_w, router_b, w1, b1, w2, b2):
        import jax, jax.numpy as jnp
        import numpy as np
        DIM = 128
        HIDDEN = 512
        E = 8
        B, S = (2, 512)
        logits = jnp.einsum('bsd,de->bse', x, router_w) + router_b
        probs = jax.nn.softmax(logits, axis=-1)
        top1 = jnp.argmax(probs, axis=-1)
        out = jnp.zeros_like(x)
        for i in range(E):
            h = jnp.einsum('bsd,df->bsf', x, w1[i]) + b1[i]
            a, g = jnp.split(h, 2, axis=-1)
            y = jnp.einsum('bsh,hd->bsd', a * jax.nn.sigmoid(g), w2[i]) + b2[i]
            out = out + jnp.where((top1 == i)[..., None], y, 0.0)
        return out
    x = L0_attn_x
    x = x + 0.5 * _L0_ffn_ref(_layernorm(x, axis=-1), L0_ffn_gate_w, L0_ffn_gate_b, L0_ffn_sw1, L0_ffn_sb1, L0_ffn_sw2, L0_ffn_sb2, L0_ffn_rw1, L0_ffn_rb1, L0_ffn_rw2, L0_ffn_rb2)
    x = x + _L0_attn_ref(_layernorm(x, axis=-1), L0_attn_W_attn, L0_attn_b_attn, L0_attn_W_proj, L0_attn_b_proj)
    x = x + 0.5 * _L0_ffn_ref(_layernorm(x, axis=-1), L0_ffn_gate_w, L0_ffn_gate_b, L0_ffn_sw1, L0_ffn_sb1, L0_ffn_sw2, L0_ffn_sb2, L0_ffn_rw1, L0_ffn_rb1, L0_ffn_rw2, L0_ffn_rb2)
    x = x + 0.5 * _L1_ffn_ref(_layernorm(x, axis=-1), L1_ffn_router_w, L1_ffn_router_b, L1_ffn_w1, L1_ffn_b1, L1_ffn_w2, L1_ffn_b2)
    x = x + _L1_attn_ref(_layernorm(x, axis=-1), L1_attn_Wqkv, L1_attn_bqkv, L1_attn_Wout, L1_attn_bout)
    x = x + 0.5 * _L1_ffn_ref(_layernorm(x, axis=-1), L1_ffn_router_w, L1_ffn_router_b, L1_ffn_w1, L1_ffn_b1, L1_ffn_w2, L1_ffn_b2)
    return x

_drawn_inputs = setup_inputs


def setup_inputs(seed=0):
    import zlib

    import numpy as np

    out = dict(_drawn_inputs(seed))
    spreads = {'L0_ffn_gate_b': (0.0, 0.331),
     'L0_ffn_sb1': (0.0, 0.678),
     'L0_ffn_sb2': (0.0, 0.1),
     'L0_ffn_rb1': (0.0, 0.8),
     'L0_ffn_rb2': (0.0, 0.1),
     'L1_attn_bqkv': (0.0, 0.1),
     'L1_attn_bout': (0.0, 0.1)}
    factors = {'L0_attn_W_attn': 2.972,
     'L0_attn_b_attn': 4.677,
     'L0_ffn_sw1': 4.758,
     'L0_ffn_sw2': 4.152,
     'L0_ffn_rw1': 8.0,
     'L0_ffn_rw2': 8.0,
     'L1_ffn_b1': 3.513,
     'L1_ffn_b2': 3.958}
    for name, (base, spread) in spreads.items():
        noise = np.random.default_rng([zlib.crc32(name.encode()), seed]).standard_normal(out[name].shape)
        drawn = base * np.exp(spread * noise) if base else spread * noise
        out[name] = jnp.asarray(drawn.astype(out[name].dtype))
    for name, factor in factors.items():
        out[name] = (out[name] * factor).astype(out[name].dtype)
    return out
```

```python
from contextlib import ExitStack

import concourse.bass as bass
from concourse import mybir

F32 = mybir.dt.float32
F32R = mybir.dt.float32r
F16 = mybir.dt.float16
BF16 = mybir.dt.bfloat16
U32 = mybir.dt.uint32
I32 = mybir.dt.int32
ALU = mybir.AluOpType
ACT = mybir.ActivationFunctionType
AX = mybir.AxisListType

P = 128
NT = 16
NB = 8
SEQ = 256
H = 16
HD = P // H
G = 4
SL = 32
M_SLOT = 26
E = 8
E0 = E + 1
HID = 512
WIN = 64
PAD = WIN // 2
NEG = -1e30
EPS = 1e-5
CH = 4
NS = NT + E - 1
ROUNDS = {"causal": [(0, 0, 0), (0, 0, 1), (1, 0, 0), (1, 1, 0), (1, 0, 1), (1, 1, 1)],
          "window": [(0, 0, 0), (0, 0, 1), (1, 0, 0), (1, 0, 1)]}


class Chain:

    def __init__(self, eng, sem, base=0):
        self.eng, self.sem, self.base, self.n = eng, sem, base, 0

    def step(self, ins):
        self.n += 1
        ins.then_inc(self.sem, 1)

    def wait(self):
        self.eng.wait_ge(self.sem, self.base + self.n)

    def link(self, ins):
        self.step(ins)
        self.wait()


def macaron(nc, d, out, phases=("F0", "A0", "F0", "F1", "A1", "F1")):
    ctx = ExitStack()
    with ctx:
        def sb(name, shape, dt=F32):
            return ctx.enter_context(nc.sbuf_tensor(name, shape, dt))

        def sem(name):
            return ctx.enter_context(nc.semaphore(name))

        X = sb("residual", [P, NT, P])
        ident = sb("ident", [P, P])
        identb = sb("identb", [P, P], BF16)
        masksb = sb("masksb", [P, 4, P], BF16)
        tri = sb("tri", [P, P])
        trib = sb("trib", [P, P], BF16)
        onesb = sb("onesb", [P, P], BF16)
        ones1 = sb("ones1", [1, P])
        em8 = sb("em8", [P, NT, E])
        k128 = sb("k128", [P, E, NT])
        cols = sb("cols", [P, 4])
        valid = sb("valid", [1, SEQ + 2 * PAD])
        small = sb("small", [2 * E, 3 * 16 + NS + 2])
        halfpow = sb("halfpow", [P, NT])
        stage = sb("stage", [P, E0 * 2 * P])
        w1h = sb("w1h", [P, E0, 2 * P], F32R)
        w1l = sb("w1l", [P, E0, 2 * P], F32R)
        b1 = sb("b1", [P, E0, 2])
        w2 = sb("w2", [P, E0, P])
        b2 = sb("b2", [E0, P])
        gate_w = sb("gate_w", [P, E])
        gate_b = sb("gate_b", [1, E])
        wqkh = sb("wqkh", [P, 2, G * P], F32R)
        wqkl = sb("wqkl", [P, 2, G * P], F32R)
        bqk = [sb(f"bqk{a}", [P, 2, G]) for a in range(2)]
        add_qk = sb("add_qk", [P, 2, G, SEQ])
        wv = [sb(f"wv{a}", [P, P]) for a in range(2)]
        bv = [sb(f"bv{a}", [1, P]) for a in range(2)]
        wp = [sb(f"wp{a}", [P, P]) for a in range(2)]
        bp = [sb(f"bp{a}", [1, P]) for a in range(2)]
        v1h = sb("v1h", [P, E, 2 * HID], F32R)
        v1l = sb("v1l", [P, E, 2 * HID], F32R)
        v2 = sb("v2", [P, E, HID // P, P])
        c1hl = sb("c1hl", [2 * E, 2 * HID], F32R)
        c2 = sb("c2", [E, P])
        router_w = sb("router_w", [P, E])
        router_b = sb("router_b", [1, E])
        xn = sb("xn", [P, NT, P])
        masks = xn[:, 4:8, :]
        c1f = xn[0:2 * E, 8:16, :].rearrange("p a c -> p (a c)")
        stats = sb("stats", [P, NT, 6])
        mv = sb("mv", [P, NT, 2])
        ve = sb("ve", [P, NT])
        rstd = sb("rstd", [P, NT])
        xT = sb("xT", [P, CH * P])
        xTp = sb("xTp", [P, SEQ + 2 * PAD])
        xTh = sb("xTh", [P, CH * P], F32R)
        xTl = sb("xTl", [P, CH * P], F32R)
        r8 = [sb(f"r8_{i}", [P, NT, E]) for i in range(4)]
        r1 = [sb(f"r1_{i}", [P, NT]) for i in range(3)]
        cw = sb("cw", [P, CH, E0])
        cwT = sb("cwT", [E0, CH * P])
        big = sb("big", [P, 4 * 2 * G * P])
        prob = big[:].rearrange("p (r j g k) -> p r j g k", r=4, j=2, g=G)
        act_s = big[:, 0:1024].rearrange("p (a b) -> p a b", a=2)
        hid = big[:, 1024:2048].rearrange("p (a b) -> p a b", a=2)
        hT = big[:, 2048:3072].rearrange("p (a b) -> p a b", a=2)
        wqkf = big[:, 3072:4096].rearrange("p (s c) -> p s c", s=2)
        tqk = stage[:, 0:1024].rearrange("p (a g k) -> p a g k", a=2, g=2)
        hqk = stage[:, 1024:1536].bitcast(F16).rearrange("p (a g k) -> p a g k", a=2, g=2)
        q16 = sb("q16", [P, G, SEQ], F16)
        k16 = sb("k16", [P, G, SEQ + 2 * PAD], F16)
        qm16 = sb("qm16", [P, G, SEQ], F16)
        mtmp = sb("mtmp", [P, 2, 2, G, 2])
        mpad = sb("mpad", [P, 2, G, 4, SL])
        vaug = sb("vaug", [P, 4, H, HD + 1])
        rec = sb("rec", [P, 2, H])
        att = sb("att", [P, 2, P])
        attT = sb("attT", [P, 2, P])
        onehot = sb("onehot", [P, NT, E], BF16)
        ohsum = sb("ohsum", [P, 2, E], BF16)
        gtk = sb("gtk", [P, E, NT])
        ntl = sb("ntl", [P, 3, E])
        spare = sb("spare", [P, 1])
        zero8 = sb("zero8", [P, E])
        slotf = sb("slotf", [P, NT])
        slot = sb("slot", [P, NT], U32)
        gtT = sb("gtT", [2 * E, 16])
        ntT = sb("ntT", [2 * E, 1])
        offT = sb("offT", [2 * E, 2])
        cmpT = sb("cmpT", [2 * E, 2, NS])
        ohT = sb("ohT", [2 * E, NS])
        eid = sb("eid", [1, NS], I32)
        oh_tile = sb("oh_tile", [2 * E, 2, P], F32R)
        xg = sb("xg", [P, 2, P])
        xgh = sb("xgh", [P, 2, P], F32R)
        xgl = sb("xgl", [P, 2, P], F32R)
        ysb = att
        PS = ctx.enter_context(nc.psum_tensor("PS", [P, 8, 512], F32))

        xs_dram = nc.dram_tensor("xs_dram", [NS * P, P], F32).ap()
        ys_dram = nc.dram_tensor("ys_dram", [NS * P, P], F32).ap()

        k128T = small[:, 0:16]
        tri_incl = small[:, 16:32]
        tri_excl = small[:, 32:48]
        iota_s = small[:, 48:48 + NS]
        eid_col = small[:, 48 + NS:49 + NS]
        neg_lo16 = small[:, 49 + NS:50 + NS]
        neg_lo = [cols[:, 0:1], cols[:, 1:2]]
        m_one = cols[:, 2:3]

        def tile_of(x, i):
            return x[:, bass.ds(i, 1), :].rearrange("p a c -> p (a c)")

        ld = {n: sem("ld_" + n) for n in ("x", "const", "w1", "f0", "a0", "wqk", "add", "f1", "b1", "stage0", "stage1", "zero")}
        LOADS = {
            "const": [(ident, "c_ident"), (masks, "c_masks"), (tri, "c_tri"), (em8, "c_em8"), (k128, "c_k128"),
                      (cols, "c_cols"), (valid, "c_valid"), (small, "c_small")],
            "f0": [(b1, "b1_0"), (w2, "w2_0"), (b2, "b2_0"), (gate_w, "gate_w"), (gate_b, "gate_b")],
            "a0": [(bqk[0], "bqk_0"), (wv[0], "wv_0"), (bv[0], "bv_0"), (wp[0], "wp_0"), (bp[0], "bp_0"),
                   (bqk[1], "bqk_1"), (wv[1], "wv_1"), (bv[1], "bv_1"), (wp[1], "wp_1"), (bp[1], "bp_1")],
            "f1": [(v2, "w2_1"), (c2, "b2_1"), (router_w, "router_w"), (router_b, "router_b")],
        }
        s_set = sem("setup_dve")
        s_constp = sem("const_pool")
        s_consta = sem("const_act")
        s_constd = sem("const_dve")
        s_w1h = sem("w1_high")
        s_w1l = sem("w1_low")
        s_c1h = sem("c1_high")
        s_c1 = sem("c1_ready")
        s_stage_h = sem("stage_high")
        s_stage_l = sem("stage_low")
        s_out = sem("stored")
        s_zero = sem("zero_ready")

        NAMES = {
            "F0": "ln dln rstd xn tr xt xh xl lgt dch dlg ex cw cwt cwts yb up sg h dn acc",
            "A": "wsc wh wl wadd ln dln rstd xn tr xt xh xl qk t hi qk16 v vs s mt mx mp qm st p pv at atT atS pj acc rec",
            "F1": "ln dln rstd xn tr xt lgt dch oh cnt ntT incl sl offs ohT eidp eid scat xld0 xld1 trx xh xl oht up sg h trh hT dn y yst0 yst1 gat acc",
        }
        by_kind = {kind: {s: sem(f"{kind}_{s}") for s in NAMES["A" if kind[0] == "A" else kind].split()}
                   for kind in sorted(set(phases))}
        ph = [by_kind[kind] for kind in phases]
        nth = [phases[:n].count(kind) for n, kind in enumerate(phases)]
        NTP = ((NS + 1) // 2, NS // 2)
        attn_phases = [n for n, kind in enumerate(phases) if kind[0] == "A"]
        DLG = 2
        NR = {"A0": len(ROUNDS["causal"]), "A1": len(ROUNDS["window"])}

        def x_ready(eng, n):
            if n == 0:
                eng.wait_ge(ld["x"], 16)
            else:
                eng.wait_ge(ph[n - 1]["acc"], (nth[n - 1] + 1) * {
                    "F0": NT // CH * (1 + E0 * CH), "A0": 2 * NB, "A1": 2 * NB, "F1": 4}[phases[n - 1]])

        def slot_tiles(eng, tile):
            tile(0, 0, 0, True)
            tile(1, 1, 0, True)
            with eng.Fori(1, NS // 2) as k:
                tile(k * 2, 0, k, False)
                tile(k * 2 + 1, 1, k, False)
            tile(NS - 1, 0, NS // 2, False)

        block = ctx.enter_context(nc.Block())

        @block.sync
        def _(sp):
            sp.dma_start(X[:], d["x"]).then_inc(ld["x"], 16)
            sp.dma_start(stage[:], d["w1_0"]).then_inc(ld["w1"], 16)
            for group in ("const", "f0", "a0", "f1"):
                for dst, src in LOADS[group]:
                    sp.dma_start(dst if dst is masks else dst[:], d[src]).then_inc(ld[group], 16)
            sp.dma_start(c1f[0:E, :], d["b1_1"]).then_inc(ld["b1"], 16)
            sp.dma_start(c1f[E:2 * E, :], d["b1_1"]).then_inc(ld["b1"], 16)
            if "A0" in phases:
                sp.dma_start(wqkf, d["wqk_0"]).then_inc(ld["wqk"], 16)
            sp.dma_start(add_qk[:], d["c_add_qk"]).then_inc(ld["add"], 16)
            sp.wait_ge(s_zero, 1)
            for a in range(0, NS, 8):
                sp.dma_start(xs_dram.rearrange("(a p) c -> p a c", p=P)[:, a:min(a + 8, NS), :],
                             mpad[:].rearrange("p q g j s -> p (q g) (j s)")[:, 0:min(8, NS - a), :]).then_inc(ld["zero"], 16)
            def load_second():
                for e in range(E):
                    if e >= 2:
                        sp.wait_ge(s_stage_h, e - 1)
                        sp.wait_ge(s_stage_l, e - 1)
                    sp.dma_start(stage[:, (e % 2) * 2 * HID:(e % 2 + 1) * 2 * HID], d["w1_1"][:, e, :])\
                      .then_inc(ld[f"stage{e % 2}"], 16)

            for n, kind in enumerate(phases):
                s, m = ph[n], nth[n]
                if kind == "A1":
                    x_ready(sp, n)
                    sp.dma_start(wqkf, d["wqk_1"]).then_inc(ld["wqk"], 16)
                if kind == "F1":
                    if n == phases.index("F1"):
                        if n:
                            x_ready(sp, n)
                        else:
                            sp.wait_ge(s_w1h, 1)
                            sp.wait_ge(s_w1l, 1)
                        load_second()

                    def tile(i, par, k, first):
                        if not first:
                            sp.wait_ge(s["trx"], NS * m + i - 1)
                        sp.dma_start(xg[:, par, :], xs_dram[bass.ds(i * P, P), :]).then_inc(s[f"xld{par}"], 16)

                    sp.wait_ge(s["scat"], 16 * NT * (m + 1))
                    slot_tiles(sp, tile)
            for group in ("a0", "f1"):
                sp.wait_ge(ld[group], 16 * len(LOADS[group]))
            sp.wait_ge(ld["f0"], 16 * len(LOADS["f0"]))
            sp.wait_ge(ld["add"], 16)
            sp.wait_ge(ld["zero"], 16 * ((NS + 7) // 8))
            if "A0" in phases:
                sp.wait_ge(ld["wqk"], 16)
            x_ready(sp, len(phases))
            sp.dma_start(out, X[:]).then_inc(s_out, 16)
            sp.wait_ge(s_out, 16)

        @block.gpsimd
        def _(pool):
            pool.memset(halfpow[:], -0.5).then_inc(s_constp, 1)
            pool.wait_ge(s_constp, 1)

            def rstd_of(s, i, nt):
                pool.wait_ge(s["ln"], i + 1)
                pool.tensor_tensor(rstd[:, 0:nt], ve[:, 0:nt], halfpow[:, 0:nt], ALU.pow).then_inc(s["rstd"], 1)

            for n, kind in enumerate(phases):
                s, m = ph[n], nth[n]
                if kind == "F0":
                    with pool.Fori(NT // CH * m, NT // CH * (m + 1)) as c:
                        rstd_of(s, c, CH)
                elif kind[0] == "A":
                    with pool.Fori(0, NB) as b:
                        rstd_of(s, b, 2)
                else:
                    rstd_of(s, m, NT)
                    pool.wait_ge(s["sl"], m + 1)
                    pool.wait_ge(s["xn"], NT * (m + 1))
                    pool.wait_ge(ld["zero"], 16 * ((NS + 7) // 8))
                    for t in range(NT):
                        pool.indirect_dma_start(
                            out=xs_dram, out_offset=bass.IndirectOffsetOnAxis(ap=slot[:, t:t + 1], axis=0),
                            in_=xn[:, t, :], in_offset=None).then_inc(s["scat"], 16)

                    def tile(i, par, k, first):
                        if not first:
                            pool.wait_ge(s["dn"], NS * m + i - 1)
                        pool.tensor_copy(oh_tile[:, par, :],
                                         ohT[:, bass.ds(i, 1)].broadcast_to([2 * E, P])).then_inc(s["oht"], 1)

                    pool.wait_ge(s["ohT"], m + 1)
                    slot_tiles(pool, tile)
                    for par in range(2):
                        pool.wait_ge(s[f"yst{par}"], 16 * NTP[par] * (m + 1))
                    pool.wait_ge(s["scat"], 16 * NT * (m + 1))
                    for t in range(NT):
                        pool.indirect_dma_start(
                            out=xn[:, t, :], out_offset=None, in_=ys_dram,
                            in_offset=bass.IndirectOffsetOnAxis(ap=slot[:, t:t + 1], axis=0)).then_inc(s["gat"], 16)

        @block.scalar
        def _(act):
            act.wait_ge(ld["w1"], 16)
            act.activation(w1h[:].rearrange("p e f -> p (e f)"), stage[:], ACT.Copy).then_inc(s_w1h, 1)
            act.wait_ge(ld["const"], 16 * len(LOADS["const"]))
            act.activation(identb[:], ident[:], ACT.Copy).then_inc(s_consta, 1)
            act.activation(masksb[:], masks, ACT.Copy).then_inc(s_consta, 1)
            act.activation(trib[:], tri[:], ACT.Copy).then_inc(s_consta, 1)
            act.wait_ge(ld["b1"], 32)
            act.activation(c1hl[:], c1f, ACT.Copy).then_inc(s_c1h, 1)

            def split_second():
                for e in range(E):
                    act.wait_ge(ld[f"stage{e % 2}"], 16 * (e // 2 + 1))
                    act.activation(v1h[:, e, :], stage[:, (e % 2) * 2 * HID:(e % 2 + 1) * 2 * HID],
                                   ACT.Copy).then_inc(s_stage_h, 1)

            for n, kind in enumerate(phases):
                s, m = ph[n], nth[n]
                if kind == "F0":
                    act.wait_ge(ld["f0"], 16 * len(LOADS["f0"]))
                    with act.Fori(NT // CH * m, NT // CH * (m + 1)) as c:
                        act.wait_ge(s["tr"], c + 1)
                        act.activation(xT[:], PS[:, 0, :], ACT.Copy).then_inc(s["xt"], 1)
                        act.wait_ge(s["xt"], c + 1)
                        act.activation(xTh[:], xT[:], ACT.Copy).then_inc(s["xh"], 1)
                        act.wait_ge(s["dlg"], c + 1)
                        act.activation(r8[1][:, 0:CH, :], r8[0][:, 0:CH, :], ACT.Exp).then_inc(s["ex"], 1)
                        act.wait_ge(s["cwt"], c + 1)
                        act.activation(cwT[:], PS[0:E0, 0, :], ACT.Copy).then_inc(s["cwts"], 1)
                        for e in range(E0):
                            act.wait_ge(s["up"], c * E0 + e + 1)
                            if e >= 2:
                                act.wait_ge(s["h"], c * E0 + e - 1)
                            act.activation(act_s[:, e % 2, :], PS[:, 2 + 2 * (e % 2), :], ACT.Silu,
                                           bias=b1[:, e, 0:1]).then_inc(s["sg"], 1)
                elif kind[0] == "A":
                    a = int(kind[1])
                    dst = xTp[:, PAD:PAD + SEQ]
                    nv = 2 if a == 0 else 4
                    act.wait_ge(s["wsc"], 1)
                    act.activation(wqkh[:], wqkf, ACT.Copy).then_inc(s["wh"], 1)
                    with act.Fori(0, NB) as b:
                        act.wait_ge(s["tr"], b + 1)
                        act.activation(dst, PS[:, 4, 0:SEQ], ACT.Copy).then_inc(s["xt"], 1)
                        act.wait_ge(s["xt"], b + 1)
                        act.activation(xTh[:, 0:SEQ], dst, ACT.Copy).then_inc(s["xh"], 1)
                        for r in range(4):
                            act.wait_ge(s["t"], 4 * b + r + 1)
                            act.activation(hqk[:, r % 2, :, :], tqk[:, r % 2, :, :], ACT.Copy).then_inc(s["hi"], 1)
                        for t in range(nv):
                            act.wait_ge(s["v"], nv * b + t + 1)
                            act.activation(vaug[:, t, :, 0:HD], PS[:, 7, 0:P].rearrange("p (h x) -> p h x", h=H),
                                           ACT.Copy).then_inc(s["vs"], 1)
                        for r in range(NR[kind]):
                            if r >= 4:
                                act.wait_ge(s["pv"], 2 * b + 1)
                            act.wait_ge(s["st"], NR[kind] * b + r + 1)
                            act.activation(prob[:, r % 4, :, :, :],
                                           PS[:, 2 * (r % 2):2 * (r % 2) + 2, :].rearrange("p j (g k) -> p j g k", g=G),
                                           ACT.Exp).then_inc(s["p"], 1)
                        for t in range(2):
                            act.wait_ge(s["atT"], 2 * b + t + 1)
                            act.activation(attT[:, t, :], PS[:, 4, 0:P], ACT.Copy).then_inc(s["atS"], 1)
                else:
                    if n == phases.index("F1"):
                        split_second()
                    for c in range(4):
                        act.wait_ge(s["tr"], 4 * m + c + 1)
                        if c >= 1:
                            act.wait_ge(s["lgt"], 4 * m + c)
                        act.activation(xT[:], PS[:, 0, :], ACT.Copy).then_inc(s["xt"], 1)

                    def tile(i, par, k, first):
                        act.wait_ge(s["trx"], NS * m + i + 1)
                        act.activation(xgh[:, par, :], PS[:, par, 0:P], ACT.Copy).then_inc(s["xh"], 1)
                        act.wait_ge(s["up"], NS * m + i + 1)
                        if not first:
                            act.wait_ge(s["h"], NS * m + i - 1)
                        act.activation(act_s[:, par, :], PS[:, 4 + par, :], ACT.Sigmoid).then_inc(s["sg"], 1)
                        act.wait_ge(s["trh"], NS * m + i + 1)
                        act.activation(hT[:, par, :], PS[:, 6, :], ACT.Copy).then_inc(s["hT"], 1)
                        act.wait_ge(s["y"], NS * m + i + 1)
                        act.dma_start(ys_dram[bass.ds(i * P, P), :], ysb[:, par, :]).then_inc(s[f"yst{par}"], 16)

                    slot_tiles(act, tile)

        @block.vector
        def _(dve):
            ch = Chain(dve, s_set)
            dve.memset(mpad[:], 0.0).then_inc(s_zero, 1)
            for tile_, value in ((onesb, 1.0), (ones1, 1.0), (vaug, 1.0), (xTp, 0.0), (cw, 0.5),
                                 (zero8, 0.0), (k16, 0.0)):
                ch.step(dve.memset(tile_[:], value))
            dve.wait_ge(ld["const"], 16 * len(LOADS["const"]))
            ch.wait()
            for lo in (0, SEQ + PAD):
                ch.step(dve.tensor_scalar(k16[:, :, lo:lo + PAD], k16[:, :, lo:lo + PAD], m_one, None, ALU.add))
            ch.wait()
            dve.wait_ge(s_w1h, 1)
            dve.tensor_tensor(w1l[:].rearrange("p e f -> p (e f)"), stage[:],
                              w1h[:].rearrange("p e f -> p (e f)").bitcast(F32), ALU.subtract).then_inc(s_w1l, 1)
            dve.wait_ge(s_c1h, 1)
            dve.scalar_tensor_tensor(out=c1hl[:], in0=c1hl[:].bitcast(F32), scalar=neg_lo16, in1=c1f,
                                     op0=ALU.mult, op1=ALU.add).then_inc(s_c1, 1)

            def split_second():
                for e in range(E):
                    dve.wait_ge(s_stage_h, e + 1)
                    dve.tensor_tensor(v1l[:, e, :], stage[:, (e % 2) * 2 * HID:(e % 2 + 1) * 2 * HID],
                                      v1h[:, e, :].bitcast(F32), ALU.subtract).then_inc(s_stage_l, 1)

            def layer_norm(s, i, nt, xi):
                ln = Chain(dve, s["dln"], i * 2 * nt)
                for t in range(nt):
                    ln.step(dve.bn_stats(stats[:, t, :], tile_of(X, xi + t)))
                for t in range(nt):
                    if t == 0:
                        ln.wait()
                        dve.memset(spare[:], 0.0)
                    ln.step(dve.bn_aggr(mv[:, t, :], stats[:, t, :]))
                ln.wait()
                dve.tensor_scalar(ve[:, 0:nt], mv[:, 0:nt, 1], EPS, None, ALU.add).then_inc(s["ln"], 1)
                dve.wait_ge(s["rstd"], i + 1)
                for t in range(nt):
                    dve.tensor_scalar(xn[:, t, :], tile_of(X, xi + t), mv[:, t, 0:1], rstd[:, t:t + 1],
                                      ALU.subtract, ALU.mult).then_inc(s["xn"], 1)

            def first_of_max(c, values, nt, eq, top, first, onehot_out):
                c.link(dve.tensor_reduce(top[:, 0:nt], values, AX.X, ALU.max))
                c.link(dve.tensor_tensor(eq[:, 0:nt, :], values, top[:, 0:nt].unsqueeze(2).broadcast_to([P, nt, E]),
                                         ALU.is_equal))
                c.link(dve.tensor_tensor(eq[:, 0:nt, :], eq[:, 0:nt, :], em8[:, 0:nt, :], ALU.mult))
                c.link(dve.tensor_reduce(first[:, 0:nt], eq[:, 0:nt, :], AX.X, ALU.min))
                c.link(dve.tensor_tensor(onehot_out, em8[:, 0:nt, :],
                                         first[:, 0:nt].unsqueeze(2).broadcast_to([P, nt, E]), ALU.is_equal))

            for n, kind in enumerate(phases):
                s, m = ph[n], nth[n]
                x_ready(dve, n)
                if kind == "F0":
                    dve.wait_ge(ld["f0"], 16 * len(LOADS["f0"]))
                    with dve.Fori(NT // CH * m, NT // CH * (m + 1)) as c:
                        c0 = (c - NT // CH * m) * CH
                        layer_norm(s, c, CH, c0)
                        dve.wait_ge(s["xh"], c + 1)
                        dve.tensor_tensor(xTl[:], xT[:], xTh[:].bitcast(F32), ALU.subtract).then_inc(s["xl"], 1)
                        c_ = Chain(dve, s["dch"], c * 16)
                        dve.wait_ge(s["lgt"], c + 1)
                        lg = PS[:, 1, 0:CH * E].rearrange("p (t e) -> p t e", e=E)
                        bc = lambda x: x[:, 0:CH].unsqueeze(2).broadcast_to([P, CH, E])
                        c_.link(dve.tensor_reduce(r1[0][:, 0:CH], lg, AX.X, ALU.max))
                        dve.tensor_tensor(r8[0][:, 0:CH, :], lg, bc(r1[0]), ALU.subtract).then_inc(s["dlg"], 1)
                        dve.wait_ge(s["ex"], c + 1)
                        pr = r8[1][:, 0:CH, :]
                        c_.link(dve.tensor_reduce(r1[0][:, 0:CH], pr, AX.X, ALU.add))
                        c_.link(dve.reciprocal(r1[1][:, 0:CH], r1[0][:, 0:CH]))
                        c_.link(dve.tensor_tensor(pr, pr, bc(r1[1]), ALU.mult))
                        o1, o2, eq = r8[2][:, 0:CH, :], r8[3][:, 0:CH, :], r8[0]
                        first_of_max(c_, pr, CH, eq, r1[0], r1[1], o1)
                        c_.link(dve.scalar_tensor_tensor(out=o2, in0=o1, scalar=-2.0, in1=pr, op0=ALU.mult, op1=ALU.add))
                        first_of_max(c_, o2, CH, eq, r1[0], r1[1], o2)
                        c_.link(dve.tensor_tensor(o1, o1, o2, ALU.add))
                        dve.scalar_tensor_tensor(out=cw[:, :, 0:E], in0=pr, scalar=0.5, in1=o1, op0=ALU.mult,
                                                 op1=ALU.mult).then_inc(s["cw"], 1)
                        assert c_.n == 16, c_.n
                        PER = 1 + E0 * CH

                        def accumulate(e):
                            if e < 0:
                                dve.wait_ge(s["yb"], c + 1)
                                dve.wait_ge(s["cw"], c + 1)
                                xs = X[:, bass.ds(c0, CH), :]
                                dve.tensor_tensor(xs, PS[:, 1, :].rearrange("p (t k) -> p t k", t=CH), xs,
                                                  ALU.add).then_inc(s["acc"], 1)
                                return
                            dve.wait_ge(s["dn"], c * E0 + e + 1)
                            for t in range(CH):
                                dve.wait_ge(s["acc"], c * PER + (1 if e == 0 else 1 + (e - 1) * CH + t + 1))
                                xs = tile_of(X, c0 + t)
                                dve.scalar_tensor_tensor(out=xs, in0=PS[:, 6 + e % 2, t * P:(t + 1) * P],
                                                         scalar=cw[:, t, e:e + 1], in1=xs, op0=ALU.mult,
                                                         op1=ALU.add).then_inc(s["acc"], 1)

                        accumulate(-1)
                        for e in range(E0):
                            dve.wait_ge(s["sg"], c * E0 + e + 1)
                            if e >= 2:
                                dve.wait_ge(s["dn"], c * E0 + e - 1)
                            dve.scalar_tensor_tensor(out=hid[:, e % 2, :], in0=PS[:, 3 + 2 * (e % 2), :],
                                                     scalar=b1[:, e, 1:2], in1=act_s[:, e % 2, :], op0=ALU.add,
                                                     op1=ALU.mult).then_inc(s["h"], 1)
                            if e >= 1:
                                accumulate(e - 1)
                        accumulate(E0 - 1)
                elif kind[0] == "A":
                    a = int(kind[1])
                    k_of_n = attn_phases.index(n)
                    causal = a == 0
                    dve.wait_ge(ld["a0"], 16 * len(LOADS["a0"]))
                    dve.wait_ge(ld["zero"], 16 * ((NS + 7) // 8))
                    dve.wait_ge(ld["wqk"], 16 * (k_of_n + 1))
                    dve.wait_ge(ld["add"], 16)
                    w = Chain(dve, s["wadd"])
                    dve.tensor_scalar(wqkf[:, 0, :], wqkf[:, 0, :], HD ** -0.5, None, ALU.mult).then_inc(s["wsc"], 1)
                    w.link(dve.tensor_scalar(bqk[a][:, 0, :], bqk[a][:, 0, :], HD ** -0.5, None, ALU.mult))
                    dve.wait_ge(s["wh"], 1)
                    dve.tensor_tensor(wqkl[:], wqkf, wqkh[:].bitcast(F32), ALU.subtract).then_inc(s["wl"], 1)
                    if not causal:
                        w.link(dve.memset(add_qk[:], 0.0))
                        w.link(dve.tensor_scalar(bqk[a][:, 1, :], bqk[a][:, 1, :], m_one, None, ALU.add))
                    for side in range(2):
                        for g in range(G):
                            w.step(dve.tensor_scalar(add_qk[:, side, g, :], add_qk[:, side, g, :],
                                                     bqk[a][:, side, g:g + 1], None, ALU.add))
                    w.wait()
                    rounds = ROUNDS["causal" if causal else "window"]
                    NRK = len(rounds)
                    with dve.Fori(0, NB) as b:
                        layer_norm(s, b, 2, b * 2)
                        dve.wait_ge(s["xh"], b + 1)
                        dve.tensor_tensor(xTl[:, 0:SEQ], xTp[:, PAD:PAD + SEQ], xTh[:, 0:SEQ].bitcast(F32),
                                          ALU.subtract).then_inc(s["xl"], 1)
                        for r in range(4):
                            side, half = r // 2, r % 2
                            dve.wait_ge(s["qk"], 4 * b + r + 1)
                            dve.tensor_tensor(tqk[:, r % 2, :, :], PS[:, 5 + r % 2, :].rearrange("p (g k) -> p g k", g=2),
                                              add_qk[:, side, 2 * half:2 * half + 2, :], ALU.add).then_inc(s["t"], 1)
                            dve.wait_ge(s["hi"], 4 * b + r + 1)
                            dst = (q16[:, 2 * half:2 * half + 2, :] if side == 0 else
                                   k16[:, 2 * half:2 * half + 2, PAD:PAD + SEQ])
                            dve.scalar_tensor_tensor(out=dst, in0=hqk[:, r % 2, :, :], scalar=neg_lo[side],
                                                     in1=tqk[:, r % 2, :, :], op0=ALU.mult, op1=ALU.add)\
                               .then_inc(s["qk16"], 1)
                        for r, (qt, kb, hf) in enumerate(rounds):
                            dve.wait_ge(s["s"], NRK * b + r + 1)
                            src = PS[:, 2 * (r % 2):2 * (r % 2) + 2, :].rearrange("p j (g k) -> p g j k", g=G)
                            if causal and qt == 1:
                                dst = mtmp[:, hf, kb, :, :]
                            else:
                                dst = mpad[:, qt, :, 2 * hf:2 * hf + 2, M_SLOT]
                            dve.tensor_reduce(dst, src, AX.X, ALU.max, negate=True).then_inc(s["mx"], 1)
                            if causal and kb == 1:
                                dve.wait_ge(s["mx"], NRK * b + r + 1)
                                dve.tensor_tensor(mpad[:, qt, :, 2 * hf:2 * hf + 2, M_SLOT], mtmp[:, hf, 0, :, :],
                                                  mtmp[:, hf, 1, :, :], ALU.min).then_inc(s["mp"], 1)
                        for qt in range(2):
                            dve.wait_ge(s["mt"], 2 * b + qt + 1)
                            dve.tensor_tensor(qm16[:, :, qt * P:(qt + 1) * P],
                                              PS[:, 4, :].rearrange("p (g k) -> p g k", g=G),
                                              q16[:, :, qt * P:(qt + 1) * P], ALU.add).then_inc(s["qm"], 1)
                        for qt in range(2):
                            pv = PS[:, 5 + qt, 0:H * (HD + 1)].rearrange("p (h x) -> p h x", h=H)
                            dve.wait_ge(s["pv"], 2 * b + qt + 1)
                            dve.reciprocal(rec[:, qt, :], pv[:, :, HD]).then_inc(s["rec"], 1)
                            dve.wait_ge(s["rec"], 2 * b + qt + 1)
                            dve.tensor_tensor(att[:, qt, :].rearrange("p (h x) -> p h x", h=H), pv[:, :, 0:HD],
                                              rec[:, qt, :].unsqueeze(2).broadcast_to([P, H, HD]), ALU.mult)\
                               .then_inc(s["at"], 1)
                        for qt in range(2):
                            dve.wait_ge(s["pj"], 2 * b + qt + 1)
                            xs = tile_of(X, b * 2 + qt)
                            dve.tensor_tensor(xs, PS[:, 7, 0:P], xs, ALU.add).then_inc(s["acc"], 1)
                else:
                    if n == phases.index("F1"):
                        split_second()
                    dve.wait_ge(ld["f1"], 16 * len(LOADS["f1"]))
                    ln = Chain(dve, s["dln"], 2 * NT * m)
                    for t in range(NT):
                        ln.step(dve.bn_stats(stats[:, t, :], X[:, t, :]))
                    ln.wait()
                    for t in range(NT):
                        ln.step(dve.bn_aggr(mv[:, t, :], stats[:, t, :]))
                    ln.wait()
                    dve.tensor_scalar(ve[:], mv[:, :, 1], EPS, None, ALU.add).then_inc(s["ln"], 1)
                    dve.wait_ge(s["rstd"], m + 1)
                    for t in range(NT):
                        dve.tensor_scalar(xn[:, t, :], X[:, t, :], mv[:, t, 0:1], rstd[:, t:t + 1],
                                          ALU.subtract, ALU.mult).then_inc(s["xn"], 1)
                    dve.wait_ge(s["lgt"], 4 * (m + 1))
                    c_ = Chain(dve, s["dch"], 19 * m)
                    lg = PS[:, 1, 0:NT * E].rearrange("p (t e) -> p t e", e=E)
                    first_of_max(c_, lg, NT, r8[0], r1[0], r1[1], onehot[:])
                    for twice in range(2):
                        c_.step(dve.tensor_reduce(r8[1][:, twice, :], onehot[:].rearrange("p t e -> p e t"), AX.X, ALU.add))
                    c_.wait()
                    dve.tensor_copy(ohsum[:], r8[1][:, 0:2, :]).then_inc(s["oh"], 1)
                    dve.wait_ge(s["cnt"], m + 1)
                    c_.link(dve.tensor_tensor(gtk[:], PS[:, 2, 0:E].unsqueeze(2).broadcast_to([P, E, NT]), k128[:],
                                              ALU.is_gt))
                    c_.link(dve.tensor_reduce(ntl[:, 0, :], gtk[:], AX.X, ALU.add))
                    c_.link(dve.tensor_tensor_scan(ntl[:, 1, :], ntl[:, 0, :], zero8[:], 0.0, ALU.add, ALU.add))
                    c_.link(dve.tensor_tensor(ntl[:, 2, :], ntl[:, 1, :], ntl[:, 0, :], ALU.subtract))
                    c_.link(dve.scalar_tensor_tensor(out=r8[0][:], in0=ntl[:, 2, :].unsqueeze(1).broadcast_to([P, NT, E]),
                                                     scalar=float(P), in1=PS[:, 3, 0:NT * E].rearrange("p (t e) -> p t e", e=E),
                                                     op0=ALU.mult, op1=ALU.add))
                    c_.link(dve.tensor_tensor(r8[0][:], r8[0][:], onehot[:], ALU.mult))
                    c_.link(dve.tensor_reduce(slotf[:], r8[0][:], AX.X, ALU.add))
                    dve.tensor_copy(slot[:], slotf[:]).then_inc(s["sl"], 1)
                    c_.link(dve.tensor_copy(offT[:, 0:1], PS[0:2 * E, 4, 0:1]))
                    c_.link(dve.tensor_scalar(gtT[:], k128T, offT[:, 0:1], None, ALU.is_lt))
                    dve.tensor_reduce(ntT[:], gtT[:], AX.X, ALU.add).then_inc(s["ntT"], 1)
                    dve.wait_ge(s["incl"], m + 1)
                    c_.link(dve.tensor_copy(offT[:], PS[0:2 * E, 4, 0:2]))
                    for k in range(2):
                        c_.step(dve.tensor_scalar(cmpT[:, k, :], iota_s, offT[:, k:k + 1], None, ALU.is_lt))
                    c_.wait()
                    dve.tensor_tensor(ohT[:], cmpT[:, 0, :], cmpT[:, 1, :], ALU.subtract).then_inc(s["ohT"], 1)
                    assert c_.n == 19, c_.n
                    dve.wait_ge(s["eidp"], m + 1)
                    dve.tensor_copy(eid[:], PS[0:1, 4, 0:NS]).then_inc(s["eid"], 1)

                    def tile(i, par, k, first):
                        dve.wait_ge(s["xh"], NS * m + i + 1)
                        dve.tensor_tensor(xgl[:, par, :], PS[:, par, 0:P], xgh[:, par, :].bitcast(F32),
                                          ALU.subtract).then_inc(s["xl"], 1)
                        dve.wait_ge(s["sg"], NS * m + i + 1)
                        if not first:
                            dve.wait_ge(s["trh"], NS * m + i - 1)
                        dve.tensor_tensor(hid[:, par, :], PS[:, 2 + par, :], act_s[:, par, :], ALU.mult).then_inc(s["h"], 1)
                        dve.wait_ge(s["dn"], NS * m + i + 1)
                        if not first:
                            dve.wait_ge(s[f"yst{par}"], (NTP[par] * m + k) * 16)
                        dve.tensor_copy(ysb[:, par, :], PS[:, 7, 0:P]).then_inc(s["y"], 1)

                    slot_tiles(dve, tile)
                    dve.wait_ge(s["gat"], 16 * NT * (m + 1))
                    for c in range(4):
                        xs = X[:, 4 * c:4 * c + 4, :]
                        dve.scalar_tensor_tensor(out=xs, in0=xn[:, 4 * c:4 * c + 4, :], scalar=0.5, in1=xs,
                                                 op0=ALU.mult, op1=ALU.add).then_inc(s["acc"], 1)

        @block.tensor
        def _(pe):
            pe.wait_ge(ld["const"], 16 * len(LOADS["const"]))
            pe.wait_ge(s_consta, 3)
            pe.wait_ge(s_set, 7)

            def mm3(out_, wh, wl, xh, xl, stop=True):
                pe.matmul(out_, wh, xh, start=True, stop=False)
                pe.matmul(out_, wl, xh, start=False, stop=False)
                return pe.matmul(out_, wh, xl, start=False, stop=stop)

            for n, kind in enumerate(phases):
                s, m = ph[n], nth[n]
                if kind == "F0":
                    pe.wait_ge(ld["f0"], 16 * len(LOADS["f0"]))
                    pe.wait_ge(s_w1l, 1)
                    with pe.Fori(NT // CH * m, NT // CH * (m + 1)) as c:
                        pe.wait_ge(s["xn"], (c + 1) * CH)
                        for t in range(CH):
                            ins = pe.transpose(PS[:, 0, t * P:(t + 1) * P], xn[:, t, :], ident[:])
                        ins.then_inc(s["tr"], 1)
                        pe.wait_ge(s["xt"], c + 1)
                        for t in range(CH):
                            o = PS[:, 1, t * E:(t + 1) * E]
                            pe.matmul(o, xT[:, t * P:(t + 1) * P], gate_w[:], start=True, stop=False)
                            ins = pe.matmul(o, ones1[:], gate_b[:], start=False, stop=True)
                        ins.then_inc(s["lgt"], 1)

                        def up(e):
                            if e >= 2:
                                pe.wait_ge(s["h"], c * E0 + e - 1)
                            for half in range(2):
                                w = slice(half * P, (half + 1) * P)
                                ins = mm3(PS[:, 2 + 2 * (e % 2) + half, :], w1h[:, e, w], w1l[:, e, w], xTh[:], xTl[:])
                            ins.then_inc(s["up"], 1)

                        def down(e):
                            pe.wait_ge(s["h"], c * E0 + e + 1)
                            if e >= 2:
                                pe.wait_ge(s["acc"], c * (1 + E0 * CH) + 1 + (e - 1) * CH)
                            for t in range(CH):
                                ins = pe.matmul(PS[:, 6 + e % 2, t * P:(t + 1) * P], hid[:, e % 2, t * P:(t + 1) * P],
                                                w2[:, e, :], start=True, stop=True)
                            ins.then_inc(s["dn"], 1)

                        pe.wait_ge(s["xl"], c + 1)
                        up(0)
                        up(1)
                        pe.wait_ge(s["cw"], c + 1)
                        for t in range(CH):
                            ins = pe.transpose(PS[0:E0, 0, t * P:(t + 1) * P], cw[:, t, :], ident[:])
                        ins.then_inc(s["cwt"], 1)
                        pe.wait_ge(s["cwts"], c + 1)
                        for t in range(CH):
                            ins = pe.matmul(PS[:, 1, t * P:(t + 1) * P], cwT[:, t * P:(t + 1) * P], b2[:],
                                            start=True, stop=True)
                        ins.then_inc(s["yb"], 1)
                        for e in range(E0):
                            if e >= 1 and e + 1 < E0:
                                up(e + 1)
                            down(e)
                elif kind[0] == "A":
                    a = int(kind[1])
                    causal = a == 0
                    rounds = ROUNDS["causal" if causal else "window"]
                    NRK = len(rounds)
                    nv = 2 if causal else 4
                    pe.wait_ge(ld["a0"], 16 * len(LOADS["a0"]))
                    pe.wait_ge(s["wl"], 1)

                    def masked(bank, which, scores):
                        if which is not None:
                            pe.matmul(PS[:, bank, :].rearrange("p (g k) -> p g k", g=G), identb[:],
                                      masksb[:, which, :].unsqueeze(1).broadcast_to([P, G, P]), start=True, stop=False)
                        return scores(which is None)

                    with pe.Fori(0, NB) as b:
                        pe.wait_ge(s["xn"], (b + 1) * 2)
                        for t in range(2):
                            ins = pe.transpose(PS[:, 4, t * P:(t + 1) * P], xn[:, t, :], ident[:])
                        ins.then_inc(s["tr"], 1)
                        pe.wait_ge(s["xl"], b + 1)
                        for r in range(4):
                            side, half = r // 2, r % 2
                            if r >= 2:
                                pe.wait_ge(s["t"], 4 * b + r - 1)
                            for gg in range(2):
                                g = 2 * half + gg
                                w = slice(g * P, (g + 1) * P)
                                ins = mm3(PS[:, 5 + r % 2, gg * SEQ:(gg + 1) * SEQ], wqkh[:, side, w],
                                          wqkl[:, side, w], xTh[:, 0:SEQ], xTl[:, 0:SEQ])
                            ins.then_inc(s["qk"], 1)
                        for t in range(nv):
                            if t >= 1:
                                pe.wait_ge(s["vs"], nv * b + t)
                            lo = PAD + t * P if causal else t * WIN
                            pe.matmul(PS[:, 7, 0:P], xTp[:, lo:lo + P], wv[a][:], start=True, stop=False)
                            pe.matmul(PS[:, 7, 0:P], valid[:, lo:lo + P], bv[a][:], start=False, stop=True)\
                              .then_inc(s["v"], 1)
                        pe.wait_ge(s["qk16"], 4 * (b + 1))
                        for r, (qt, kb, hf) in enumerate(rounds):
                            if r >= 2:
                                pe.wait_ge(s["mx"], NRK * b + r - 1)
                            which = (0 if qt == kb else None) if causal else 2
                            for j in range(2):
                                if which is not None:
                                    pe.matmul(PS[:, 2 * (r % 2) + j, :].rearrange("p (g k) -> p g k", g=G), identb[:],
                                              masksb[:, which, :].unsqueeze(1).broadcast_to([P, G, P]),
                                              start=True, stop=False, skip_group_check=True)
                            for g in range(G):
                                for j in range(2):
                                    sl = slice(SL * (2 * hf + j), SL * (2 * hf + j + 1))
                                    o = PS[:, 2 * (r % 2) + j, g * P:(g + 1) * P]
                                    if causal:
                                        ins = pe.matmul(o, q16[sl, g, qt * P:(qt + 1) * P],
                                                        k16[sl, g, PAD + kb * P:PAD + (kb + 1) * P],
                                                        start=which is None, stop=True, skip_group_check=True)
                                    else:
                                        for w in range(2):
                                            lo = (2 * qt + w) * WIN
                                            ins = pe.matmul(o[w * WIN:(w + 1) * WIN, :], q16[sl, g, lo:lo + WIN],
                                                            k16[sl, g, lo:lo + P], start=False, stop=True,
                                                            skip_group_check=True)
                            ins.then_inc(s["s"], 1)
                        for qt in range(2):
                            if causal:
                                pe.wait_ge(s["mx"], NRK * b + (2 if qt == 0 else NRK))
                                if qt == 1:
                                    pe.wait_ge(s["mp"], 2 * (b + 1))
                            else:
                                pe.wait_ge(s["mx"], NRK * b + 2 * (qt + 1))
                            if qt == 1:
                                pe.wait_ge(s["qm"], 2 * b + 1)
                            for g in range(G):
                                ins = pe.transpose(PS[:, 4, g * P:(g + 1) * P],
                                                   mpad[:, qt, g, :, :].rearrange("p j s -> p (j s)"), ident[:])
                            ins.then_inc(s["mt"], 1)

                        def weighted(qt, r):
                            hf = rounds[r][2]
                            for g in range(G):
                                for j in range(2):
                                    h = 4 * g + 2 * hf + j
                                    o = PS[:, 5 + qt, h * (HD + 1):(h + 1) * (HD + 1)]
                                    if causal:
                                        kbs = range(qt + 1)
                                        for kb in kbs:
                                            rr = r - qt + kb
                                            ins = pe.matmul(o, prob[:, rr % 4, j, g, :], vaug[:, kb, h, :],
                                                            start=kb == 0, stop=kb == qt)
                                    else:
                                        for w in range(2):
                                            ins = pe.matmul(o[w * WIN:(w + 1) * WIN, :],
                                                            prob[:, r % 4, j, g, w * WIN:(w + 1) * WIN],
                                                            vaug[:, 2 * qt + w, h, :], start=True, stop=True)
                            return ins

                        pe.wait_ge(s["vs"], nv * (b + 1))
                        pe.wait_ge(s["mx"], NRK * (b + 1))
                        for r, (qt, kb, hf) in enumerate(rounds):
                            pe.wait_ge(s["qm"], 2 * b + qt + 1)
                            if r >= 2:
                                pe.wait_ge(s["p"], NRK * b + r - 1)
                            which = (1 if qt == kb else None) if causal else 3
                            for j in range(2):
                                if which is not None:
                                    pe.matmul(PS[:, 2 * (r % 2) + j, :].rearrange("p (g k) -> p g k", g=G), identb[:],
                                              masksb[:, which, :].unsqueeze(1).broadcast_to([P, G, P]),
                                              start=True, stop=False, skip_group_check=True)
                            for g in range(G):
                                for j in range(2):
                                    sl = slice(SL * (2 * hf + j), SL * (2 * hf + j + 1))
                                    o = PS[:, 2 * (r % 2) + j, g * P:(g + 1) * P]
                                    if causal:
                                        ins = pe.matmul(o, k16[sl, g, PAD + kb * P:PAD + (kb + 1) * P],
                                                        qm16[sl, g, qt * P:(qt + 1) * P],
                                                        start=which is None, stop=True, skip_group_check=True)
                                    else:
                                        for w in range(2):
                                            lo = (2 * qt + w) * WIN
                                            ins = pe.matmul(o[:, w * WIN:(w + 1) * WIN], k16[sl, g, lo:lo + P],
                                                            qm16[sl, g, lo:lo + WIN], start=False, stop=True,
                                                            skip_group_check=True)
                            ins.then_inc(s["st"], 1)
                            if r == 2:
                                pe.wait_ge(s["p"], NRK * b + 2)
                                weighted(0, 0)
                                weighted(0, 1).then_inc(s["pv"], 1)
                        pe.wait_ge(s["p"], NRK * (b + 1))
                        weighted(1, 3 if causal else 2)
                        weighted(1, NRK - 1).then_inc(s["pv"], 1)
                        for qt in range(2):
                            pe.wait_ge(s["at"], 2 * b + qt + 1)
                            if qt == 1:
                                pe.wait_ge(s["atS"], 2 * b + 1)
                            pe.transpose(PS[:, 4, 0:P], att[:, qt, :], ident[:]).then_inc(s["atT"], 1)
                            pe.wait_ge(s["atS"], 2 * b + qt + 1)
                            if qt == 1:
                                pe.wait_ge(s["acc"], 2 * b + 1)
                            pe.matmul(PS[:, 7, 0:P], attT[:, qt, :], wp[a][:], start=True, stop=False)
                            pe.matmul(PS[:, 7, 0:P], ones1[:], bp[a][:], start=False, stop=True).then_inc(s["pj"], 1)
                        pe.wait_ge(s["acc"], 2 * (b + 1))
                else:
                    pe.wait_ge(ld["f1"], 16 * len(LOADS["f1"]))
                    for c in range(4):
                        pe.wait_ge(s["xn"], NT * m + (c + 1) * 4)
                        if c >= 1:
                            pe.wait_ge(s["xt"], 4 * m + c)
                        for t in range(4):
                            ins = pe.transpose(PS[:, 0, t * P:(t + 1) * P], xn[:, 4 * c + t, :], ident[:])
                        ins.then_inc(s["tr"], 1)
                        pe.wait_ge(s["xt"], 4 * m + c + 1)
                        for t in range(4):
                            o = PS[:, 1, (4 * c + t) * E:(4 * c + t + 1) * E]
                            pe.matmul(o, xT[:, t * P:(t + 1) * P], router_w[:], start=True, stop=False)
                            ins = pe.matmul(o, ones1[:], router_b[:], start=False, stop=True)
                        ins.then_inc(s["lgt"], 1)
                    pe.wait_ge(s["oh"], m + 1)
                    pe.matmul(PS[:, 2, 0:E], onesb[:], ohsum[:, 0, :], start=True, stop=True)
                    pe.matmul(PS[0:2 * E, 4, 0:1], ohsum[:].rearrange("p a e -> p (a e)"), onesb[:, 0:1],
                              start=True, stop=True)
                    oh = onehot[:].rearrange("p t e -> p (t e)")
                    for back in range(1, NT):
                        pe.matmul(PS[:, 3, back * E:NT * E], onesb[:], oh[:, 0:(NT - back) * E],
                                  start=back == 1, stop=False, skip_group_check=True)
                    pe.matmul(PS[:, 3, 0:NT * E], trib[:], oh, start=False, stop=True,
                              skip_group_check=True).then_inc(s["cnt"], 1)
                    pe.wait_ge(s["ntT"], m + 1)
                    pe.matmul(PS[0:2 * E, 4, 0:1], tri_incl, ntT[:], start=True, stop=True)
                    pe.matmul(PS[0:2 * E, 4, 1:2], tri_excl, ntT[:], start=True, stop=True).then_inc(s["incl"], 1)
                    pe.wait_ge(s["ohT"], m + 1)
                    pe.matmul(PS[0:1, 4, 0:NS], eid_col, ohT[:], start=True, stop=True).then_inc(s["eidp"], 1)
                    pe.wait_ge(s["eid"], m + 1)
                    pe.wait_ge(s_c1, 1)
                    pe.wait_ge(s_stage_l, E)

                    def tile(i, par, k, first):
                        e = pe.value_load(eid[0:1, bass.ds(i, 1)], min_val=0, max_val=E - 1)
                        pe.wait_ge(s[f"xld{par}"], (NTP[par] * m + k + 1) * 16)
                        pe.transpose(PS[:, par, 0:P], xg[:, par, :], ident[:]).then_inc(s["trx"], 1)
                        pe.wait_ge(s["xl"], NS * m + i + 1)
                        pe.wait_ge(s["oht"], NS * m + i + 1)
                        if not first:
                            pe.wait_ge(s["h"], NS * m + i - 1)
                        vh = v1h[:].rearrange("p e f -> p (e f)")
                        vl = v1l[:].rearrange("p e f -> p (e f)")
                        for half, bank in ((1, 4 + par), (0, 2 + par)):
                            at = e * (2 * HID) + half * HID
                            o = PS[:, bank, :]
                            pe.matmul(o, xgh[:, par, :], vh[:, bass.ds(at, HID)], start=True, stop=False)
                            pe.matmul(o, xgl[:, par, :], vh[:, bass.ds(at, HID)], start=False, stop=False)
                            pe.matmul(o, xgh[:, par, :], vl[:, bass.ds(at, HID)], start=False, stop=False)
                            ins = pe.matmul(o, oh_tile[:, par, :], c1hl[:, half * HID:(half + 1) * HID],
                                            start=False, stop=True)
                        ins.then_inc(s["up"], 1)
                        pe.wait_ge(s["h"], NS * m + i + 1)
                        for q in range(4):
                            ins = pe.transpose(PS[:, 6, q * P:(q + 1) * P], hid[:, par, q * P:(q + 1) * P], ident[:])
                        ins.then_inc(s["trh"], 1)
                        pe.wait_ge(s["hT"], NS * m + i + 1)
                        v2_ = v2[:].rearrange("p e q c -> p (e q c)")
                        if not first or par == 1:
                            pe.wait_ge(s["y"], NS * m + i)
                        for q in range(4):
                            pe.matmul(PS[:, 7, 0:P], hT[:, par, q * P:(q + 1) * P],
                                      v2_[:, bass.ds(e * HID + q * P, P)], start=q == 0, stop=False)
                        pe.matmul(PS[:, 7, 0:P], oh_tile[0:E, par, :].bitcast(F32), c2[:], start=False, stop=True)\
                          .then_inc(s["dn"], 1)

                    slot_tiles(pe, tile)


def _constants():
    import numpy as np
    f = np.float32
    i = np.arange(P)
    c = {"c_ident": np.eye(P, dtype=f)}
    q, k = i[:, None], i[None, :]
    causal = np.where(k > q, NEG, 0.0)
    w = np.where((k >= q % WIN) & (k < q % WIN + WIN), 0.0, NEG)
    c["c_masks"] = np.stack([causal, causal.T, w, w.T], axis=1).astype(f)
    c["c_tri"] = (q < k).astype(f)
    c["c_em8"] = np.broadcast_to(np.arange(E) - float(E), (P, NT, E)).astype(f)
    c["c_k128"] = np.broadcast_to(float(P) * np.arange(NT), (P, E, NT)).astype(f)
    slot = i % SL
    cols = np.zeros((P, 4), f)
    cols[:, 0] = np.where((slot >= HD) & (slot < 2 * HD), -1, 0)
    cols[:, 1] = np.where((slot >= 2 * HD) & (slot < 3 * HD), -1, 0)
    cols[:, 2] = slot == M_SLOT
    c["c_cols"] = cols
    v = np.zeros((1, SEQ + 2 * PAD), f)
    v[:, PAD:PAD + SEQ] = 1
    c["c_valid"] = v
    e = np.arange(2 * E)
    same = (e[:, None] // E) == (e[None, :] // E)
    c["c_small"] = np.concatenate([
        np.broadcast_to(float(P) * np.arange(16), (2 * E, 16)),
        same & (e[:, None] <= e[None, :]), same & (e[:, None] < e[None, :]),
        np.broadcast_to(np.arange(NS), (2 * E, NS)), np.where(e < E, e, 0)[:, None], -(e >= E)[:, None].astype(f)],
        axis=1).astype(f)
    add = np.zeros((P, 2, G, SEQ), f)
    pos = np.arange(SEQ)
    for h in range(H):
        g, r = h // 4, SL * (h % 4)
        slope = 2.0 ** -(h + 1)
        add[r + 24, 0, g], add[r + 24, 1, g] = 1, slope * pos
        add[r + 25, 0, g], add[r + 25, 1, g] = -slope * pos, 1
        add[r + M_SLOT, 1, g] = 1
    c["c_add_qk"] = add
    return c


def _laid_out(i):
    import numpy as np

    def slots(w, b, k0):
        n = w.shape[0]
        pw, pb = np.zeros((n, H, SL), w.dtype), np.zeros((H, SL), w.dtype)
        for r in range(3):
            pw[:, :, r * HD:(r + 1) * HD] = w[:, k0:k0 + P].reshape(n, H, HD)
            pb[:, r * HD:(r + 1) * HD] = b[k0:k0 + P].reshape(H, HD)
        return pw.reshape(n, H * SL), pb.reshape(G, P).T

    a = {"x": i["L0_attn_x"].reshape(NT, P, P).transpose(1, 0, 2)}
    w1 = np.concatenate([i["L0_ffn_rw1"], i["L0_ffn_sw1"]])
    a["w1_0"] = w1.transpose(1, 0, 2).reshape(P, E0 * 2 * P)
    b1 = np.concatenate([i["L0_ffn_rb1"], i["L0_ffn_sb1"]])
    a["b1_0"] = b1.reshape(E0, 2, P).transpose(2, 0, 1)
    a["w2_0"] = np.concatenate([i["L0_ffn_rw2"], i["L0_ffn_sw2"]]).transpose(1, 0, 2)
    a["b2_0"] = np.concatenate([i["L0_ffn_rb2"], i["L0_ffn_sb2"]])
    a["gate_w"], a["gate_b"] = i["L0_ffn_gate_w"], i["L0_ffn_gate_b"][None]
    for n, (w, b, wp, bp) in enumerate([
            (i["L0_attn_W_attn"], i["L0_attn_b_attn"], i["L0_attn_W_proj"], i["L0_attn_b_proj"]),
            (i["L1_attn_Wqkv"].T, i["L1_attn_bqkv"], i["L1_attn_Wout"].T, i["L1_attn_bout"])]):
        qw, qb = slots(w, b, 0)
        kw, kb = slots(w, b, P)
        a[f"wqk_{n}"] = np.stack([qw, kw], axis=1)
        a[f"bqk_{n}"] = np.stack([qb, kb], axis=1)
        a[f"wv_{n}"], a[f"bv_{n}"] = w[:, 2 * P:], b[None, 2 * P:]
        a[f"wp_{n}"], a[f"bp_{n}"] = wp, bp[None]
    a["router_w"], a["router_b"] = i["L1_ffn_router_w"], i["L1_ffn_router_b"][None]
    a["w1_1"] = i["L1_ffn_w1"].transpose(1, 0, 2)
    a["b1_1"] = i["L1_ffn_b1"]
    a["w2_1"] = i["L1_ffn_w2"].reshape(E, HID // P, P, P).transpose(2, 0, 1, 3)
    a["b2_1"] = i["L1_ffn_b2"]
    return a


def kernel(**inputs):
    import numpy as np
    import concourse.bacc as bacc
    from concourse.bass_utils import run_bass_kernel_spmd

    nc = bacc.Bacc("TRN2", target_bir_lowering=False, num_devices=1)
    arrays, d = {}, {}
    for name, a in {**_laid_out({k: np.asarray(v) for k, v in inputs.items()}), **_constants()}.items():
        a = np.ascontiguousarray(a)
        arrays[f"in_{name}"] = a
        d[name] = nc.dram_tensor(f"in_{name}", a.shape, mybir.dt.from_np(a.dtype), kind="ExternalInput").ap()
    out = nc.dram_tensor("out_x", (P, NT, P), F32, kind="ExternalOutput").ap()
    macaron(nc, d, out)
    r = run_bass_kernel_spmd(nc, [arrays], core_ids=[0])
    got = r.results[0]["out_x"]
    return got.transpose(1, 0, 2).reshape(NB, SEQ, P)
```

```python
from contextlib import ExitStack

import concourse.bass as bass
from concourse import mybir

F32 = mybir.dt.float32
F32R = mybir.dt.float32r
F16 = mybir.dt.float16
BF16 = mybir.dt.bfloat16
U32 = mybir.dt.uint32
I32 = mybir.dt.int32
ALU = mybir.AluOpType
ACT = mybir.ActivationFunctionType
AX = mybir.AxisListType

P = 128
NT = 16
NB = 8
SEQ = 256
H = 16
HD = P // H
G = 4
SL = 32
M_SLOT = 26
E = 8
E0 = E + 1
HID = 512
WIN = 64
PAD = WIN // 2
NEG = -1e30
EPS = 1e-5
CH = 4
NS = NT + E - 1
ROUNDS = {"causal": [(0, 0, c) for c in range(4)] + [(1, kb, c) for c in range(4) for kb in range(2)],
          "window": [(qt, 0, c) for qt in range(2) for c in range(4)]}
LEAD = 4


def positive(value):
    return not isinstance(value, int) or value > 0


class Chain:

    def __init__(self, eng, sem, base=0):
        self.eng, self.sem, self.base, self.n = eng, sem, base, 0

    def step(self, ins):
        self.n += 1
        ins.then_inc(self.sem, 1)

    def wait(self):
        self.eng.wait_ge(self.sem, self.base + self.n)

    def link(self, ins):
        self.step(ins)
        self.wait()


def macaron(nc, d, out, phases=("F0", "A0", "F0", "F1", "A1", "F1")):
    ctx = ExitStack()
    with ctx:
        def sb(name, shape, dt=F32):
            return ctx.enter_context(nc.sbuf_tensor(name, shape, dt))

        def sem(name):
            return ctx.enter_context(nc.semaphore(name))

        X = sb("residual", [P, NT, P])
        ident = sb("ident", [P, P])
        identb = sb("identb", [P, P], BF16)
        masksb = sb("masksb", [P, 4, P], BF16)
        tri = sb("tri", [P, P])
        trib = sb("trib", [P, P], BF16)
        onesb = sb("onesb", [P, P], BF16)
        ones1 = sb("ones1", [1, P])
        em8 = sb("em8", [P, NT, E])
        k128 = sb("k128", [P, E, NT])
        cols = sb("cols", [P, 4])
        valid = sb("valid", [1, SEQ + 2 * PAD])
        small = sb("small", [2 * E, 3 * 16 + NS + 2])
        halfpow = sb("halfpow", [P, NT])
        stage = sb("stage", [P, E0 * 2 * P])
        w1h = sb("w1h", [P, E0, 2 * P], F32R)
        w1l = sb("w1l", [P, E0, 2 * P], F32R)
        b1 = sb("b1", [P, E0, 2])
        w2 = sb("w2", [P, E0, P])
        b2 = sb("b2", [E0, P])
        gate_w = sb("gate_w", [P, E])
        gate_b = sb("gate_b", [1, E])
        wqkh = sb("wqkh", [P, 2, G * P], F32R)
        wqkl = sb("wqkl", [P, 2, G * P], F32R)
        addw = sb("addw", [4, 2, G * P], F32R)
        addx = sb("addx", [4, SEQ], F32R)
        wv = [sb(f"wv{a}", [P, P]) for a in range(2)]
        bv = [sb(f"bv{a}", [1, P]) for a in range(2)]
        wp = [sb(f"wp{a}", [P, P]) for a in range(2)]
        bp = [sb(f"bp{a}", [1, P]) for a in range(2)]
        v1h = sb("v1h", [P, E, 2 * HID], F32R)
        v1l = sb("v1l", [P, E, 2 * HID], F32R)
        v2 = sb("v2", [P, E, HID // P, P])
        c1hl = sb("c1hl", [2 * E, 2 * HID], F32R)
        c2 = sb("c2", [E, P])
        router_w = sb("router_w", [P, E])
        router_b = sb("router_b", [1, E])
        xn = sb("xn", [P, NT, P])
        masks = xn[:, 4:8, :]
        c1f = xn[0:2 * E, 8:16, :].rearrange("p a c -> p (a c)")
        stats = sb("stats", [P, NT, 6])
        mv = sb("mv", [P, NT, 2])
        ve = sb("ve", [P, NT])
        rstd = sb("rstd", [P, NT])
        xT = sb("xT", [P, CH * P])
        xTp = sb("xTp", [P, SEQ + 2 * PAD])
        xTh = sb("xTh", [P, CH * P], F32R)
        xTl = sb("xTl", [P, CH * P], F32R)
        r8 = [sb(f"r8_{i}", [P, NT, E]) for i in range(4)]
        r1 = [sb(f"r1_{i}", [P, NT]) for i in range(3)]
        cw = sb("cw", [P, CH, E0])
        cwT = sb("cwT", [E0, CH * P])
        big = sb("big", [P, 4 * 2 * G * P])
        prob = stage[:, 512:1536].rearrange("p (r g k) -> p r g k", r=2, g=G)
        prob16 = [big[:, 2048 * half:2048 * (half + 1)].bitcast(F16).rearrange("p (r g k) -> p r g k", r=8, g=G)
                  for half in range(2)]
        act_s = big[:, 0:1024].rearrange("p (a b) -> p a b", a=2)
        hid = big[:, 1024:2048].rearrange("p (a b) -> p a b", a=2)
        hT = big[:, 2048:3072].rearrange("p (a b) -> p a b", a=2)
        wqkf = big[:, 3072:4096].rearrange("p (s c) -> p s c", s=2)
        hqk = stage[:, 0:512].bitcast(F16).rearrange("p (a g k) -> p a g k", a=2, g=2)
        addf = stage[0:4, 512:1536].rearrange("p (s c) -> p s c", s=2)
        q16 = sb("q16", [P, 2, G, SEQ], F16)
        KW = SEQ + 2 * PAD
        k16 = [sb("k16", [P, G, KW], F16)[:],
               xn[:, 4:9, :].rearrange("p a c -> p (a c)").bitcast(F16).rearrange("p (g k) -> p g k", g=G)]
        vaug = [sb("vaug", [P, 2, 4, H, HD + 1], F16)[:],
                xn[:, 9:14, :].rearrange("p a c -> p (a c)")[:, 0:4 * H * (HD + 1)].bitcast(F16)
                .rearrange("p (l t h x) -> p l t h x", l=2, t=4, h=H)]
        mtmp = sb("mtmp", [P, 2, G, 4])
        mpad = sb("mpad", [P, 2, G, 4, SL], F16)
        ident16 = sb("ident16", [P, P], F16)
        rec = sb("rec", [P, 2, H])
        att = sb("att", [P, 2, P])
        attT = sb("attT", [P, 2, P])
        onehot = sb("onehot", [P, NT, E], BF16)
        ohsum = sb("ohsum", [P, 2, E], BF16)
        gtk = sb("gtk", [P, E, NT])
        ntl = sb("ntl", [P, 3, E])
        spare = sb("spare", [P, 1])
        zero8 = sb("zero8", [P, E])
        slotf = sb("slotf", [P, NT])
        slot = sb("slot", [P, NT], U32)
        gtT = sb("gtT", [2 * E, 16])
        ntT = sb("ntT", [2 * E, 1])
        offT = sb("offT", [2 * E, 2])
        cmpT = sb("cmpT", [2 * E, 2, NS])
        ohT = sb("ohT", [2 * E, NS])
        eid = sb("eid", [1, NS], I32)
        oh_up = xTh[0:2 * E, 0:2 * P].rearrange("p (a k) -> p a k", a=2)
        xg = q16[:, 0].rearrange("p g k -> p (g k)")[:, 0:512].bitcast(F32).rearrange("p (a k) -> p a k", a=2)
        oh_down = attT[0:E]
        xgh = sb("xgh", [P, 2, P], F32R)
        xgl = sb("xgl", [P, 2, P], F32R)
        ysb = att
        PS = ctx.enter_context(nc.psum_tensor("PS", [P, 8, 512], F32))

        xs_dram = nc.dram_tensor("xs_dram", [NS * P, P], F32).ap()
        ys_dram = nc.dram_tensor("ys_dram", [NS * P, P], F32).ap()

        k128T = small[:, 0:16]
        tri_incl = small[:, 16:32]
        tri_excl = small[:, 32:48]
        iota_s = small[:, 48:48 + NS]
        eid_col = small[:, 48 + NS:49 + NS]
        neg_lo16 = small[:, 49 + NS:50 + NS]
        neg_lo = [cols[:, 0:1], cols[:, 1:2]]
        m_one = cols[:, 2:3]

        def tile_of(x, i):
            return x[:, bass.ds(i, 1), :].rearrange("p a c -> p (a c)")

        ld = {n: sem("ld_" + n) for n in ("x", "const", "w1", "f0", "a0", "wqk", "addx", "addw", "f1", "b1", "stage0", "stage1", "zero")}
        LOADS = {
            "const": [(ident, "c_ident"), (masks, "c_masks"), (tri, "c_tri"), (em8, "c_em8"), (k128, "c_k128"),
                      (cols, "c_cols"), (valid, "c_valid"), (small, "c_small")],
            "f0": [(b1, "b1_0"), (w2, "w2_0"), (b2, "b2_0"), (gate_w, "gate_w"), (gate_b, "gate_b")],
            "a0": [(wv[0], "wv_0"), (bv[0], "bv_0"), (wp[0], "wp_0"), (bp[0], "bp_0"),
                   (wv[1], "wv_1"), (bv[1], "bv_1"), (wp[1], "wp_1"), (bp[1], "bp_1")],
            "f1": [(v2, "w2_1"), (c2, "b2_1"), (router_w, "router_w"), (router_b, "router_b")],
        }
        s_set = sem("setup_dve")
        s_constp = sem("const_pool")
        s_consta = sem("const_act")
        s_constd = sem("const_dve")
        s_w1h = sem("w1_high")
        s_w1l = sem("w1_low")
        s_addx = sem("addx_ready")
        s_c1h = sem("c1_high")
        s_c1 = sem("c1_ready")
        s_stage_h = sem("stage_high")
        s_stage_l = sem("stage_low")
        s_out = sem("stored")
        s_zero = sem("zero_ready")

        NAMES = {
            "F0": "ln dln rstd xn tr xt xh xl lgt dch dlg ex cw cwt cwts yb up sg h dn acc",
            "A": "wsc wh wl asc ah al pads ln dln rstd xn tr xt xh xl qk hi qk16 v vs s mt mx mn qm st pf p pl vl pv at atT atS pj acc rec",
            "F1": "ln dln rstd xn tr xt lgt dch oh cnt ntT incl sl offs ohT eidp eid scat xld0 xld1 trx xh xl ohu ohd up sg h trh hT dn y yst0 yst1 gat acc",
        }
        by_kind = {kind: {s: sem(f"{kind}_{s}") for s in NAMES["A" if kind[0] == "A" else kind].split()}
                   for kind in sorted(set(phases))}
        ph = [by_kind[kind] for kind in phases]
        nth = [phases[:n].count(kind) for n, kind in enumerate(phases)]
        NTP = ((NS + 1) // 2, NS // 2)
        attn_phases = [n for n, kind in enumerate(phases) if kind[0] == "A"]
        DLG = 2
        NPV = {"A0": 5, "A1": 2}

        def x_ready(eng, n):
            if n == 0:
                eng.wait_ge(ld["x"], 16)
            else:
                eng.wait_ge(ph[n - 1]["acc"], (nth[n - 1] + 1) * {
                    "F0": NT // CH * (1 + E0 * CH), "A0": NB, "A1": NB, "F1": 4}[phases[n - 1]])

        def slot_tiles(eng, tasks):
            def step(t, r, steady):
                for task, ahead in tasks:
                    p = (t + ahead) % 2
                    turn = (t + ahead - p) // 2
                    if steady:
                        task((r + turn) * 2 + p, p, r + turn, False)
                    elif 0 <= t + ahead < NS:
                        task(t + ahead, p, turn, turn == 0)

            lo, hi = 4, (NS - 3) // 2 * 2
            for t in range(-3, lo):
                step(t, 0, False)
            with eng.Fori(lo // 2, hi // 2) as r:
                step(0, r, True)
                step(1, r, True)
            for t in range(hi, NS + 3):
                step(t, 0, False)

        def sequences(eng, step):
            def at(t):
                return lambda ahead: (t + ahead, (t + ahead) % 2) if 0 <= t + ahead < NB else None

            lo, pairs = 1, (NB - 4) // 2
            for t in range(-3, lo):
                step(at(t))
            with eng.Fori(0, pairs) as r:
                for u in range(2):
                    step(lambda ahead, u=u: (r * 2 + (lo + u + ahead), (lo + u + ahead) % 2))
            for t in range(lo + 2 * pairs, NB + 1):
                step(at(t))

        block = ctx.enter_context(nc.Block())

        @block.sync
        def _(sp):
            sp.dma_start(X[:], d["x"]).then_inc(ld["x"], 16)
            sp.dma_start(stage[:], d["w1_0"]).then_inc(ld["w1"], 16)
            for group in ("const", "f0", "a0", "f1"):
                for dst, src in LOADS[group]:
                    sp.dma_start(dst if dst is masks else dst[:], d[src]).then_inc(ld[group], 16)
            sp.dma_start(c1f[0:E, :], d["b1_1"]).then_inc(ld["b1"], 16)
            sp.dma_start(c1f[E:2 * E, :], d["b1_1"]).then_inc(ld["b1"], 16)
            if "A0" in phases:
                sp.dma_start(wqkf, d["wqk_0"]).then_inc(ld["wqk"], 16)
            sp.wait_ge(s_w1h, 1)
            sp.wait_ge(s_w1l, 1)
            sp.dma_start(stage[0:4, 1536:1536 + SEQ], d["c_addx"]).then_inc(ld["addx"], 16)
            if "A0" in phases:
                sp.dma_start(addf, d["add_0"]).then_inc(ld["addw"], 16)
            sp.wait_ge(s_zero, 1)
            zeros = mpad[:].rearrange("p q g j s -> p (q g j s)").bitcast(F32).rearrange("p (a c) -> p a c", c=P)
            for a in range(0, NS, 4):
                sp.dma_start(xs_dram.rearrange("(a p) c -> p a c", p=P)[:, a:min(a + 4, NS), :],
                             zeros[:, 0:min(4, NS - a), :]).then_inc(ld["zero"], 16)
            def load_second():
                for e in range(E):
                    if e >= 2:
                        sp.wait_ge(s_stage_h, e - 1)
                        sp.wait_ge(s_stage_l, e - 1)
                    sp.dma_start(stage[:, (e % 2) * 2 * HID:(e % 2 + 1) * 2 * HID], d["w1_1"][:, e, :])\
                      .then_inc(ld[f"stage{e % 2}"], 16)

            for n, kind in enumerate(phases):
                s, m = ph[n], nth[n]
                if kind == "A1":
                    x_ready(sp, n)
                    sp.wait_ge(s_addx, 1)
                    sp.dma_start(wqkf, d["wqk_1"]).then_inc(ld["wqk"], 16)
                    sp.dma_start(addf, d["add_1"]).then_inc(ld["addw"], 16)
                if kind == "F1":
                    if n == phases.index("F1"):
                        if n:
                            x_ready(sp, n)
                        sp.wait_ge(s_addx, 1)
                        load_second()

                    def load(i, par, k, first):
                        if not first:
                            sp.wait_ge(s["trx"], NS * m + i - 1)
                        sp.dma_start(xg[:, par, :], xs_dram[bass.ds(i * P, P), :]).then_inc(s[f"xld{par}"], 16)

                    sp.wait_ge(s["scat"], 16 * NT * (m + 1))
                    def store(i, par, k, first):
                        sp.wait_ge(s["y"], NS * m + i + 1)
                        sp.dma_start(ys_dram[bass.ds(i * P, P), :], ysb[:, par, :]).then_inc(s[f"yst{par}"], 16)

                    slot_tiles(sp, [(load, 3), (store, -1)])
            for group in ("a0", "f1"):
                sp.wait_ge(ld[group], 16 * len(LOADS[group]))
            sp.wait_ge(ld["f0"], 16 * len(LOADS["f0"]))
            sp.wait_ge(ld["addx"], 16)
            sp.wait_ge(ld["zero"], 16 * ((NS + 3) // 4))
            if "A0" in phases:
                sp.wait_ge(ld["wqk"], 16)
                sp.wait_ge(ld["addw"], 16)
            x_ready(sp, len(phases))
            sp.dma_start(out, X[:]).then_inc(s_out, 16)
            sp.wait_ge(s_out, 16)

        @block.gpsimd
        def _(pool):
            pool.memset(halfpow[:], -0.5).then_inc(s_constp, 1)
            pool.wait_ge(s_constp, 1)

            def rstd_of(s, i, nt):
                pool.wait_ge(s["ln"], i + 1)
                pool.tensor_tensor(rstd[:, 0:nt], ve[:, 0:nt], halfpow[:, 0:nt], ALU.pow).then_inc(s["rstd"], 1)

            for n, kind in enumerate(phases):
                s, m = ph[n], nth[n]
                if kind == "F0":
                    with pool.Fori(NT // CH * m, NT // CH * (m + 1)) as c:
                        rstd_of(s, c, CH)
                elif kind[0] == "A":
                    NR = len(ROUNDS["causal" if kind == "A0" else "window"])

                    def step(item):
                        now, far = item(0), item(3)
                        if now:
                            i, par = now
                            for r in range(NR):
                                pool.wait_ge(s["pf"], i * NR + (r + 1))
                                at_r = (NR * par + r) % 8
                                pool.tensor_tensor(prob16[1][:, at_r, :, :], prob[:, r % 2, :, :],
                                                   prob16[0][:, at_r, :, :], ALU.subtract).then_inc(s["pl"], 1)
                        if far:
                            rstd_of(s, far[0], 2)

                    sequences(pool, step)
                else:
                    rstd_of(s, m, NT)
                    pool.wait_ge(s["sl"], m + 1)
                    pool.wait_ge(s["xn"], NT * (m + 1))
                    pool.wait_ge(ld["zero"], 16 * ((NS + 3) // 4))
                    for t in range(NT):
                        pool.indirect_dma_start(
                            out=xs_dram, out_offset=bass.IndirectOffsetOnAxis(ap=slot[:, t:t + 1], axis=0),
                            in_=xn[:, t, :], in_offset=None).then_inc(s["scat"], 16)

                    def onehot_up(i, par, k, first):
                        if not first:
                            pool.wait_ge(s["up"], NS * m + i - 1)
                        pool.tensor_copy(oh_up[:, par, :],
                                         ohT[:, bass.ds(i, 1)].broadcast_to([2 * E, P])).then_inc(s["ohu"], 1)

                    def onehot_down(i, par, k, first):
                        if not first:
                            pool.wait_ge(s["dn"], NS * m + i - 1)
                        pool.tensor_copy(oh_down[:, par, :],
                                         ohT[0:E, bass.ds(i, 1)].broadcast_to([E, P])).then_inc(s["ohd"], 1)

                    pool.wait_ge(s["ohT"], m + 1)
                    slot_tiles(pool, [(onehot_up, 2), (onehot_down, 0)])
                    for par in range(2):
                        pool.wait_ge(s[f"yst{par}"], 16 * NTP[par] * (m + 1))
                    pool.wait_ge(s["scat"], 16 * NT * (m + 1))
                    for t in range(NT):
                        pool.indirect_dma_start(
                            out=xn[:, t, :], out_offset=None, in_=ys_dram,
                            in_offset=bass.IndirectOffsetOnAxis(ap=slot[:, t:t + 1], axis=0)).then_inc(s["gat"], 16)

        @block.scalar
        def _(act):
            act.wait_ge(ld["w1"], 16)
            act.activation(w1h[:].rearrange("p e f -> p (e f)"), stage[:], ACT.Copy).then_inc(s_w1h, 1)
            act.wait_ge(ld["const"], 16 * len(LOADS["const"]))
            act.activation(identb[:], ident[:], ACT.Copy).then_inc(s_consta, 1)
            act.activation(ident16[:], ident[:], ACT.Copy).then_inc(s_consta, 1)
            act.activation(masksb[:], masks, ACT.Copy).then_inc(s_consta, 1)
            act.activation(trib[:], tri[:], ACT.Copy).then_inc(s_consta, 1)
            act.wait_ge(ld["b1"], 32)
            act.activation(c1hl[:], c1f, ACT.Copy).then_inc(s_c1h, 1)
            act.wait_ge(ld["addx"], 16)
            act.activation(addx[:], stage[0:4, 1536:1536 + SEQ], ACT.Copy).then_inc(s_addx, 1)

            def split_second():
                for e in range(E):
                    act.wait_ge(ld[f"stage{e % 2}"], 16 * (e // 2 + 1))
                    act.activation(v1h[:, e, :], stage[:, (e % 2) * 2 * HID:(e % 2 + 1) * 2 * HID],
                                   ACT.Copy).then_inc(s_stage_h, 1)

            for n, kind in enumerate(phases):
                s, m = ph[n], nth[n]
                if kind == "F0":
                    act.wait_ge(ld["f0"], 16 * len(LOADS["f0"]))
                    with act.Fori(NT // CH * m, NT // CH * (m + 1)) as c:
                        act.wait_ge(s["tr"], c + 1)
                        act.activation(xT[:], PS[:, 0, :], ACT.Copy).then_inc(s["xt"], 1)
                        act.wait_ge(s["xt"], c + 1)
                        act.activation(xTh[:], xT[:], ACT.Copy).then_inc(s["xh"], 1)
                        act.wait_ge(s["dlg"], c + 1)
                        act.activation(r8[1][:, 0:CH, :], r8[0][:, 0:CH, :], ACT.Exp).then_inc(s["ex"], 1)
                        act.wait_ge(s["cwt"], c + 1)
                        act.activation(cwT[:], PS[0:E0, 0, :], ACT.Copy).then_inc(s["cwts"], 1)
                        for e in range(E0):
                            act.wait_ge(s["up"], c * E0 + e + 1)
                            if e >= 2:
                                act.wait_ge(s["h"], c * E0 + e - 1)
                            act.activation(act_s[:, e % 2, :], PS[:, 2 + 2 * (e % 2), :], ACT.Silu,
                                           bias=b1[:, e, 0:1]).then_inc(s["sg"], 1)
                elif kind[0] == "A":
                    causal = kind == "A0"
                    rounds = ROUNDS["causal" if causal else "window"]
                    NR, NV = len(rounds), 2 if causal else 4
                    act.wait_ge(s["wsc"], 1)
                    act.activation(wqkh[:], wqkf, ACT.Copy).then_inc(s["wh"], 1)
                    act.wait_ge(s["asc"], 1)
                    act.activation(addw[:], addf, ACT.Copy).then_inc(s["ah"], 1)

                    def high_qk(i, par, r):
                        act.wait_ge(s["qk"], i * 4 + (r + 1))
                        if positive(i * 4 + (r - 1)):
                            act.wait_ge(s["qk16"], i * 4 + (r - 1))
                        act.activation(hqk[:, r % 2, :, :], PS[:, 5 + r % 2, :].rearrange("p (g k) -> p g k", g=2),
                                       ACT.Copy).then_inc(s["hi"], 1)

                    def exponentials(i, par, r):
                        act.wait_ge(s["st"], i * NR + (r + 1))
                        if causal:
                            used = i * 5 + (1 if r >= 8 else 0 if r >= 4 else -2)
                        else:
                            used = i * 2 + (r // 4 - 1)
                        if positive(used):
                            act.wait_ge(s["pv"], used)
                        sc = PS[:, 2 + r % 2, :].rearrange("p (g k) -> p g k", g=G)
                        act.activation(prob16[0][:, (NR * par + r) % 8, :, :], sc, ACT.Exp).then_inc(s["p"], 1)
                        if positive(i * NR + (r - 1)):
                            act.wait_ge(s["pl"], i * NR + (r - 1))
                        act.activation(prob[:, r % 2, :, :], sc, ACT.Exp).then_inc(s["pf"], 1)

                    def step(item):
                        prev, now, nxt, nn = (item(ahead) for ahead in (-1, 0, 1, 2))
                        for r in range(LEAD):
                            if now:
                                exponentials(*now, r)
                            if nxt and r < 2:
                                high_qk(*nxt, 2 + r)
                        if nxt:
                            i, par = nxt
                            act.wait_ge(s["v"], i + 1)
                            if positive(i - 1):
                                act.wait_ge(s["pv"], (i - 1) * NPV[kind])
                            act.activation(vaug[par][:, 0, 0:NV, :, 0:HD],
                                           PS[:, 5, 0:NV * P].rearrange("p (t h x) -> p t h x", t=NV, h=H),
                                           ACT.Copy).then_inc(s["vs"], 1)
                        if prev:
                            act.wait_ge(s["atT"], prev[0] + 1)
                            if nn:
                                act.wait_ge(s["tr"], nn[0] + 1)
                            act.activation(attT[:], PS[:, 4, 0:2 * P].rearrange("p (t c) -> p t c", t=2),
                                           ACT.Copy).then_inc(s["atS"], 1)
                        if nn:
                            i, _ = nn
                            act.wait_ge(s["tr"], i + 1)
                            if positive(i):
                                act.wait_ge(s["v"], i)
                            act.activation(xTp[:, PAD:PAD + SEQ], PS[:, 4, SEQ:2 * SEQ], ACT.Copy).then_inc(s["xt"], 1)
                            act.wait_ge(s["xt"], i + 1)
                            act.activation(xTh[:, 0:SEQ], xTp[:, PAD:PAD + SEQ], ACT.Copy).then_inc(s["xh"], 1)
                        if now:
                            for r in range(LEAD, NR):
                                exponentials(*now, r)
                        if nn:
                            high_qk(*nn, 0)
                            high_qk(*nn, 1)

                    sequences(act, step)
                else:
                    if n == phases.index("F1"):
                        split_second()
                    for c in range(4):
                        act.wait_ge(s["tr"], 4 * m + c + 1)
                        if c >= 1:
                            act.wait_ge(s["lgt"], 4 * m + c)
                        act.activation(xT[:], PS[:, 0, :], ACT.Copy).then_inc(s["xt"], 1)

                    def high(i, par, k, first):
                        act.wait_ge(s["trx"], NS * m + i + 1)
                        if not first:
                            act.wait_ge(s["up"], NS * m + i - 1)
                        act.activation(xgh[:, par, :], PS[:, par, 0:P], ACT.Copy).then_inc(s["xh"], 1)

                    def gate(i, par, k, first):
                        act.wait_ge(s["up"], NS * m + i + 1)
                        if not first:
                            act.wait_ge(s["h"], NS * m + i - 1)
                        act.activation(act_s[:, par, :], PS[:, 4 + par, :], ACT.Sigmoid).then_inc(s["sg"], 1)

                    def turned(i, par, k, first):
                        act.wait_ge(s["trh"], NS * m + i + 1)
                        if not first:
                            act.wait_ge(s["dn"], NS * m + i - 1)
                        act.activation(hT[:, par, :], PS[:, 6, :], ACT.Copy).then_inc(s["hT"], 1)

                    slot_tiles(act, [(gate, 1), (turned, 0), (high, 2)])

        @block.vector
        def _(dve):
            ch = Chain(dve, s_set)
            dve.memset(mpad[:], 0.0).then_inc(s_zero, 1)
            for tile_, value in ((onesb, 1.0), (ones1, 1.0), (xTp, 0.0), (cw, 0.5),
                                 (zero8, 0.0)):
                ch.step(dve.memset(tile_[:], value))
            dve.wait_ge(ld["const"], 16 * len(LOADS["const"]))
            dve.wait_ge(s_w1h, 1)
            dve.tensor_tensor(w1l[:].rearrange("p e f -> p (e f)"), stage[:],
                              w1h[:].rearrange("p e f -> p (e f)").bitcast(F32), ALU.subtract).then_inc(s_w1l, 1)
            dve.wait_ge(s_c1h, 1)
            dve.scalar_tensor_tensor(out=c1hl[:], in0=c1hl[:].bitcast(F32), scalar=neg_lo16, in1=c1f,
                                     op0=ALU.mult, op1=ALU.add).then_inc(s_c1, 1)

            def split_second():
                for e in range(E):
                    dve.wait_ge(s_stage_h, e + 1)
                    dve.tensor_tensor(v1l[:, e, :], stage[:, (e % 2) * 2 * HID:(e % 2 + 1) * 2 * HID],
                                      v1h[:, e, :].bitcast(F32), ALU.subtract).then_inc(s_stage_l, 1)

            def layer_norm(s, i, nt, xi):
                ln = Chain(dve, s["dln"], i * 2 * nt)
                for t in range(nt):
                    ln.step(dve.bn_stats(stats[:, t, :], tile_of(X, xi + t)))
                for t in range(nt):
                    if t == 0:
                        ln.wait()
                        dve.memset(spare[:], 0.0)
                    ln.step(dve.bn_aggr(mv[:, t, :], stats[:, t, :]))
                ln.wait()
                dve.tensor_scalar(ve[:, 0:nt], mv[:, 0:nt, 1], EPS, None, ALU.add).then_inc(s["ln"], 1)
                dve.wait_ge(s["rstd"], i + 1)
                for t in range(nt):
                    dve.tensor_scalar(xn[:, t, :], tile_of(X, xi + t), mv[:, t, 0:1], rstd[:, t:t + 1],
                                      ALU.subtract, ALU.mult).then_inc(s["xn"], 1)

            def first_of_max(c, values, nt, eq, top, first, onehot_out):
                c.link(dve.tensor_reduce(top[:, 0:nt], values, AX.X, ALU.max))
                c.link(dve.tensor_tensor(eq[:, 0:nt, :], values, top[:, 0:nt].unsqueeze(2).broadcast_to([P, nt, E]),
                                         ALU.is_equal))
                c.link(dve.tensor_tensor(eq[:, 0:nt, :], eq[:, 0:nt, :], em8[:, 0:nt, :], ALU.mult))
                c.link(dve.tensor_reduce(first[:, 0:nt], eq[:, 0:nt, :], AX.X, ALU.min))
                c.link(dve.tensor_tensor(onehot_out, em8[:, 0:nt, :],
                                         first[:, 0:nt].unsqueeze(2).broadcast_to([P, nt, E]), ALU.is_equal))

            for n, kind in enumerate(phases):
                s, m = ph[n], nth[n]
                x_ready(dve, n)
                if kind == "F0":
                    dve.wait_ge(ld["f0"], 16 * len(LOADS["f0"]))
                    with dve.Fori(NT // CH * m, NT // CH * (m + 1)) as c:
                        c0 = (c - NT // CH * m) * CH
                        layer_norm(s, c, CH, c0)
                        dve.wait_ge(s["xh"], c + 1)
                        dve.tensor_tensor(xTl[:], xT[:], xTh[:].bitcast(F32), ALU.subtract).then_inc(s["xl"], 1)
                        c_ = Chain(dve, s["dch"], c * 16)
                        dve.wait_ge(s["lgt"], c + 1)
                        lg = PS[:, 1, 0:CH * E].rearrange("p (t e) -> p t e", e=E)
                        bc = lambda x: x[:, 0:CH].unsqueeze(2).broadcast_to([P, CH, E])
                        c_.link(dve.tensor_reduce(r1[0][:, 0:CH], lg, AX.X, ALU.max))
                        dve.tensor_tensor(r8[0][:, 0:CH, :], lg, bc(r1[0]), ALU.subtract).then_inc(s["dlg"], 1)
                        dve.wait_ge(s["ex"], c + 1)
                        pr = r8[1][:, 0:CH, :]
                        c_.link(dve.tensor_reduce(r1[0][:, 0:CH], pr, AX.X, ALU.add))
                        c_.link(dve.reciprocal(r1[1][:, 0:CH], r1[0][:, 0:CH]))
                        c_.link(dve.tensor_tensor(pr, pr, bc(r1[1]), ALU.mult))
                        o1, o2, eq = r8[2][:, 0:CH, :], r8[3][:, 0:CH, :], r8[0]
                        first_of_max(c_, pr, CH, eq, r1[0], r1[1], o1)
                        c_.link(dve.scalar_tensor_tensor(out=o2, in0=o1, scalar=-2.0, in1=pr, op0=ALU.mult, op1=ALU.add))
                        first_of_max(c_, o2, CH, eq, r1[0], r1[1], o2)
                        c_.link(dve.tensor_tensor(o1, o1, o2, ALU.add))
                        dve.scalar_tensor_tensor(out=cw[:, :, 0:E], in0=pr, scalar=0.5, in1=o1, op0=ALU.mult,
                                                 op1=ALU.mult).then_inc(s["cw"], 1)
                        assert c_.n == 16, c_.n
                        PER = 1 + E0 * CH

                        def accumulate(e):
                            if e < 0:
                                dve.wait_ge(s["yb"], c + 1)
                                dve.wait_ge(s["cw"], c + 1)
                                xs = X[:, bass.ds(c0, CH), :]
                                dve.tensor_tensor(xs, PS[:, 1, :].rearrange("p (t k) -> p t k", t=CH), xs,
                                                  ALU.add).then_inc(s["acc"], 1)
                                return
                            dve.wait_ge(s["dn"], c * E0 + e + 1)
                            for t in range(CH):
                                dve.wait_ge(s["acc"], c * PER + (1 if e == 0 else 1 + (e - 1) * CH + t + 1))
                                xs = tile_of(X, c0 + t)
                                dve.scalar_tensor_tensor(out=xs, in0=PS[:, 6 + e % 2, t * P:(t + 1) * P],
                                                         scalar=cw[:, t, e:e + 1], in1=xs, op0=ALU.mult,
                                                         op1=ALU.add).then_inc(s["acc"], 1)

                        accumulate(-1)
                        for e in range(E0):
                            dve.wait_ge(s["sg"], c * E0 + e + 1)
                            if e >= 2:
                                dve.wait_ge(s["dn"], c * E0 + e - 1)
                            dve.scalar_tensor_tensor(out=hid[:, e % 2, :], in0=PS[:, 3 + 2 * (e % 2), :],
                                                     scalar=b1[:, e, 1:2], in1=act_s[:, e % 2, :], op0=ALU.add,
                                                     op1=ALU.mult).then_inc(s["h"], 1)
                            if e >= 1:
                                accumulate(e - 1)
                        accumulate(E0 - 1)
                elif kind[0] == "A":
                    k_of_n = attn_phases.index(n)
                    causal = kind == "A0"
                    rounds = ROUNDS["causal" if causal else "window"]
                    NR, NV = len(rounds), 2 if causal else 4
                    dve.wait_ge(ld["a0"], 16 * len(LOADS["a0"]))
                    dve.wait_ge(ld["zero"], 16 * ((NS + 3) // 4))
                    dve.wait_ge(s_set, 5)
                    dve.wait_ge(s_consta, 4)
                    dve.wait_ge(s_c1, 1)
                    w = Chain(dve, s["pads"])
                    for par in range(2):
                        for half in range(2):
                            w.step(dve.memset(vaug[par][:, half, :, :, HD:HD + 1], 1.0 - half))
                        for lo in (0, SEQ + PAD):
                            w.step(dve.memset(k16[par][:, :, lo:lo + PAD], 0.0))
                    w.wait()
                    for par in range(2):
                        for lo in (0, SEQ + PAD):
                            kp = k16[par][:, :, lo:lo + PAD]
                            w.step(dve.tensor_scalar(kp, kp, m_one, None, ALU.add))
                    dve.wait_ge(ld["wqk"], 16 * (k_of_n + 1))
                    dve.wait_ge(ld["addw"], 16 * (k_of_n + 1))
                    dve.tensor_scalar(wqkf[:, 0, :], wqkf[:, 0, :], HD ** -0.5, None, ALU.mult).then_inc(s["wsc"], 1)
                    dve.tensor_scalar(addf[0:2, 0, :], addf[0:2, 0, :], HD ** -0.5, None, ALU.mult).then_inc(s["asc"], 1)
                    dve.wait_ge(s["wh"], 1)
                    dve.tensor_tensor(wqkl[:], wqkf, wqkh[:].bitcast(F32), ALU.subtract).then_inc(s["wl"], 1)
                    dve.wait_ge(s["ah"], 1)
                    dve.scalar_tensor_tensor(out=addw[:], in0=addw[:].bitcast(F32), scalar=cols[0:4, 3:4], in1=addf,
                                             op0=ALU.mult, op1=ALU.add).then_inc(s["al"], 1)

                    def statistics(i):
                        ln = Chain(dve, s["dln"], i * 4)
                        for t in range(2):
                            ln.step(dve.bn_stats(stats[:, t, :], tile_of(X, i * 2 + t)))
                        ln.wait()
                        if positive(i):
                            dve.wait_ge(s["xn"], i * 2)
                        dve.memset(spare[:], 0.0)
                        for t in range(2):
                            ln.step(dve.bn_aggr(mv[:, t, :], stats[:, t, :]))
                        ln.wait()
                        dve.tensor_scalar(ve[:, 0:2], mv[:, 0:2, 1], EPS, None, ALU.add).then_inc(s["ln"], 1)

                    def normalised(i, par):
                        dve.wait_ge(s["rstd"], i + 1)
                        if positive(i - 1):
                            dve.wait_ge(s["tr"], i - 1)
                        for t in range(2):
                            dve.tensor_scalar(xn[:, 2 * par + t, :], tile_of(X, i * 2 + t), mv[:, t, 0:1],
                                              rstd[:, t:t + 1], ALU.subtract, ALU.mult).then_inc(s["xn"], 1)

                    def blend(i, par, r):
                        side, half = r // 2, r % 2
                        dve.wait_ge(s["hi"], i * 4 + (r + 1))
                        if positive(i - 1):
                            dve.wait_ge(s["st"], (i - 1) * NR)
                        gs = slice(2 * half, 2 * half + 2)
                        dst = q16[:, par, gs, :] if side == 0 else k16[par][:, gs, PAD:PAD + SEQ]
                        dve.scalar_tensor_tensor(out=dst, in0=hqk[:, half, :, :], scalar=neg_lo[side],
                                                 in1=PS[:, 5 + half, :].rearrange("p (g k) -> p g k", g=2),
                                                 op0=ALU.mult, op1=ALU.add).then_inc(s["qk16"], 1)

                    def maxima(i, par, r):
                        qt, kb, c = rounds[r]
                        dve.wait_ge(s["s"], i * NR + (r + 1))
                        dst = mtmp[:, kb, :, c] if causal and qt == 1 else mpad[:, qt, :, c, M_SLOT]
                        dve.tensor_reduce(dst, PS[:, r % 2, :].rearrange("p (g k) -> p g k", g=G), AX.X, ALU.max,
                                          negate=True).then_inc(s["mx"], 1)

                    def with_maxima(i, par, qt):
                        dve.wait_ge(s["mt"], i * 2 + (qt + 1))
                        q = q16[:, par, :, qt * P:(qt + 1) * P]
                        dve.tensor_tensor(q, PS[:, 4, :].rearrange("p (g k) -> p g k", g=G), q, ALU.add)\
                           .then_inc(s["qm"], 1)

                    def step(item):
                        prev, now, nxt, nn, far = (item(ahead) for ahead in (-1, 0, 1, 2, 3))
                        if nxt:
                            blend(*nxt, 0)
                            blend(*nxt, 1)
                        if prev:
                            i, _ = prev
                            pv = PS[:, 7, 0:2 * H * (HD + 1)].rearrange("p (t h x) -> p t h x", t=2, h=H)
                            dve.wait_ge(s["pv"], (i + 1) * NPV[kind])
                            dve.reciprocal(rec[:], pv[:, :, :, HD]).then_inc(s["rec"], 1)
                            dve.wait_ge(s["rec"], i + 1)
                            dve.tensor_tensor(att[:].rearrange("p t (h x) -> p t h x", h=H), pv[:, :, :, 0:HD],
                                              rec[:].unsqueeze(3).broadcast_to([P, 2, H, HD]), ALU.mult)\
                               .then_inc(s["at"], 1)
                        if nn:
                            normalised(*nn)
                        if nxt:
                            blend(*nxt, 2)
                            blend(*nxt, 3)
                        for r in range(NR):
                            if nxt:
                                maxima(*nxt, r)
                            if r == 1 and nxt:
                                i, par = nxt
                                dve.wait_ge(s["vs"], i + 1)
                                dve.tensor_tensor(vaug[par][:, 1, 0:NV, :, 0:HD],
                                                  PS[:, 5, 0:NV * P].rearrange("p (t h x) -> p t h x", t=NV, h=H),
                                                  vaug[par][:, 0, 0:NV, :, 0:HD], ALU.subtract).then_inc(s["vl"], 1)
                            if r == NR // 2 - 1 and nn:
                                i, _ = nn
                                dve.wait_ge(s["xh"], i + 1)
                                dve.tensor_tensor(xTl[:, 0:SEQ], xTp[:, PAD:PAD + SEQ], xTh[:, 0:SEQ].bitcast(F32),
                                                  ALU.subtract).then_inc(s["xl"], 1)
                            if r == NR // 2 and prev:
                                i, _ = prev
                                dve.wait_ge(s["pj"], i + 1)
                                xs = X[:, bass.ds(i * 2, 2), :]
                                dve.tensor_tensor(xs, PS[:, 6, 0:2 * P].rearrange("p (t c) -> p t c", t=2), xs,
                                                  ALU.add).then_inc(s["acc"], 1)
                            if r == NR - 2 and nxt:
                                with_maxima(*nxt, 0)
                        if nxt and causal:
                            i, _ = nxt
                            dve.wait_ge(s["mx"], (i + 1) * NR)
                            dve.tensor_tensor(mpad[:, 1, :, :, M_SLOT], mtmp[:, 0, :, :], mtmp[:, 1, :, :],
                                              ALU.min).then_inc(s["mn"], 1)
                        if far:
                            statistics(far[0])
                        if nxt:
                            with_maxima(*nxt, 1)

                    sequences(dve, step)
                else:
                    if n == phases.index("F1"):
                        split_second()
                    dve.wait_ge(ld["f1"], 16 * len(LOADS["f1"]))
                    ln = Chain(dve, s["dln"], 2 * NT * m)
                    for t in range(NT):
                        ln.step(dve.bn_stats(stats[:, t, :], X[:, t, :]))
                    ln.wait()
                    for t in range(NT):
                        ln.step(dve.bn_aggr(mv[:, t, :], stats[:, t, :]))
                    ln.wait()
                    dve.tensor_scalar(ve[:], mv[:, :, 1], EPS, None, ALU.add).then_inc(s["ln"], 1)
                    dve.wait_ge(s["rstd"], m + 1)
                    for t in range(NT):
                        dve.tensor_scalar(xn[:, t, :], X[:, t, :], mv[:, t, 0:1], rstd[:, t:t + 1],
                                          ALU.subtract, ALU.mult).then_inc(s["xn"], 1)
                    dve.wait_ge(s["lgt"], 4 * (m + 1))
                    c_ = Chain(dve, s["dch"], 19 * m)
                    lg = PS[:, 1, 0:NT * E].rearrange("p (t e) -> p t e", e=E)
                    first_of_max(c_, lg, NT, r8[0], r1[0], r1[1], onehot[:])
                    for twice in range(2):
                        c_.step(dve.tensor_reduce(r8[1][:, twice, :], onehot[:].rearrange("p t e -> p e t"), AX.X, ALU.add))
                    c_.wait()
                    dve.tensor_copy(ohsum[:], r8[1][:, 0:2, :]).then_inc(s["oh"], 1)
                    dve.wait_ge(s["cnt"], m + 1)
                    c_.link(dve.tensor_tensor(gtk[:], PS[:, 2, 0:E].unsqueeze(2).broadcast_to([P, E, NT]), k128[:],
                                              ALU.is_gt))
                    c_.link(dve.tensor_reduce(ntl[:, 0, :], gtk[:], AX.X, ALU.add))
                    c_.link(dve.tensor_tensor_scan(ntl[:, 1, :], ntl[:, 0, :], zero8[:], 0.0, ALU.add, ALU.add))
                    c_.link(dve.tensor_tensor(ntl[:, 2, :], ntl[:, 1, :], ntl[:, 0, :], ALU.subtract))
                    c_.link(dve.scalar_tensor_tensor(out=r8[0][:], in0=ntl[:, 2, :].unsqueeze(1).broadcast_to([P, NT, E]),
                                                     scalar=float(P), in1=PS[:, 3, 0:NT * E].rearrange("p (t e) -> p t e", e=E),
                                                     op0=ALU.mult, op1=ALU.add))
                    c_.link(dve.tensor_tensor(r8[0][:], r8[0][:], onehot[:], ALU.mult))
                    c_.link(dve.tensor_reduce(slotf[:], r8[0][:], AX.X, ALU.add))
                    dve.tensor_copy(slot[:], slotf[:]).then_inc(s["sl"], 1)
                    c_.link(dve.tensor_copy(offT[:, 0:1], PS[0:2 * E, 4, 0:1]))
                    c_.link(dve.tensor_scalar(gtT[:], k128T, offT[:, 0:1], None, ALU.is_lt))
                    dve.tensor_reduce(ntT[:], gtT[:], AX.X, ALU.add).then_inc(s["ntT"], 1)
                    dve.wait_ge(s["incl"], m + 1)
                    c_.link(dve.tensor_copy(offT[:], PS[0:2 * E, 4, 0:2]))
                    for k in range(2):
                        c_.step(dve.tensor_scalar(cmpT[:, k, :], iota_s, offT[:, k:k + 1], None, ALU.is_lt))
                    c_.wait()
                    dve.tensor_tensor(ohT[:], cmpT[:, 0, :], cmpT[:, 1, :], ALU.subtract).then_inc(s["ohT"], 1)
                    assert c_.n == 19, c_.n
                    dve.wait_ge(s["eidp"], m + 1)
                    dve.tensor_copy(eid[:], PS[0:1, 4, 0:NS]).then_inc(s["eid"], 1)

                    def low(i, par, k, first):
                        dve.wait_ge(s["xh"], NS * m + i + 1)
                        dve.tensor_tensor(xgl[:, par, :], PS[:, par, 0:P], xgh[:, par, :].bitcast(F32),
                                          ALU.subtract).then_inc(s["xl"], 1)

                    def hidden(i, par, k, first):
                        dve.wait_ge(s["sg"], NS * m + i + 1)
                        if not first:
                            dve.wait_ge(s["trh"], NS * m + i - 1)
                        dve.tensor_tensor(hid[:, par, :], PS[:, 2 + par, :], act_s[:, par, :], ALU.mult).then_inc(s["h"], 1)

                    def result(i, par, k, first):
                        dve.wait_ge(s["dn"], NS * m + i + 1)
                        if not first:
                            dve.wait_ge(s[f"yst{par}"], (NTP[par] * m + k) * 16)
                        dve.tensor_copy(ysb[:, par, :], PS[:, 7, 0:P]).then_inc(s["y"], 1)

                    slot_tiles(dve, [(hidden, 1), (low, 2), (result, -1)])
                    dve.wait_ge(s["gat"], 16 * NT * (m + 1))
                    for c in range(4):
                        xs = X[:, 4 * c:4 * c + 4, :]
                        dve.scalar_tensor_tensor(out=xs, in0=xn[:, 4 * c:4 * c + 4, :], scalar=0.5, in1=xs,
                                                 op0=ALU.mult, op1=ALU.add).then_inc(s["acc"], 1)

        @block.tensor
        def _(pe):
            pe.wait_ge(ld["const"], 16 * len(LOADS["const"]))
            pe.wait_ge(s_consta, 4)
            pe.wait_ge(s_set, 5)

            def mm3(out_, wh, wl, xh, xl, stop=True):
                pe.matmul(out_, wh, xh, start=True, stop=False)
                pe.matmul(out_, wl, xh, start=False, stop=False)
                return pe.matmul(out_, wh, xl, start=False, stop=stop)

            for n, kind in enumerate(phases):
                s, m = ph[n], nth[n]
                if kind == "F0":
                    pe.wait_ge(ld["f0"], 16 * len(LOADS["f0"]))
                    pe.wait_ge(s_w1l, 1)
                    with pe.Fori(NT // CH * m, NT // CH * (m + 1)) as c:
                        pe.wait_ge(s["xn"], (c + 1) * CH)
                        for t in range(CH):
                            ins = pe.transpose(PS[:, 0, t * P:(t + 1) * P], xn[:, t, :], ident[:])
                        ins.then_inc(s["tr"], 1)
                        pe.wait_ge(s["xt"], c + 1)
                        for t in range(CH):
                            o = PS[:, 1, t * E:(t + 1) * E]
                            pe.matmul(o, xT[:, t * P:(t + 1) * P], gate_w[:], start=True, stop=False)
                            ins = pe.matmul(o, ones1[:], gate_b[:], start=False, stop=True)
                        ins.then_inc(s["lgt"], 1)

                        def up(e):
                            if e >= 2:
                                pe.wait_ge(s["h"], c * E0 + e - 1)
                            for half in range(2):
                                w = slice(half * P, (half + 1) * P)
                                ins = mm3(PS[:, 2 + 2 * (e % 2) + half, :], w1h[:, e, w], w1l[:, e, w], xTh[:], xTl[:])
                            ins.then_inc(s["up"], 1)

                        def down(e):
                            pe.wait_ge(s["h"], c * E0 + e + 1)
                            if e >= 2:
                                pe.wait_ge(s["acc"], c * (1 + E0 * CH) + 1 + (e - 1) * CH)
                            for t in range(CH):
                                ins = pe.matmul(PS[:, 6 + e % 2, t * P:(t + 1) * P], hid[:, e % 2, t * P:(t + 1) * P],
                                                w2[:, e, :], start=True, stop=True)
                            ins.then_inc(s["dn"], 1)

                        pe.wait_ge(s["xl"], c + 1)
                        up(0)
                        up(1)
                        pe.wait_ge(s["cw"], c + 1)
                        for t in range(CH):
                            ins = pe.transpose(PS[0:E0, 0, t * P:(t + 1) * P], cw[:, t, :], ident[:])
                        ins.then_inc(s["cwt"], 1)
                        pe.wait_ge(s["cwts"], c + 1)
                        for t in range(CH):
                            ins = pe.matmul(PS[:, 1, t * P:(t + 1) * P], cwT[:, t * P:(t + 1) * P], b2[:],
                                            start=True, stop=True)
                        ins.then_inc(s["yb"], 1)
                        for e in range(E0):
                            if e >= 1 and e + 1 < E0:
                                up(e + 1)
                            down(e)
                elif kind[0] == "A":
                    a = int(kind[1])
                    causal = kind == "A0"
                    rounds = ROUNDS["causal" if causal else "window"]
                    NR, NV = len(rounds), 2 if causal else 4
                    pe.wait_ge(ld["a0"], 16 * len(LOADS["a0"]))
                    pe.wait_ge(s["wl"], 1)
                    pe.wait_ge(s["al"], 1)
                    pe.wait_ge(s_addx, 1)
                    pe.wait_ge(s["pads"], 12)

                    def queries_keys(i, par, r):
                        side, half = r // 2, r % 2
                        if r >= 2:
                            pe.wait_ge(s["qk16"], i * 4 + (r - 1))
                        elif r == 0:
                            pe.wait_ge(s["xl"], i + 1)
                            if positive(i):
                                pe.wait_ge(s["vl"], i)
                        elif positive(i - 2):
                            pe.wait_ge(s["acc"], i - 2)
                        for gg in range(2):
                            g = 2 * half + gg
                            w = slice(g * P, (g + 1) * P)
                            o = PS[:, 5 + half, gg * SEQ:(gg + 1) * SEQ]
                            mm3(o, wqkh[:, side, w], wqkl[:, side, w], xTh[:, 0:SEQ], xTl[:, 0:SEQ], stop=False)
                            ins = pe.matmul(o, addw[:, side, w], addx[:], start=False, stop=True)
                        ins.then_inc(s["qk"], 1)

                    def masked(bank, which):
                        pe.matmul(PS[:, bank, :].rearrange("p (g k) -> p g k", g=G), identb[:],
                                  masksb[:, which, :].unsqueeze(1).broadcast_to([P, G, P]),
                                  start=True, stop=False, skip_group_check=True)

                    def scores(i, par, r):
                        qt, kb, c = rounds[r]
                        if r == 0:
                            pe.wait_ge(s["qk16"], i * 4 + 4)
                        if positive(i * NR + (r - 1)):
                            pe.wait_ge(s["mx"], i * NR + (r - 1))
                        diagonal = not causal or qt == kb
                        if diagonal:
                            masked(r % 2, 0 if causal else 2)
                        sl = slice(SL * c, SL * (c + 1))
                        for g in range(G):
                            o = PS[:, r % 2, g * P:(g + 1) * P]
                            if causal:
                                ins = pe.matmul(o, q16[sl, par, g, qt * P:(qt + 1) * P],
                                                k16[par][sl, g, PAD + kb * P:PAD + (kb + 1) * P],
                                                start=not diagonal, stop=True, skip_group_check=True)
                            else:
                                for w in range(2):
                                    lo = (2 * qt + w) * WIN
                                    ins = pe.matmul(o[w * WIN:(w + 1) * WIN, :], q16[sl, par, g, lo:lo + WIN],
                                                    k16[par][sl, g, lo:lo + P], start=False, stop=True,
                                                    skip_group_check=True)
                        ins.then_inc(s["s"], 1)

                    def scores_turned(i, par, r):
                        qt, kb, c = rounds[r]
                        if (qt, kb, c) in ((0, 0, 0), (1, 0, 0)):
                            pe.wait_ge(s["qm"], i * 2 + (qt + 1))
                        if positive(i * NR + (r - 1)):
                            pe.wait_ge(s["pf"], i * NR + (r - 1))
                        diagonal = not causal or qt == kb
                        if diagonal:
                            masked(2 + r % 2, 1 if causal else 3)
                        sl = slice(SL * c, SL * (c + 1))
                        for g in range(G):
                            o = PS[:, 2 + r % 2, g * P:(g + 1) * P]
                            if causal:
                                ins = pe.matmul(o, k16[par][sl, g, PAD + kb * P:PAD + (kb + 1) * P],
                                                q16[sl, par, g, qt * P:(qt + 1) * P],
                                                start=not diagonal, stop=True, skip_group_check=True)
                            else:
                                for w in range(2):
                                    lo = (2 * qt + w) * WIN
                                    ins = pe.matmul(o[:, w * WIN:(w + 1) * WIN], k16[par][sl, g, lo:lo + P],
                                                    q16[sl, par, g, lo:lo + WIN], start=False, stop=True,
                                                    skip_group_check=True)
                        ins.then_inc(s["st"], 1)

                    def weighted(i, par, qt, heads):
                        if qt == 0:
                            pe.wait_ge(s["vl"], i + 1)
                            if positive(i):
                                pe.wait_ge(s["at"], i)
                        last = max(r for r, (q, _, c) in enumerate(rounds) if q == qt and c in heads)
                        pe.wait_ge(s["pl"], i * NR + (last + 1))
                        for c in heads:
                            for g in range(G):
                                at = (qt * H + 4 * g + c) * (HD + 1)
                                o = PS[:, 7, at:at + HD + 1]
                                for kb in range(qt + 1 if causal else 1):
                                    at_r = (NR * par + rounds.index((qt, kb, c))) % 8
                                    for n_, (hp, hv) in enumerate(((0, 0), (1, 0), (0, 1))):
                                        pr = prob16[hp][:, at_r, g, :]
                                        if causal:
                                            ins = pe.matmul(o, pr, vaug[par][:, hv, kb, 4 * g + c, :],
                                                            start=kb == 0 and n_ == 0, stop=kb == qt and n_ == 2)
                                        else:
                                            for w in range(2):
                                                ins = pe.matmul(o[w * WIN:(w + 1) * WIN, :], pr[:, w * WIN:(w + 1) * WIN],
                                                                vaug[par][:, hv, 2 * qt + w, 4 * g + c, :],
                                                                start=n_ == 0, stop=n_ == 2, skip_group_check=True)
                        ins.then_inc(s["pv"], 1)

                    def turn_maxima(i, qt):
                        if qt == 1:
                            if causal:
                                pe.wait_ge(s["mn"], i + 1)
                            else:
                                pe.wait_ge(s["mx"], (i + 1) * NR)
                            pe.wait_ge(s["qm"], i * 2 + 1)
                        else:
                            pe.wait_ge(s["mx"], i * NR + 4)
                            if positive(i - 1):
                                pe.wait_ge(s["atS"], i - 1)
                        for g in range(G):
                            ins = pe.matmul(PS[:, 4, g * P:(g + 1) * P],
                                            mpad[:, qt, g, :, :].rearrange("p j s -> p (j s)"), ident16[:],
                                            start=True, stop=True)
                        ins.then_inc(s["mt"], 1)

                    after = ({3: (0, range(4)), 6: (1, (0,)), 8: (1, (1,)), 10: (1, (2,)), 11: (1, (3,))} if causal else
                             {3: (0, range(4)), 6: (1, range(4))})

                    def step(item):
                        prev, now, nxt, nn = (item(ahead) for ahead in (-1, 0, 1, 2))
                        for r in range(LEAD):
                            if now:
                                scores_turned(*now, r)
                            if nxt and r < 2:
                                queries_keys(*nxt, 2 + r)
                        if nxt:
                            i, _ = nxt
                            pe.wait_ge(s["qk16"], i * 4 + 3)
                            for t in range(NV):
                                lo = PAD + t * P if causal else t * WIN
                                o = PS[:, 5, t * P:(t + 1) * P]
                                pe.matmul(o, xTp[:, lo:lo + P], wv[a][:], start=True, stop=False)
                                ins = pe.matmul(o, valid[:, lo:lo + P], bv[a][:], start=False, stop=True)
                            ins.then_inc(s["v"], 1)
                        if prev:
                            i, _ = prev
                            pe.wait_ge(s["at"], i + 1)
                            if now:
                                pe.wait_ge(s["qm"], (i + 2) * 2)
                            for t in range(2):
                                ins = pe.transpose(PS[:, 4, t * P:(t + 1) * P], att[:, t, :], ident[:])
                            ins.then_inc(s["atT"], 1)
                        if nn:
                            i, par = nn
                            pe.wait_ge(s["xn"], (i + 1) * 2)
                            if positive(i - 1):
                                pe.wait_ge(s["qm"], (i - 1) * 2)
                            for t in range(2):
                                ins = pe.transpose(PS[:, 4, SEQ + t * P:SEQ + (t + 1) * P], xn[:, 2 * par + t, :], ident[:])
                            ins.then_inc(s["tr"], 1)
                        for r in range(NR):
                            if nxt:
                                scores(*nxt, r)
                            if now and r + LEAD < NR:
                                scores_turned(*now, r + LEAD)
                            if now and r in after:
                                weighted(*now, *after[r])
                            if r == 3 and prev:
                                i, _ = prev
                                pe.wait_ge(s["atS"], i + 1)
                                for t in range(2):
                                    o = PS[:, 6, t * P:(t + 1) * P]
                                    pe.matmul(o, attT[:, t, :], wp[a][:], start=True, stop=False)
                                    ins = pe.matmul(o, ones1[:], bp[a][:], start=False, stop=True)
                                ins.then_inc(s["pj"], 1)
                            if r == NR // 2 and nxt:
                                if nn:
                                    pe.wait_ge(s["xt"], nn[0] + 1)
                                turn_maxima(nxt[0], 0)
                        if nn:
                            queries_keys(*nn, 0)
                            queries_keys(*nn, 1)
                        if nxt:
                            turn_maxima(nxt[0], 1)

                    sequences(pe, step)
                else:
                    pe.wait_ge(ld["f1"], 16 * len(LOADS["f1"]))
                    for c in range(4):
                        pe.wait_ge(s["xn"], NT * m + (c + 1) * 4)
                        if c >= 1:
                            pe.wait_ge(s["xt"], 4 * m + c)
                        for t in range(4):
                            ins = pe.transpose(PS[:, 0, t * P:(t + 1) * P], xn[:, 4 * c + t, :], ident[:])
                        ins.then_inc(s["tr"], 1)
                        pe.wait_ge(s["xt"], 4 * m + c + 1)
                        for t in range(4):
                            o = PS[:, 1, (4 * c + t) * E:(4 * c + t + 1) * E]
                            pe.matmul(o, xT[:, t * P:(t + 1) * P], router_w[:], start=True, stop=False)
                            ins = pe.matmul(o, ones1[:], router_b[:], start=False, stop=True)
                        ins.then_inc(s["lgt"], 1)
                    pe.wait_ge(s["oh"], m + 1)
                    pe.matmul(PS[:, 2, 0:E], onesb[:], ohsum[:, 0, :], start=True, stop=True)
                    pe.matmul(PS[0:2 * E, 4, 0:1], ohsum[:].rearrange("p a e -> p (a e)"), onesb[:, 0:1],
                              start=True, stop=True)
                    oh = onehot[:].rearrange("p t e -> p (t e)")
                    for back in range(1, NT):
                        pe.matmul(PS[:, 3, back * E:NT * E], onesb[:], oh[:, 0:(NT - back) * E],
                                  start=back == 1, stop=False, skip_group_check=True)
                    pe.matmul(PS[:, 3, 0:NT * E], trib[:], oh, start=False, stop=True,
                              skip_group_check=True).then_inc(s["cnt"], 1)
                    pe.wait_ge(s["ntT"], m + 1)
                    pe.matmul(PS[0:2 * E, 4, 0:1], tri_incl, ntT[:], start=True, stop=True)
                    pe.matmul(PS[0:2 * E, 4, 1:2], tri_excl, ntT[:], start=True, stop=True).then_inc(s["incl"], 1)
                    pe.wait_ge(s["ohT"], m + 1)
                    pe.matmul(PS[0:1, 4, 0:NS], eid_col, ohT[:], start=True, stop=True).then_inc(s["eidp"], 1)
                    pe.wait_ge(s["eid"], m + 1)
                    pe.wait_ge(s_c1, 1)
                    pe.wait_ge(s_stage_l, E)

                    vh = v1h[:].rearrange("p e f -> p (e f)")
                    vl = v1l[:].rearrange("p e f -> p (e f)")
                    v2_ = v2[:].rearrange("p e q c -> p (e q c)")

                    def turn_rows(i, par, k, first):
                        pe.wait_ge(s[f"xld{par}"], (NTP[par] * m + k + 1) * 16)
                        pe.transpose(PS[:, par, 0:P], xg[:, par, :], ident[:]).then_inc(s["trx"], 1)

                    def up(i, par, k, first):
                        e = pe.value_load(eid[0:1, bass.ds(i, 1)], min_val=0, max_val=E - 1)
                        pe.wait_ge(s["xl"], NS * m + i + 1)
                        pe.wait_ge(s["ohu"], NS * m + i + 1)
                        if not first:
                            pe.wait_ge(s["h"], NS * m + i - 1)
                        for half, bank in ((1, 4 + par), (0, 2 + par)):
                            at = e * (2 * HID) + half * HID
                            o = PS[:, bank, :]
                            pe.matmul(o, oh_up[:, par, :], c1hl[:, half * HID:(half + 1) * HID],
                                      start=True, stop=False)
                            pe.matmul(o, xgh[:, par, :], vh[:, bass.ds(at, HID)], start=False, stop=False)
                            pe.matmul(o, xgl[:, par, :], vh[:, bass.ds(at, HID)], start=False, stop=False)
                            ins = pe.matmul(o, xgh[:, par, :], vl[:, bass.ds(at, HID)], start=False, stop=True)
                        ins.then_inc(s["up"], 1)

                    def turn_hidden(i, par, k, first):
                        pe.wait_ge(s["h"], NS * m + i + 1)
                        if not first or par == 1:
                            pe.wait_ge(s["hT"], NS * m + i)
                        for q in range(4):
                            ins = pe.transpose(PS[:, 6, q * P:(q + 1) * P], hid[:, par, q * P:(q + 1) * P], ident[:])
                        ins.then_inc(s["trh"], 1)

                    def down(i, par, k, first):
                        e = pe.value_load(eid[0:1, bass.ds(i, 1)], min_val=0, max_val=E - 1)
                        pe.wait_ge(s["hT"], NS * m + i + 1)
                        pe.wait_ge(s["ohd"], NS * m + i + 1)
                        if not first or par == 1:
                            pe.wait_ge(s["y"], NS * m + i)
                        for q in range(4):
                            pe.matmul(PS[:, 7, 0:P], hT[:, par, q * P:(q + 1) * P],
                                      v2_[:, bass.ds(e * HID + q * P, P)], start=q == 0, stop=False)
                        pe.matmul(PS[:, 7, 0:P], oh_down[:, par, :], c2[:], start=False, stop=True)\
                          .then_inc(s["dn"], 1)

                    slot_tiles(pe, [(up, 1), (turn_hidden, 0), (turn_rows, 2), (down, -1)])


def _constants():
    import numpy as np
    f = np.float32
    i = np.arange(P)
    c = {"c_ident": np.eye(P, dtype=f)}
    q, k = i[:, None], i[None, :]
    causal = np.where(k > q, NEG, 0.0)
    w = np.where((k >= q % WIN) & (k < q % WIN + WIN), 0.0, NEG)
    c["c_masks"] = np.stack([causal, causal.T, w, w.T], axis=1).astype(f)
    c["c_tri"] = (q < k).astype(f)
    c["c_em8"] = np.broadcast_to(np.arange(E) - float(E), (P, NT, E)).astype(f)
    c["c_k128"] = np.broadcast_to(float(P) * np.arange(NT), (P, E, NT)).astype(f)
    slot = i % SL
    cols = np.zeros((P, 4), f)
    cols[:, 0] = np.where((slot >= HD) & (slot < 2 * HD), -1, 0)
    cols[:, 1] = np.where((slot >= 2 * HD) & (slot < 3 * HD), -1, 0)
    cols[:, 2] = slot == M_SLOT
    cols[1, 3] = -1
    c["c_cols"] = cols
    v = np.zeros((1, SEQ + 2 * PAD), f)
    v[:, PAD:PAD + SEQ] = 1
    c["c_valid"] = v
    e = np.arange(2 * E)
    same = (e[:, None] // E) == (e[None, :] // E)
    c["c_small"] = np.concatenate([
        np.broadcast_to(float(P) * np.arange(16), (2 * E, 16)),
        same & (e[:, None] <= e[None, :]), same & (e[:, None] < e[None, :]),
        np.broadcast_to(np.arange(NS), (2 * E, NS)), np.where(e < E, e, 0)[:, None], -(e >= E)[:, None].astype(f)],
        axis=1).astype(f)
    c["c_addx"] = np.stack([np.ones(SEQ), np.ones(SEQ), np.ones(SEQ), np.arange(SEQ)]).astype(f)
    return c


def _laid_out(i):
    import numpy as np

    def slots(w, b, k0):
        n = w.shape[0]
        pw, pb = np.zeros((n, H, SL), w.dtype), np.zeros((H, SL), w.dtype)
        for r in range(3):
            pw[:, :, r * HD:(r + 1) * HD] = w[:, k0:k0 + P].reshape(n, H, HD)
            pb[:, r * HD:(r + 1) * HD] = b[k0:k0 + P].reshape(H, HD)
        return pw.reshape(n, H * SL), pb.reshape(H * SL)

    a = {"x": i["L0_attn_x"].reshape(NT, P, P).transpose(1, 0, 2)}
    w1 = np.concatenate([i["L0_ffn_rw1"], i["L0_ffn_sw1"]])
    a["w1_0"] = w1.transpose(1, 0, 2).reshape(P, E0 * 2 * P)
    b1 = np.concatenate([i["L0_ffn_rb1"], i["L0_ffn_sb1"]])
    a["b1_0"] = b1.reshape(E0, 2, P).transpose(2, 0, 1)
    a["w2_0"] = np.concatenate([i["L0_ffn_rw2"], i["L0_ffn_sw2"]]).transpose(1, 0, 2)
    a["b2_0"] = np.concatenate([i["L0_ffn_rb2"], i["L0_ffn_sb2"]])
    a["gate_w"], a["gate_b"] = i["L0_ffn_gate_w"], i["L0_ffn_gate_b"][None]
    for n, (w, b, wp, bp) in enumerate([
            (i["L0_attn_W_attn"], i["L0_attn_b_attn"], i["L0_attn_W_proj"], i["L0_attn_b_proj"]),
            (i["L1_attn_Wqkv"].T, i["L1_attn_bqkv"], i["L1_attn_Wout"].T, i["L1_attn_bout"])]):
        qw, qb = slots(w, b, 0)
        kw, kb = slots(w, b, P)
        a[f"wqk_{n}"] = np.stack([qw, kw], axis=1)
        const, slope = np.zeros((2, H, SL), w.dtype), np.zeros((2, H, SL), w.dtype)
        const[1, :, M_SLOT] = 1
        if n == 0:
            const[0, :, 24] = const[1, :, 25] = 1
            slope[1, :, 24] = 2.0 ** -np.arange(1, H + 1)
            slope[0, :, 25] = -slope[1, :, 24]
        b2 = np.stack([qb, kb])
        a[f"add_{n}"] = np.stack([b2, b2, const.reshape(2, -1), slope.reshape(2, -1)])
        a[f"wv_{n}"], a[f"bv_{n}"] = w[:, 2 * P:], b[None, 2 * P:]
        a[f"wp_{n}"], a[f"bp_{n}"] = wp, bp[None]
    a["router_w"], a["router_b"] = i["L1_ffn_router_w"], i["L1_ffn_router_b"][None]
    a["w1_1"] = i["L1_ffn_w1"].transpose(1, 0, 2)
    a["b1_1"] = i["L1_ffn_b1"]
    a["w2_1"] = i["L1_ffn_w2"].reshape(E, HID // P, P, P).transpose(2, 0, 1, 3)
    a["b2_1"] = i["L1_ffn_b2"]
    return a


def kernel(**inputs):
    import numpy as np
    import concourse.bacc as bacc
    from concourse.bass_utils import run_bass_kernel_spmd

    nc = bacc.Bacc("TRN2", target_bir_lowering=False, num_devices=1)
    arrays, d = {}, {}
    for name, a in {**_laid_out({k: np.asarray(v) for k, v in inputs.items()}), **_constants()}.items():
        a = np.ascontiguousarray(a)
        arrays[f"in_{name}"] = a
        d[name] = nc.dram_tensor(f"in_{name}", a.shape, mybir.dt.from_np(a.dtype), kind="ExternalInput").ap()
    out = nc.dram_tensor("out_x", (P, NT, P), F32, kind="ExternalOutput").ap()
    macaron(nc, d, out)
    r = run_bass_kernel_spmd(nc, [arrays], core_ids=[0])
    got = r.results[0]["out_x"]
    return got.transpose(1, 0, 2).reshape(NB, SEQ, P)
```

```python
from contextlib import ExitStack

import concourse.bass as bass
from concourse import mybir

F32 = mybir.dt.float32
F32R = mybir.dt.float32r
F16 = mybir.dt.float16
BF16 = mybir.dt.bfloat16
U32 = mybir.dt.uint32
I32 = mybir.dt.int32
ALU = mybir.AluOpType
ACT = mybir.ActivationFunctionType
AX = mybir.AxisListType

P = 128
NT = 16
NB = 8
SEQ = 256
H = 16
HD = P // H
G = 4
SL = 32
M_SLOT = 26
E = 8
E0 = E + 1
HID = 512
WIN = 64
PAD = WIN // 2
NEG = -1e30
EPS = 1e-5
CH = 4
NS = NT + E - 1
ROUNDS = {"causal": [(0, 0, c) for c in range(4)] + [(1, kb, c) for c in range(4) for kb in range(2)],
          "window": [(qt, 0, c) for qt in range(2) for c in range(4)]}
PLACES = {"A0": dict(low=5, project=3, add=6, turn=6, join=10, products=(9, 11), high=(10, 11)),
          "A1": dict(low=1, project=2, add=3, turn=4, join=6, products=(3, 5), high=(5, 6))}
LEAD = 4


def positive(value):
    return not isinstance(value, int) or value > 0


class Chain:

    def __init__(self, eng, sem, base=0):
        self.eng, self.sem, self.base, self.n = eng, sem, base, 0

    def step(self, ins):
        self.n += 1
        ins.then_inc(self.sem, 1)

    def wait(self):
        self.eng.wait_ge(self.sem, self.base + self.n)

    def link(self, ins):
        self.step(ins)
        self.wait()


def macaron(nc, d, out, phases=("F0", "A0", "F0", "F1", "A1", "F1")):
    ctx = ExitStack()
    with ctx:
        def sb(name, shape, dt=F32):
            return ctx.enter_context(nc.sbuf_tensor(name, shape, dt))

        def sem(name):
            return ctx.enter_context(nc.semaphore(name))

        X = sb("residual", [P, NT, P])
        ident = sb("ident", [P, P])
        identb = sb("identb", [P, P], BF16)
        masksb = sb("masksb", [P, 4, P], BF16)
        tri = sb("tri", [P, P])
        trib = sb("trib", [P, P], BF16)
        onesb = sb("onesb", [P, P], BF16)
        ones1 = sb("ones1", [P, P])
        em8 = sb("em8", [P, NT, E])
        k128 = sb("k128", [P, E, NT])
        cols = sb("cols", [P, 4])
        valid = sb("valid", [P, SEQ + 2 * PAD])
        small = sb("small", [2 * E, 3 * 16 + NS + 2])
        halfpow = sb("halfpow", [P, NT])
        stage = sb("stage", [P, E0 * 2 * P])
        w1h = sb("w1h", [P, E0, 2 * P], F32R)
        w1l = sb("w1l", [P, E0, 2 * P], F32R)
        b1 = sb("b1", [P, E0, 2])
        w2 = sb("w2", [P, E0, P])
        b2 = sb("b2", [E0, P])
        gate_w = sb("gate_w", [P, E])
        gate_b = sb("gate_b", [P, E])
        wqkh = sb("wqkh", [P, 2, G * P], F32R)
        wqkl = sb("wqkl", [P, 2, G * P], F32R)
        addw = sb("addw", [P, 2, G * P], F32R)
        addx = sb("addx", [P, SEQ], F32R)
        wv = [sb(f"wv{a}", [P, P]) for a in range(2)]
        bv = [sb(f"bv{a}", [P, P]) for a in range(2)]
        wp = [sb(f"wp{a}", [P, P]) for a in range(2)]
        bp = [sb(f"bp{a}", [P, P]) for a in range(2)]
        v1h = sb("v1h", [P, E, 2 * HID], F32R)
        v1l = sb("v1l", [P, E, 2 * HID], F32R)
        v2 = sb("v2", [P, E, HID // P, P])
        c1hl = sb("c1hl", [2 * E, 2 * HID], F32R)
        c2 = sb("c2", [E, P])
        router_w = sb("router_w", [P, E])
        router_b = sb("router_b", [P, E])
        xn = sb("xn", [P, NT, P + 1])
        stats = sb("stats", [P, NT, 6])
        mv = sb("mv", [P, NT, 2])
        ve = sb("ve", [P, NT])
        rstd = sb("rstd", [P, NT])
        big = sb("big", [P, 8 * G * P])
        xT = sb("xT", [P, CH * P])
        xT2 = [xT[:], big[:, 1024:1536]]
        xTp = sb("xTp", [P, SEQ + 2 * PAD])
        xTh = sb("xTh", [P, CH * P], F32R)
        xTl = sb("xTl", [P, CH * P], F32R)
        r8 = [sb(f"r8_{i}", [P, NT, E]) for i in range(4)]
        r1 = [sb(f"r1_{i}", [P, NT]) for i in range(3)]
        xTh4 = v1h[:, 0:2, :].rearrange("p e (c k) -> p (e c) k", k=CH * P)
        xTl4 = v1l[:, 0:2, :].rearrange("p e (c k) -> p (e c) k", k=CH * P)
        cw = sb("cw", [P, NT, E0])
        cw_chunk = sb("cw_chunk", [P, CH, E0])
        cwT = sb("cwT", [E0, CH * P])
        prob = stage[:, 512:1536].rearrange("p (r g k) -> p r g k", r=2, g=G)
        masks = big[:, 0:4 * P].rearrange("p (a c) -> p a c", a=4)
        prob16 = [big[:, 2048 * half:2048 * (half + 1)].bitcast(F16).rearrange("p (r g k) -> p r g k", r=8, g=G)
                  for half in range(2)]
        act_s = big[:, 0:1024].rearrange("p (a b) -> p a b", a=2)
        hid = big[:, 1024:2048].rearrange("p (a b) -> p a b", a=2)
        hT = big[:, 2048:3072].rearrange("p (a b) -> p a b", a=2)
        wqkf = big[:, 3072:4096].rearrange("p (s c) -> p s c", s=2)
        hqk = stage[:, 0:512].bitcast(F16).rearrange("p (a g k) -> p a g k", a=2, g=2)
        addf = [x.rearrange("p (s c) -> p s c", s=2) for x in (big[:, 2048:3072], stage[:, 0:1024])]
        q16 = sb("q16", [P, 2, G, SEQ], F16)
        c1f = q16[0:2 * E].rearrange("p a g k -> p (a g k)").bitcast(F32)
        KW = SEQ + 2 * PAD
        flat = xn[:].rearrange("p a c -> p (a c)")
        k16 = [sb("k16", [P, G, KW], F16)[:],
               flat[:, 4 * (P + 1):4 * (P + 1) + G * KW // 2].bitcast(F16).rearrange("p (g k) -> p g k", g=G)]
        vaug = [sb("vaug", [P, 2, 4, H, HD + 1], F16)[:],
                flat[:, 10 * P:10 * P + 4 * H * (HD + 1)].bitcast(F16)
                .rearrange("p (l t h x) -> p l t h x", l=2, t=4, h=H)]
        mtmp = sb("mtmp", [P, 2, G, 4])
        mpad = sb("mpad", [P, 2, G, 4, SL], F16)
        ident16 = sb("ident16", [P, P], F16)
        rec = sb("rec", [P, 2, H])
        att = sb("att", [P, 2, P])
        addxf = att[:].rearrange("p a c -> p (a c)")
        attT = sb("attT", [P, 2, P])
        onehot = sb("onehot", [P, NT, E], BF16)
        ohsum = sb("ohsum", [P, 2, E], BF16)
        gtk = sb("gtk", [P, E, NT])
        ntl = sb("ntl", [P, 3, E])
        spare = sb("spare", [P, 1])
        spare_pool = sb("spare_pool", [P, 2])
        zero8 = sb("zero8", [P, E])
        slotf = sb("slotf", [P, NT])
        slot = sb("slot", [P, NT], U32)
        gtT = sb("gtT", [2 * E, 16])
        ntT = sb("ntT", [2 * E, 1])
        offT = sb("offT", [2 * E, 2])
        cmpT = sb("cmpT", [2 * E, 2, NS])
        ohT = sb("ohT", [2 * E, NS])
        eid = sb("eid", [1, NS], I32)
        oh_up = xTh[0:2 * E, 0:2 * P].rearrange("p (a k) -> p a k", a=2)
        xg = q16[:, 0].rearrange("p g k -> p (g k)")[:, 0:512].bitcast(F32).rearrange("p (a k) -> p a k", a=2)
        ids = sb("ids", [P, NT])
        idf = sb("idf", [P, NS])
        idu = sb("idu", [P, NS], U32)
        unused = sb("unused", [P, NS])
        rest = sb("rest", [P, NS])
        idt = sb("idt", [P, 2], U32)
        oh_down = attT[0:E]
        xgh = sb("xgh", [P, 2, P], F32R)
        xgl = sb("xgl", [P, 2, P], F32R)
        ysb = att
        PS = ctx.enter_context(nc.psum_tensor("PS", [P, 8, 512], F32))

        xs_dram = [nc.dram_tensor(f"xs_dram{k}", [NS * P, P + 1], F32).ap() for k in range(phases.count("F1"))]
        yt_dram = nc.dram_tensor("yt_dram", [1 + (NT + NS) * P, P], F32).ap()
        ZW = 512
        ZEROED = [(k, lo, min(lo + ZW, NS * (P + 1))) for k in range(len(xs_dram)) for lo in range(0, NS * (P + 1), ZW)]

        k128T = small[:, 0:16]
        tri_incl = small[:, 16:32]
        tri_excl = small[:, 32:48]
        iota_s = small[:, 48:48 + NS]
        eid_col = small[:, 48 + NS:49 + NS]
        neg_lo16 = small[:, 49 + NS:50 + NS]
        neg_lo = [cols[:, 0:1], cols[:, 1:2]]
        m_one = cols[:, 2:3]

        PER = 1 + E0 * CH

        def added(j, e):
            return j * PER + CH * (e + 1) + 1

        def tile_of(x, i):
            return x[:, bass.ds(i, 1), :].rearrange("p a c -> p (a c)")

        ld = {n: sem("ld_" + n) for n in ("x", "const", "w1", "f0", "a0", "wqk", "addx", "addw", "f1", "b1", "stage0", "stage1", "zero")}
        LOADS = {
            "const": [(ident, "c_ident"), (masks, "c_masks"), (tri, "c_tri"), (em8, "c_em8"), (k128, "c_k128"),
                      (cols, "c_cols"), (ids, "c_ids"), (rest, "c_rest"), (valid, "c_valid"), (small, "c_small")],
            "f0": [(b1, "b1_0"), (w2, "w2_0"), (b2, "b2_0"), (gate_w, "gate_w"), (gate_b, "gate_b")],
            "a0": [(wv[0], "wv_0"), (bv[0], "bv_0"), (wp[0], "wp_0"), (bp[0], "bp_0"),
                   (wv[1], "wv_1"), (bv[1], "bv_1"), (wp[1], "wp_1"), (bp[1], "bp_1")],
            "f1": [(v2, "w2_1"), (c2, "b2_1"), (router_w, "router_w"), (router_b, "router_b")],
        }
        s_set = sem("setup_dve")
        s_constp = sem("const_pool")
        s_consta = sem("const_act")
        s_constd = sem("const_dve")
        s_w1h = sem("w1_high")
        s_w1l = sem("w1_low")
        s_addx = sem("addx_ready")
        s_c1h = sem("c1_high")
        s_c1 = sem("c1_ready")
        s_stage_h = sem("stage_high")
        s_stage_l = sem("stage_low")
        s_out = sem("stored")
        s_zero = sem("zero_ready")

        NAMES = {
            "F0": "ln dln rstd xn tr xt xh xl lgt dch dlg ex cw cwc cwt cwts yb up sg h dn acc",
            "S": "wsc wh wl asc ah al pads",
            "A": "ln dln rstd xn tr xt xh xl qk hi qk16 v vs s mt mx mn qm st pf pl vl pv at atT atS pj acc rec",
            "F1": "ln dln rstd xn tr xt lgt dch oh cnt ntT incl sl offs ohT eidp eid scat idld unused idf xld0 xld1 trx xh xl ohu ohd up sg h trh hT dn y idt put0 put1 back acc",
        }
        by_kind = {kind: {s: sem(f"{kind}_{s}") for s in NAMES["A" if kind[0] == "A" else kind].split()}
                   for kind in sorted(set(phases))}
        attn = [n for n, kind in enumerate(phases) if kind[0] == "A"]
        ready_in = {max(n - 1, 0): n for n in attn}
        setup = {s: sem(f"A_{s}") for s in NAMES["S"].split()}
        ph = [by_kind[kind] for kind in phases]
        nth = [phases[:n].count(kind) for n, kind in enumerate(phases)]
        NTP = ((NS + 1) // 2, NS // 2)
        order = [4, 5, 6, 7, 2, 3, 0, 1]
        split_in, done = {}, 0
        for n, kind in enumerate(phases):
            upto = {("F0", 0): 4, ("F0", 1): 6, ("F1", 0): E}.get((kind, nth[n]), done) if "F1" in phases else 0
            split_in[n] = list(enumerate(order))[done:upto]
            done = max(done, upto)

        def in_loop(n):
            return n == 0 and len(split_in[n]) == 4

        DLG = 2
        NPV = {"A0": 8, "A1": 8}

        def x_ready(eng, n):
            if n == 0:
                eng.wait_ge(ld["x"], 16)
            else:
                eng.wait_ge(ph[n - 1]["acc"], (nth[n - 1] + 1) * {
                    "F0": NT // CH * (1 + E0 * CH), "A0": NB, "A1": NB, "F1": 4}[phases[n - 1]])

        def slot_tiles(eng, tasks):
            def step(t, r, steady):
                for task, ahead in tasks:
                    p = (t + ahead) % 2
                    turn = (t + ahead - p) // 2
                    if steady:
                        task((r + turn) * 2 + p, p, r + turn, False)
                    elif 0 <= t + ahead < NS:
                        task(t + ahead, p, turn, turn == 0)

            lo, hi = 4, (NS - 3) // 2 * 2
            for t in range(-3, lo):
                step(t, 0, False)
            with eng.Fori(lo // 2, hi // 2) as r:
                step(0, r, True)
                step(1, r, True)
            for t in range(hi, NS + 3):
                step(t, 0, False)

        def sequences(eng, step):
            def at(t):
                return lambda ahead: (t + ahead, (t + ahead) % 2) if 0 <= t + ahead < NB else None

            lo, pairs = 1, (NB - 4) // 2
            for t in range(-3, lo):
                step(at(t))
            with eng.Fori(0, pairs) as r:
                for u in range(2):
                    step(lambda ahead, u=u: (r * 2 + (lo + u + ahead), (lo + u + ahead) % 2))
            for t in range(lo + 2 * pairs, NB + 1):
                step(at(t))

        block = ctx.enter_context(nc.Block())

        @block.sync
        def _(sp):
            sp.dma_start(X[:], d["x"]).then_inc(ld["x"], 16)
            sp.dma_start(stage[:], d["w1_0"]).then_inc(ld["w1"], 16)
            def load(*groups):
                for group in groups:
                    for dst, src in LOADS[group]:
                        sp.dma_start(dst if dst is masks else dst[:], d[src]).then_inc(ld[group], 16)

            load("const", "f0")
            sp.dma_start(c1f[0:E, :], d["b1_1"]).then_inc(ld["b1"], 16)
            sp.dma_start(c1f[E:2 * E, :], d["b1_1"]).then_inc(ld["b1"], 16)
            sp.dma_start(addxf, d["c_addx"]).then_inc(ld["addx"], 16)
            if "A0" in phases:
                sp.dma_start(wqkf, d["wqk_0"]).then_inc(ld["wqk"], 16)
                sp.dma_start(addf[0], d["add_0"]).then_inc(ld["addw"], 16)
            load("a0", "f1")
            sp.wait_ge(s_w1h, 1)
            sp.wait_ge(s_w1l, 1)
            sp.wait_ge(s_zero, 1)
            zeros = mpad[:].rearrange("p q g j s -> p (q g j s)").bitcast(F32)
            for k, lo, hi in ZEROED:
                rows = xs_dram[k].rearrange("a c -> (a c)").rearrange("(p w) -> p w", p=P)
                sp.dma_start(rows[:, lo:hi], zeros[:, 0:hi - lo]).then_inc(ld["zero"], 16)

            def load_second(n):
                for k, e in split_in[n]:
                    if k >= 2:
                        sp.wait_ge(s_stage_h, k - 1)
                        sp.wait_ge(s_stage_l, k - 1)
                    sp.dma_start(stage[:, (k % 2) * 2 * HID:(k % 2 + 1) * 2 * HID], d["w1_1"][:, e, :])\
                      .then_inc(ld[f"stage{k % 2}"], 16)

            for n, kind in enumerate(phases):
                s, m = ph[n], nth[n]
                if split_in[n]:
                    if n:
                        x_ready(sp, n)
                    load_second(n)
                if n in ready_in and phases[ready_in[n]] == "A1":
                    x_ready(sp, n)
                    if "F1" in phases[:n + 1]:
                        sp.wait_ge(s_stage_l, E)
                    sp.dma_start(wqkf, d["wqk_1"]).then_inc(ld["wqk"], 16)
                    sp.dma_start(addf[1], d["add_1"]).then_inc(ld["addw"], 16)
                if kind == "F1":
                    def load(i, par, k, first):
                        if not first:
                            sp.wait_ge(s["trx"], NS * m + i - 1)
                        sp.dma_start(xg[:, par, :], xs_dram[m][bass.ds(i * P, P), 0:P]).then_inc(s[f"xld{par}"], 16)

                    sp.wait_ge(s["scat"], 16 * NT * (m + 1))
                    slot_tiles(sp, [(load, 3)])
                    for par in range(2):
                        sp.wait_ge(s[f"put{par}"], 16 * NTP[par] * (m + 1))
                    sp.dma_start(xn[:, :, 0:P], yt_dram[1:1 + NT * P, :].rearrange("(p t) c -> p t c", p=P))\
                      .then_inc(s["back"], 16)
            for group in ("a0", "f1"):
                sp.wait_ge(ld[group], 16 * len(LOADS[group]))
            sp.wait_ge(ld["f0"], 16 * len(LOADS["f0"]))
            sp.wait_ge(ld["addx"], 16)
            sp.wait_ge(ld["zero"], 16 * len(ZEROED))
            if "A0" in phases:
                sp.wait_ge(ld["wqk"], 16)
                sp.wait_ge(ld["addw"], 16)
            x_ready(sp, len(phases))
            sp.dma_start(out, X[:]).then_inc(s_out, 16)
            sp.wait_ge(s_out, 16)

        @block.gpsimd
        def _(pool):
            pool.memset(halfpow[:], -0.5).then_inc(s_constp, 1)
            pool.wait_ge(s_constp, 1)

            def low_w1():
                pool.wait_ge(s_w1h, 1)
                pool.tensor_tensor(w1l[:].rearrange("p e f -> p (e f)"), stage[:],
                                   w1h[:].rearrange("p e f -> p (e f)").bitcast(F32), ALU.subtract).then_inc(s_w1l, 1)

            if phases[0] != "F0":
                low_w1()

            def rstd_of(s, i, cols_):
                pool.wait_ge(s["ln"], i + 1)
                pool.tensor_tensor(rstd[:, cols_], ve[:, cols_], halfpow[:, cols_], ALU.pow).then_inc(s["rstd"], 1)

            def split_second(k, e, par):
                pool.wait_ge(s_stage_h, k + 1)
                pool.tensor_tensor(tile_of(v1l, e), stage[:, par * 2 * HID:(par + 1) * 2 * HID],
                                   tile_of(v1h, e).bitcast(F32), ALU.subtract).then_inc(s_stage_l, 1)

            for n, kind in enumerate(phases):
                s, m = ph[n], nth[n]
                if kind == "F0":
                    for c in range(4):
                        rstd_of(s, 4 * m + c, slice(c * CH, (c + 1) * CH))
                    if n == 0:
                        low_w1()
                    if in_loop(n):
                        with pool.Fori(0, 2) as r:
                            for u in range(2):
                                split_second(r * 2 + u, r * 2 + (4 + u), u)
                    else:
                        for k, e in split_in[n]:
                            split_second(k, e, k % 2)
                elif kind[0] == "A":
                    NR = len(ROUNDS["causal" if kind == "A0" else "window"])

                    def step(item):
                        now, far = item(0), item(3)
                        for r in range(NR):
                            if r == NR // 2 and far:
                                rstd_of(s, far[0], slice(0, 2))
                            if now:
                                i, par = now
                                pool.wait_ge(s["pf"], i * NR + (r + 1))
                                at_r = (NR * par + r) % 8
                                pool.tensor_tensor(prob16[1][:, at_r, :, :], prob[:, r % 2, :, :],
                                                   prob16[0][:, at_r, :, :], ALU.subtract).then_inc(s["pl"], 1)

                    sequences(pool, step)
                else:
                    for c in range(4):
                        rstd_of(s, 4 * m + c, slice(c * CH, (c + 1) * CH))
                    for k, e in split_in[n]:
                        split_second(k, e, k % 2)
                    pool.wait_ge(s["sl"], m + 1)
                    pool.wait_ge(s["xn"], NT * (m + 1))
                    pool.wait_ge(s["idt"], (NS + 1) * m + 1)
                    pool.wait_ge(ld["zero"], 16 * len(ZEROED))
                    for t in range(NT):
                        pool.indirect_dma_start(
                            out=xs_dram[m], out_offset=bass.IndirectOffsetOnAxis(ap=slot[:, t:t + 1], axis=0),
                            in_=xn[:, t, :], in_offset=None).then_inc(s["scat"], 16)

                    def onehot_up(i, par, k, first):
                        if not first:
                            pool.wait_ge(s["up"], NS * m + i - 1)
                        pool.tensor_copy(oh_up[:, par, :],
                                         ohT[:, bass.ds(i, 1)].broadcast_to([2 * E, P])).then_inc(s["ohu"], 1)

                    def onehot_down(i, par, k, first):
                        if not first:
                            pool.wait_ge(s["dn"], NS * m + i - 1)
                        pool.tensor_copy(oh_down[:, par, :],
                                         ohT[0:E, bass.ds(i, 1)].broadcast_to([E, P])).then_inc(s["ohd"], 1)

                    pool.wait_ge(s["ohT"], m + 1)
                    def small(at):
                        pool.tensor_tensor(spare_pool[:, at:at + 1], halfpow[:, 0:1], halfpow[:, 0:1], ALU.add)

                    def put(i, par, k, first):
                        if not first:
                            pool.wait_ge(s[f"put{par}"], (NTP[par] * m + k) * 16)
                        elif par == 0:
                            pool.wait_ge(s["idf"], m + 1)
                        if not first:
                            small(0)
                        pool.tensor_copy(idt[:, par:par + 1], idu[:, bass.ds(i, 1)]).then_inc(s["idt"], 1)
                        pool.wait_ge(s["idt"], (NS + 1) * m + i + 2)
                        pool.wait_ge(s["y"], NS * m + i + 1)
                        small(1)
                        pool.indirect_dma_start(
                            out=yt_dram, out_offset=bass.IndirectOffsetOnAxis(ap=idt[:, par:par + 1], axis=0),
                            in_=ysb[:, par, :], in_offset=None).then_inc(s[f"put{par}"], 16)

                    slot_tiles(pool, [(onehot_up, 2), (onehot_down, 0), (put, -1)])

        @block.scalar
        def _(act):
            act.wait_ge(ld["w1"], 16)
            act.activation(w1h[:].rearrange("p e f -> p (e f)"), stage[:], ACT.Copy).then_inc(s_w1h, 1)
            act.wait_ge(ld["const"], 16 * len(LOADS["const"]))
            act.activation(identb[:], ident[:], ACT.Copy).then_inc(s_consta, 1)
            act.activation(ident16[:], ident[:], ACT.Copy).then_inc(s_consta, 1)
            act.activation(masksb[:], masks, ACT.Copy).then_inc(s_consta, 1)
            act.activation(trib[:], tri[:], ACT.Copy).then_inc(s_consta, 1)

            def late_setup():
                act.wait_ge(ld["b1"], 32)
                act.activation(c1hl[:], c1f, ACT.Copy).then_inc(s_c1h, 1)
                act.wait_ge(ld["addx"], 16)
                act.activation(addx[:], addxf, ACT.Copy).then_inc(s_addx, 1)

            if phases[0] != "F0":
                late_setup()

            def attention_weights(n):
                a = int(phases[n][1])
                act.wait_ge(setup["wsc"], attn.index(n) + 1)
                act.activation(wqkh[:], wqkf, ACT.Copy).then_inc(setup["wh"], 1)
                act.wait_ge(setup["asc"], attn.index(n) + 1)
                act.activation(addw[:], addf[a], ACT.Copy).then_inc(setup["ah"], 1)

            def split_second(k2, e, par):
                act.wait_ge(ld[f"stage{par}"], k2 * 16 + 16)
                act.activation(tile_of(v1h, e), stage[:, par * 2 * HID:(par + 1) * 2 * HID],
                               ACT.Copy).then_inc(s_stage_h, 1)

            for n, kind in enumerate(phases):
                s, m = ph[n], nth[n]
                if kind == "F0":
                    act.wait_ge(ld["f0"], 16 * len(LOADS["f0"]))
                    for c in range(4):
                        C = 4 * m + c
                        act.wait_ge(s["tr"], C + 1)
                        if c >= 2:
                            act.wait_ge(s["lgt"], C - 1)
                        act.activation(xT2[c % 2], PS[:, c % 2, :], ACT.Copy).then_inc(s["xt"], 1)
                        act.activation(xTh4[:, c, :], PS[:, c % 2, :], ACT.Copy).then_inc(s["xh"], 1)
                    if n:
                        for k, e in split_in[n]:
                            split_second(k // 2, e, k % 2)
                    else:
                        late_setup()
                    if n in ready_in:
                        attention_weights(ready_in[n])
                    act.wait_ge(s["dlg"], m + 1)
                    act.activation(r8[1][:], r8[0][:], ACT.Exp).then_inc(s["ex"], 1)
                    with act.Fori(2 * m, 2 * (m + 1)) as r:
                        for k in range(2 * E0):
                            j, e = divmod(k, E0)
                            act.wait_ge(s["up"], r * (2 * E0) + (k + 1))
                            if k >= 2:
                                act.wait_ge(s["h"], r * (2 * E0) + (k - 1))
                            act.activation(act_s[:, k % 2, :], PS[:, 2 + 2 * (k % 2), :], ACT.Silu,
                                           bias=b1[:, e, 0:1]).then_inc(s["sg"], 1)
                            if e == 4 and in_loop(n):
                                split_second(r, r * 2 + (4 + j), j)
                            if e == 1:
                                act.wait_ge(s["cwt"], r * 2 + (j + 1))
                                act.activation(cwT[:], PS[0:E0, 0, :], ACT.Copy).then_inc(s["cwts"], 1)
                elif kind[0] == "A":
                    causal = kind == "A0"
                    rounds = ROUNDS["causal" if causal else "window"]
                    NR, NV, place = len(rounds), 2 if causal else 4, PLACES[kind]
                    if sum(len(split_in[k]) for k in range(n)):
                        act.wait_ge(s_stage_l, sum(len(split_in[k]) for k in range(n)))
                    if n == 0:
                        attention_weights(n)

                    def high_qk(i, par, r):
                        act.wait_ge(s["qk"], i * 4 + (r + 1))
                        if positive(i * 4 + (r - 1)):
                            act.wait_ge(s["qk16"], i * 4 + (r - 1))
                        act.activation(hqk[:, r % 2, :, :], PS[:, 5 + r % 2, :].rearrange("p (g k) -> p g k", g=2),
                                       ACT.Copy).then_inc(s["hi"], 1)

                    def exponentials(i, par, r):
                        act.wait_ge(s["st"], i * NR + (r + 1))
                        if causal:
                            used = i * 8 + (r - 7 if r >= 8 else (r - 4) // 2 - 1 if r >= 4 else r // 2 - 3)
                        else:
                            used = i * 8 + (r - 7)
                        if positive(used):
                            act.wait_ge(s["pv"], used)
                        sc = PS[:, 2 + r % 2, :].rearrange("p (g k) -> p g k", g=G)
                        act.activation(prob16[0][:, (NR * par + r) % 8, :, :], sc, ACT.Exp)
                        if positive(i * NR + (r - 1)):
                            act.wait_ge(s["pl"], i * NR + (r - 1))
                        act.activation(prob[:, r % 2, :, :], sc, ACT.Exp).then_inc(s["pf"], 1)

                    def step(item):
                        prev, now, nxt, nn = (item(ahead) for ahead in (-1, 0, 1, 2))
                        for r in range(2):
                            if nxt:
                                high_qk(*nxt, 2 + r)
                            if now:
                                exponentials(*now, 2 + r)
                        if nxt:
                            i, par = nxt
                            act.wait_ge(s["v"], i + 1)
                            if positive(i - 1):
                                act.wait_ge(s["pv"], (i - 1) * NPV[kind])
                            act.activation(vaug[par][:, 0, 0:NV, :, 0:HD],
                                           PS[:, 5, 0:NV * P].rearrange("p (t h x) -> p t h x", t=NV, h=H),
                                           ACT.Copy).then_inc(s["vs"], 1)
                        if prev:
                            act.wait_ge(s["atT"], prev[0] + 1)
                            if nn:
                                act.wait_ge(s["tr"], nn[0] + 1)
                            act.activation(attT[:], PS[:, 4, 0:2 * P].rearrange("p (t c) -> p t c", t=2),
                                           ACT.Copy).then_inc(s["atS"], 1)
                        if nn:
                            i, _ = nn
                            act.wait_ge(s["tr"], i + 1)
                            if positive(i):
                                act.wait_ge(s["v"], i)
                            act.activation(xTp[:, PAD:PAD + SEQ], PS[:, 4, SEQ:2 * SEQ], ACT.Copy).then_inc(s["xt"], 1)
                            act.wait_ge(s["xt"], i + 1)
                            act.activation(xTh[:, 0:SEQ], xTp[:, PAD:PAD + SEQ], ACT.Copy).then_inc(s["xh"], 1)
                        for r in range(LEAD, NR):
                            if now:
                                exponentials(*now, r)
                            if nn and r in place["high"]:
                                high_qk(*nn, place["high"].index(r))
                        if nxt:
                            exponentials(*nxt, 0)
                            exponentials(*nxt, 1)

                    sequences(act, step)
                else:
                    for c in range(4):
                        act.wait_ge(s["tr"], 4 * m + c + 1)
                        if c >= 2:
                            act.wait_ge(s["lgt"], 4 * m + c - 1)
                        act.activation(xT2[c % 2], PS[:, c % 2, :], ACT.Copy).then_inc(s["xt"], 1)
                    for k, e in split_in[n]:
                        split_second(k // 2, e, k % 2)
                    if n in ready_in and n + 1 < len(phases):
                        attention_weights(ready_in[n])

                    act.wait_ge(s["scat"], 16 * NT * (m + 1))
                    act.dma_start(idf[:], xs_dram[m][:, P:P + 1].rearrange("(i p) c -> p (i c)", p=P),
                                  allow_slow_non_contiguous=True)\
                       .then_inc(s["idld"], 16)

                    def high(i, par, k, first):
                        act.wait_ge(s["trx"], NS * m + i + 1)
                        if not first:
                            act.wait_ge(s["up"], NS * m + i - 1)
                        act.activation(xgh[:, par, :], PS[:, par, 0:P], ACT.Copy).then_inc(s["xh"], 1)

                    def gate(i, par, k, first):
                        act.wait_ge(s["up"], NS * m + i + 1)
                        if not first:
                            act.wait_ge(s["h"], NS * m + i - 1)
                        act.activation(act_s[:, par, :], PS[:, 4 + par, :], ACT.Sigmoid).then_inc(s["sg"], 1)

                    def turned(i, par, k, first):
                        act.wait_ge(s["trh"], NS * m + i + 1)
                        if not first:
                            act.wait_ge(s["dn"], NS * m + i - 1)
                        act.activation(hT[:, par, :], PS[:, 6, :], ACT.Copy).then_inc(s["hT"], 1)

                    slot_tiles(act, [(gate, 1), (turned, 0), (high, 2)])

        @block.vector
        def _(dve):
            ch = Chain(dve, s_set)
            dve.memset(mpad[:], 0.0).then_inc(s_zero, 1)
            for tile_, value in ((onesb, 1.0), (ones1, 1.0), (xTp, 0.0), (cw, 0.5),
                                 (zero8, 0.0)):
                ch.step(dve.memset(tile_[:], value))

            def late_setup():
                dve.wait_ge(s_c1h, 1)
                dve.scalar_tensor_tensor(out=c1hl[:], in0=c1hl[:].bitcast(F32), scalar=neg_lo16, in1=c1f,
                                         op0=ALU.mult, op1=ALU.add).then_inc(s_c1, 1)

            def attention_weights(n):
                a = int(phases[n][1])
                dve.wait_ge(ld["wqk"], 16 * (attn.index(n) + 1))
                dve.wait_ge(ld["addw"], 16 * (attn.index(n) + 1))
                dve.tensor_scalar(wqkf[:, 0, :], wqkf[:, 0, :], HD ** -0.5, None, ALU.mult).then_inc(setup["wsc"], 1)
                dve.tensor_scalar(addf[a][0:2, 0, :], addf[a][0:2, 0, :], HD ** -0.5, None, ALU.mult)\
                   .then_inc(setup["asc"], 1)
                dve.wait_ge(setup["wh"], attn.index(n) + 1)
                dve.tensor_tensor(wqkl[:], wqkf, wqkh[:].bitcast(F32), ALU.subtract).then_inc(setup["wl"], 1)
                dve.wait_ge(setup["ah"], attn.index(n) + 1)
                dve.scalar_tensor_tensor(out=addw[:], in0=addw[:].bitcast(F32), scalar=cols[:, 3:4], in1=addf[a],
                                         op0=ALU.mult, op1=ALU.add).then_inc(setup["al"], 1)

            if phases[0] != "F0":
                dve.wait_ge(ld["const"], 16 * len(LOADS["const"]))
                late_setup()

            def layer_norm(s, m, between=None):
                ln = Chain(dve, s["dln"], 2 * NT * m)
                for c in range(5):
                    if c < 4:
                        tiles = range(c * CH, (c + 1) * CH)
                        for t in tiles:
                            ln.step(dve.bn_stats(stats[:, t, :], X[:, t, :]))
                        ln.wait()
                        for t in tiles:
                            ln.step(dve.bn_aggr(mv[:, t, :], stats[:, t, :]))
                        ln.wait()
                        dve.tensor_scalar(ve[:, c * CH:(c + 1) * CH], mv[:, c * CH:(c + 1) * CH, 1], EPS, None, ALU.add)\
                           .then_inc(s["ln"], 1)
                    if c >= 3 and between:
                        between(c - 3)
                    if c >= 1:
                        dve.wait_ge(s["rstd"], 4 * m + c)
                        for t in range((c - 1) * CH, c * CH):
                            dve.tensor_scalar(xn[:, t, 0:P], X[:, t, :], mv[:, t, 0:1], rstd[:, t:t + 1],
                                              ALU.subtract, ALU.mult).then_inc(s["xn"], 1)

            def first_of_max(c, values, nt, eq, top, first, onehot_out):
                c.link(dve.tensor_reduce(top[:, 0:nt], values, AX.X, ALU.max))
                c.link(dve.tensor_tensor(eq[:, 0:nt, :], values, top[:, 0:nt].unsqueeze(2).broadcast_to([P, nt, E]),
                                         ALU.is_equal))
                c.link(dve.tensor_tensor(eq[:, 0:nt, :], eq[:, 0:nt, :], em8[:, 0:nt, :], ALU.mult))
                c.link(dve.tensor_reduce(first[:, 0:nt], eq[:, 0:nt, :], AX.X, ALU.min))
                c.link(dve.tensor_tensor(onehot_out, em8[:, 0:nt, :],
                                         first[:, 0:nt].unsqueeze(2).broadcast_to([P, nt, E]), ALU.is_equal))

            for n, kind in enumerate(phases):
                s, m = ph[n], nth[n]
                x_ready(dve, n)
                if kind == "F0":
                    def low_rows(c):
                        dve.wait_ge(s["xh"], 4 * m + c + 1)
                        dve.tensor_tensor(xTl4[:, c, :], PS[:, c % 2, :], xTh4[:, c, :].bitcast(F32),
                                          ALU.subtract).then_inc(s["xl"], 1)

                    layer_norm(s, m, low_rows)
                    low_rows(2)
                    low_rows(3)
                    if n == 0:
                        dve.wait_ge(ld["const"], 16 * len(LOADS["const"]))
                        late_setup()
                    if n in ready_in:
                        attention_weights(ready_in[n])
                    dve.wait_ge(ld["f0"], 16 * len(LOADS["f0"]))
                    c_ = Chain(dve, s["dch"], m * 17)
                    dve.wait_ge(s["lgt"], 4 * (m + 1))
                    lg = r8[1][:]
                    c_.link(dve.tensor_tensor(lg, PS[:, 7, 0:NT * E].rearrange("p (t e) -> p t e", e=E),
                                              gate_b[:].unsqueeze(1).broadcast_to([P, NT, E]), ALU.add))
                    bc = lambda x: x[:].unsqueeze(2).broadcast_to([P, NT, E])
                    c_.link(dve.tensor_reduce(r1[0][:], lg, AX.X, ALU.max))
                    dve.tensor_tensor(r8[0][:], lg, bc(r1[0]), ALU.subtract).then_inc(s["dlg"], 1)
                    dve.wait_ge(s["ex"], m + 1)
                    pr = r8[1][:]
                    c_.link(dve.tensor_reduce(r1[0][:], pr, AX.X, ALU.add))
                    c_.link(dve.reciprocal(r1[1][:], r1[0][:]))
                    c_.link(dve.tensor_tensor(pr, pr, bc(r1[1]), ALU.mult))
                    o1, o2, eq = r8[2][:], r8[3][:], r8[0]
                    first_of_max(c_, pr, NT, eq, r1[0], r1[1], o1)
                    c_.link(dve.scalar_tensor_tensor(out=o2, in0=o1, scalar=-2.0, in1=pr, op0=ALU.mult, op1=ALU.add))
                    first_of_max(c_, o2, NT, eq, r1[0], r1[1], o2)
                    c_.link(dve.tensor_tensor(o1, o1, o2, ALU.add))
                    dve.scalar_tensor_tensor(out=cw[:, :, 0:E], in0=pr, scalar=0.5, in1=o1, op0=ALU.mult,
                                             op1=ALU.mult).then_inc(s["cw"], 1)
                    assert c_.n == 17, c_.n
                    with dve.Fori(2 * m, 2 * (m + 1)) as r:
                        def accumulate(k):
                            j, e = divmod(k, E0)
                            dve.wait_ge(s["dn"], r * (2 * E0) + (k + 1))
                            for t in range(CH):
                                if e:
                                    before = added(j, e - 1) + (0 if e == 1 else t + 1 - CH)
                                    dve.wait_ge(s["acc"], r * (2 * PER) + before)
                                tile = (r - 2 * m) * (2 * CH) + (j * CH + t)
                                xs = tile_of(X, tile)
                                dve.scalar_tensor_tensor(out=xs, in0=PS[:, 6 + k % 2, t * P:(t + 1) * P],
                                                         scalar=cw[:, bass.ds(tile, 1), e], in1=xs,
                                                         op0=ALU.mult, op1=ALU.add).then_inc(s["acc"], 1)

                        def add_biases(j):
                            dve.wait_ge(s["yb"], r * 2 + (j + 1))
                            dve.wait_ge(s["acc"], r * (2 * PER) + (j * PER + CH))
                            xs = X[:, bass.ds((r - 2 * m) * (2 * CH) + j * CH, CH), :]
                            dve.tensor_tensor(xs, PS[:, 1, :].rearrange("p (t k) -> p t k", t=CH), xs,
                                              ALU.add).then_inc(s["acc"], 1)

                        for k in range(2 * E0):
                            j, e = divmod(k, E0)
                            dve.wait_ge(s["sg"], r * (2 * E0) + (k + 1))
                            if k >= 2:
                                dve.wait_ge(s["dn"], r * (2 * E0) + (k - 1))
                            dve.scalar_tensor_tensor(out=hid[:, k % 2, :], in0=PS[:, 3 + 2 * (k % 2), :],
                                                     scalar=b1[:, e, 1:2], in1=act_s[:, k % 2, :], op0=ALU.add,
                                                     op1=ALU.mult).then_inc(s["h"], 1)
                            if e == 0:
                                dve.wait_ge(s["cw"], m + 1)
                                dve.tensor_copy(cw_chunk[:], cw[:, bass.ds((r - 2 * m) * (2 * CH) + j * CH, CH), :])\
                                   .then_inc(s["cwc"], 1)
                            if k >= 1:
                                accumulate(k - 1)
                            if e == 1:
                                add_biases(j)
                        accumulate(2 * E0 - 1)
                elif kind[0] == "A":
                    causal = kind == "A0"
                    rounds = ROUNDS["causal" if causal else "window"]
                    NR, NV, place = len(rounds), 2 if causal else 4, PLACES[kind]
                    dve.wait_ge(ld["a0"], 16 * len(LOADS["a0"]))
                    dve.wait_ge(ld["zero"], 16 * len(ZEROED))
                    if n == 0:
                        attention_weights(n)
                    dve.wait_ge(s_set, 5)
                    w = Chain(dve, setup["pads"], 12 * attn.index(n))
                    buffers = range(2) if attn.index(n) == 0 else range(1, 2)
                    for par in buffers:
                        for half in range(2):
                            w.step(dve.memset(vaug[par][:, half, :, :, HD:HD + 1], 1.0 - half))
                        for lo in (0, SEQ + PAD):
                            w.step(dve.memset(k16[par][:, :, lo:lo + PAD], 0.0))
                    w.wait()
                    for par in buffers:
                        for lo in (0, SEQ + PAD):
                            kp = k16[par][:, :, lo:lo + PAD]
                            w.step(dve.tensor_scalar(kp, kp, m_one, None, ALU.add))

                    def statistics(i):
                        ln = Chain(dve, s["dln"], i * 4)
                        for t in range(2):
                            ln.step(dve.bn_stats(stats[:, t, :], tile_of(X, i * 2 + t)))
                        ln.wait()
                        if positive(i):
                            dve.wait_ge(s["xn"], i * 2)
                        dve.memset(spare[:], 0.0)
                        for t in range(2):
                            ln.step(dve.bn_aggr(mv[:, t, :], stats[:, t, :]))
                        ln.wait()
                        dve.tensor_scalar(ve[:, 0:2], mv[:, 0:2, 1], EPS, None, ALU.add).then_inc(s["ln"], 1)

                    def normalised(i, par):
                        dve.wait_ge(s["rstd"], i + 1)
                        if positive(i - 1):
                            dve.wait_ge(s["tr"], i - 1)
                        for t in range(2):
                            dve.tensor_scalar(xn[:, 2 * par + t, 0:P], tile_of(X, i * 2 + t), mv[:, t, 0:1],
                                              rstd[:, t:t + 1], ALU.subtract, ALU.mult).then_inc(s["xn"], 1)

                    def blend(i, par, r):
                        side, half = r // 2, r % 2
                        dve.wait_ge(s["hi"], i * 4 + (r + 1))
                        if positive(i - 1):
                            dve.wait_ge(s["st"], (i - 1) * NR)
                        gs = slice(2 * half, 2 * half + 2)
                        dst = q16[:, par, gs, :] if side == 0 else k16[par][:, gs, PAD:PAD + SEQ]
                        dve.scalar_tensor_tensor(out=dst, in0=hqk[:, half, :, :], scalar=neg_lo[side],
                                                 in1=PS[:, 5 + half, :].rearrange("p (g k) -> p g k", g=2),
                                                 op0=ALU.mult, op1=ALU.add).then_inc(s["qk16"], 1)

                    def maxima(i, par, r):
                        qt, kb, c = rounds[r]
                        dve.wait_ge(s["s"], i * NR + (r + 1))
                        dst = mtmp[:, kb, :, c] if causal and qt == 1 else mpad[:, qt, :, c, M_SLOT]
                        dve.tensor_reduce(dst, PS[:, r % 2, :].rearrange("p (g k) -> p g k", g=G), AX.X, ALU.max,
                                          negate=True).then_inc(s["mx"], 1)

                    def with_maxima(i, par, qt):
                        dve.wait_ge(s["mt"], i * 2 + (qt + 1))
                        q = q16[:, par, :, qt * P:(qt + 1) * P]
                        dve.tensor_tensor(q, PS[:, 4, :].rearrange("p (g k) -> p g k", g=G), q, ALU.add)\
                           .then_inc(s["qm"], 1)

                    def step(item):
                        prev, now, nxt, nn, far = (item(ahead) for ahead in (-1, 0, 1, 2, 3))
                        if prev:
                            i, _ = prev
                            pv = PS[:, 7, 0:2 * H * (HD + 1)].rearrange("p (t h x) -> p t h x", t=2, h=H)
                            dve.wait_ge(s["pv"], (i + 1) * NPV[kind])
                            dve.reciprocal(rec[:], pv[:, :, :, HD]).then_inc(s["rec"], 1)
                            dve.wait_ge(s["rec"], i + 1)
                            dve.tensor_tensor(att[:].rearrange("p t (h x) -> p t h x", h=H), pv[:, :, :, 0:HD],
                                              rec[:].unsqueeze(3).broadcast_to([P, 2, H, HD]), ALU.mult)\
                               .then_inc(s["at"], 1)
                        if nn:
                            normalised(*nn)
                        if nxt:
                            blend(*nxt, 2)
                            blend(*nxt, 3)
                        for r in range(NR):
                            if nxt:
                                maxima(*nxt, r)
                            if r == 2 and far:
                                statistics(far[0])
                            if r == 1 and nxt:
                                i, par = nxt
                                dve.wait_ge(s["vs"], i + 1)
                                dve.tensor_tensor(vaug[par][:, 1, 0:NV, :, 0:HD],
                                                  PS[:, 5, 0:NV * P].rearrange("p (t h x) -> p t h x", t=NV, h=H),
                                                  vaug[par][:, 0, 0:NV, :, 0:HD], ALU.subtract).then_inc(s["vl"], 1)
                            if r == place["low"] and nn:
                                i, _ = nn
                                dve.wait_ge(s["xh"], i + 1)
                                dve.tensor_tensor(xTl[:, 0:SEQ], xTp[:, PAD:PAD + SEQ], xTh[:, 0:SEQ].bitcast(F32),
                                                  ALU.subtract).then_inc(s["xl"], 1)
                            if r == place["add"] and prev:
                                i, _ = prev
                                dve.wait_ge(s["pj"], i + 1)
                                xs = X[:, bass.ds(i * 2, 2), :]
                                dve.tensor_tensor(xs, PS[:, 6, 0:2 * P].rearrange("p (t c) -> p t c", t=2), xs,
                                                  ALU.add).then_inc(s["acc"], 1)
                            if r == place["join"] and nxt:
                                with_maxima(*nxt, 0)
                        if nxt and causal:
                            i, _ = nxt
                            dve.wait_ge(s["mx"], (i + 1) * NR)
                            dve.tensor_tensor(mpad[:, 1, :, :, M_SLOT], mtmp[:, 0, :, :], mtmp[:, 1, :, :],
                                              ALU.min).then_inc(s["mn"], 1)
                        if nn:
                            blend(*nn, 0)
                        if nxt:
                            with_maxima(*nxt, 1)
                        if nn:
                            blend(*nn, 1)

                    sequences(dve, step)
                else:
                    dve.wait_ge(ld["f1"], 16 * len(LOADS["f1"]))
                    dve.tensor_copy(xn[:, :, P], ids[:]).then_inc(s["idt"], 1)
                    layer_norm(s, m)
                    dve.wait_ge(s["lgt"], 4 * (m + 1))
                    c_ = Chain(dve, s["dch"], 20 * m)
                    lg = r8[2][:]
                    c_.link(dve.tensor_tensor(lg, PS[:, 6, 0:NT * E].rearrange("p (t e) -> p t e", e=E),
                                              router_b[:].unsqueeze(1).broadcast_to([P, NT, E]), ALU.add))
                    first_of_max(c_, lg, NT, r8[0], r1[0], r1[1], onehot[:])
                    for twice in range(2):
                        c_.step(dve.tensor_reduce(r8[1][:, twice, :], onehot[:].rearrange("p t e -> p e t"), AX.X, ALU.add))
                    c_.wait()
                    dve.tensor_copy(ohsum[:], r8[1][:, 0:2, :]).then_inc(s["oh"], 1)
                    dve.wait_ge(s["cnt"], m + 1)
                    c_.link(dve.tensor_tensor(gtk[:], PS[:, 2, 0:E].unsqueeze(2).broadcast_to([P, E, NT]), k128[:],
                                              ALU.is_gt))
                    c_.link(dve.tensor_reduce(ntl[:, 0, :], gtk[:], AX.X, ALU.add))
                    c_.link(dve.tensor_tensor_scan(ntl[:, 1, :], ntl[:, 0, :], zero8[:], 0.0, ALU.add, ALU.add))
                    c_.link(dve.tensor_tensor(ntl[:, 2, :], ntl[:, 1, :], ntl[:, 0, :], ALU.subtract))
                    c_.link(dve.scalar_tensor_tensor(out=r8[0][:], in0=ntl[:, 2, :].unsqueeze(1).broadcast_to([P, NT, E]),
                                                     scalar=float(P), in1=PS[:, 3, 0:NT * E].rearrange("p (t e) -> p t e", e=E),
                                                     op0=ALU.mult, op1=ALU.add))
                    c_.link(dve.tensor_tensor(r8[0][:], r8[0][:], onehot[:], ALU.mult))
                    c_.link(dve.tensor_reduce(slotf[:], r8[0][:], AX.X, ALU.add))
                    dve.tensor_copy(slot[:], slotf[:]).then_inc(s["sl"], 1)
                    c_.link(dve.tensor_copy(offT[:, 0:1], PS[0:2 * E, 4, 0:1]))
                    c_.link(dve.tensor_scalar(gtT[:], k128T, offT[:, 0:1], None, ALU.is_lt))
                    dve.tensor_reduce(ntT[:], gtT[:], AX.X, ALU.add).then_inc(s["ntT"], 1)
                    dve.wait_ge(s["incl"], m + 1)
                    c_.link(dve.tensor_copy(offT[:], PS[0:2 * E, 4, 0:2]))
                    for k in range(2):
                        c_.step(dve.tensor_scalar(cmpT[:, k, :], iota_s, offT[:, k:k + 1], None, ALU.is_lt))
                    c_.wait()
                    dve.tensor_tensor(ohT[:], cmpT[:, 0, :], cmpT[:, 1, :], ALU.subtract).then_inc(s["ohT"], 1)
                    assert c_.n == 20, c_.n
                    dve.wait_ge(s["eidp"], m + 1)
                    dve.tensor_copy(eid[:], PS[0:1, 4, 0:NS]).then_inc(s["eid"], 1)
                    if n in ready_in and n + 1 < len(phases):
                        attention_weights(ready_in[n])

                    def addresses():
                        dve.wait_ge(s["idld"], 16 * (m + 1))
                        c_ = Chain(dve, s["unused"], 2 * m)
                        c_.link(dve.tensor_scalar(unused[:], idf[:], 0.0, None, ALU.is_equal))
                        c_.link(dve.tensor_tensor(unused[:], unused[:], rest[:], ALU.mult))
                        dve.tensor_tensor(idu[:], unused[:], idf[:], ALU.add).then_inc(s["idf"], 1)

                    def low(i, par, k, first):
                        dve.wait_ge(s["xh"], NS * m + i + 1)
                        dve.tensor_tensor(xgl[:, par, :], PS[:, par, 0:P], xgh[:, par, :].bitcast(F32),
                                          ALU.subtract).then_inc(s["xl"], 1)

                    def hidden(i, par, k, first):
                        dve.wait_ge(s["sg"], NS * m + i + 1)
                        if not first:
                            dve.wait_ge(s["trh"], NS * m + i - 1)
                        dve.tensor_tensor(hid[:, par, :], PS[:, 2 + par, :], act_s[:, par, :], ALU.mult).then_inc(s["h"], 1)
                        if first and par == 0:
                            addresses()

                    def result(i, par, k, first):
                        dve.wait_ge(s["dn"], NS * m + i + 1)
                        if not first:
                            dve.wait_ge(s[f"put{par}"], (NTP[par] * m + k) * 16)
                        dve.tensor_copy(ysb[:, par, :], PS[:, 7, 0:P]).then_inc(s["y"], 1)

                    slot_tiles(dve, [(hidden, 1), (low, 2), (result, -1)])
                    dve.wait_ge(s["back"], 16 * (m + 1))
                    for c in range(4):
                        xs = X[:, 4 * c:4 * c + 4, :]
                        dve.scalar_tensor_tensor(out=xs, in0=xn[:, 4 * c:4 * c + 4, 0:P], scalar=0.5, in1=xs,
                                                 op0=ALU.mult, op1=ALU.add).then_inc(s["acc"], 1)

        @block.tensor
        def _(pe):
            pe.wait_ge(ld["const"], 16 * len(LOADS["const"]))
            pe.wait_ge(s_consta, 4)
            pe.wait_ge(s_set, 5)

            def mm3(out_, wh, wl, xh, xl, stop=True):
                pe.matmul(out_, wh, xh, start=True, stop=False)
                pe.matmul(out_, wl, xh, start=False, stop=False)
                return pe.matmul(out_, wh, xl, start=False, stop=stop)

            def logits(s, m, bank, weights, freed):
                for c in range(5):
                    if c < 4:
                        pe.wait_ge(s["xn"], NT * m + (c + 1) * CH)
                        if c >= 2:
                            pe.wait_ge(s[freed], 4 * m + c - 1)
                        for t in range(CH):
                            ins = pe.transpose(PS[:, c % 2, t * P:(t + 1) * P], xn[:, CH * c + t, 0:P], ident[:])
                        ins.then_inc(s["tr"], 1)
                    if c >= 1:
                        pe.wait_ge(s["xt"], 4 * m + c)
                        for t in range(CH):
                            at = (CH * (c - 1) + t) * E
                            ins = pe.matmul(PS[:, bank, at:at + E], xT2[(c - 1) % 2][:, t * P:(t + 1) * P], weights[:],
                                            start=True, stop=True)
                        ins.then_inc(s["lgt"], 1)

            for n, kind in enumerate(phases):
                s, m = ph[n], nth[n]
                if kind == "F0":
                    pe.wait_ge(ld["f0"], 16 * len(LOADS["f0"]))
                    logits(s, m, 7, gate_w, "xl")
                    pe.wait_ge(s_w1l, 1)
                    pe.wait_ge(s["xl"], 4 * (m + 1))
                    with pe.Fori(2 * m, 2 * (m + 1)) as r:
                        def up(k):
                            j, e = divmod(k, E0)
                            if k >= 2:
                                pe.wait_ge(s["h"], r * (2 * E0) + (k - 1))
                            c = (r - 2 * m) * 2 + j
                            for half in range(2):
                                w = slice(half * P, (half + 1) * P)
                                ins = mm3(PS[:, 2 + 2 * (k % 2) + half, :], w1h[:, e, w], w1l[:, e, w],
                                          tile_of(xTh4, c), tile_of(xTl4, c))
                            ins.then_inc(s["up"], 1)

                        def down(k):
                            j, e = divmod(k, E0)
                            pe.wait_ge(s["h"], r * (2 * E0) + (k + 1))
                            if k >= 2:
                                jb, eb = divmod(k - 2, E0)
                                pe.wait_ge(s["acc"], r * (2 * PER) + (added(jb, eb) - (eb == 0)))
                            for t in range(CH):
                                ins = pe.matmul(PS[:, 6 + k % 2, t * P:(t + 1) * P], hid[:, k % 2, t * P:(t + 1) * P],
                                                w2[:, e, :], start=True, stop=True)
                            ins.then_inc(s["dn"], 1)

                        def biases(j):
                            pe.wait_ge(s["cwc"], r * 2 + (j + 1))
                            for t in range(CH):
                                ins = pe.transpose(PS[0:E0, 0, t * P:(t + 1) * P], cw_chunk[:, t, :], ident[:])
                            ins.then_inc(s["cwt"], 1)
                            pe.wait_ge(s["cwts"], r * 2 + (j + 1))
                            for t in range(CH):
                                ins = pe.matmul(PS[:, 1, t * P:(t + 1) * P], cwT[:, t * P:(t + 1) * P], b2[:],
                                                start=True, stop=True)
                            ins.then_inc(s["yb"], 1)

                        up(0)
                        for k in range(2 * E0):
                            if k + 1 < 2 * E0:
                                up(k + 1)
                            if k % E0 == 1:
                                biases(k // E0)
                            down(k)
                elif kind[0] == "A":
                    a = int(kind[1])
                    causal = kind == "A0"
                    rounds = ROUNDS["causal" if causal else "window"]
                    NR, NV, place = len(rounds), 2 if causal else 4, PLACES[kind]
                    pe.wait_ge(ld["a0"], 16 * len(LOADS["a0"]))
                    pe.wait_ge(setup["wl"], attn.index(n) + 1)
                    pe.wait_ge(setup["al"], attn.index(n) + 1)
                    pe.wait_ge(s_addx, 1)
                    pe.wait_ge(setup["pads"], 12 + 6 * attn.index(n))

                    def queries_keys(i, par, r):
                        side, half = r // 2, r % 2
                        if r >= 2:
                            pe.wait_ge(s["qk16"], i * 4 + (r - 1))
                        elif r == 0:
                            pe.wait_ge(s["xl"], i + 1)
                            if positive(i):
                                pe.wait_ge(s["vl"], i)
                        elif positive(i - 2):
                            pe.wait_ge(s["acc"], i - 2)
                        for gg in range(2):
                            g = 2 * half + gg
                            w = slice(g * P, (g + 1) * P)
                            o = PS[:, 5 + half, gg * SEQ:(gg + 1) * SEQ]
                            mm3(o, wqkh[:, side, w], wqkl[:, side, w], xTh[:, 0:SEQ], xTl[:, 0:SEQ], stop=False)
                            ins = pe.matmul(o, addw[:, side, w], addx[:], start=False, stop=True)
                        ins.then_inc(s["qk"], 1)

                    def masked(bank, which):
                        pe.matmul(PS[:, bank, :].rearrange("p (g k) -> p g k", g=G), identb[:],
                                  masksb[:, which, :].unsqueeze(1).broadcast_to([P, G, P]),
                                  start=True, stop=False, skip_group_check=True)

                    def scores(i, par, r):
                        qt, kb, c = rounds[r]
                        if r == 0:
                            pe.wait_ge(s["qk16"], i * 4 + 4)
                        if positive(i * NR + (r - 1)):
                            pe.wait_ge(s["mx"], i * NR + (r - 1))
                        diagonal = not causal or qt == kb
                        if diagonal:
                            masked(r % 2, 0 if causal else 2)
                        sl = slice(SL * c, SL * (c + 1))
                        for g in range(G):
                            o = PS[:, r % 2, g * P:(g + 1) * P]
                            if causal:
                                ins = pe.matmul(o, q16[sl, par, g, qt * P:(qt + 1) * P],
                                                k16[par][sl, g, PAD + kb * P:PAD + (kb + 1) * P],
                                                start=not diagonal, stop=True, skip_group_check=True)
                            else:
                                for w in range(2):
                                    lo = (2 * qt + w) * WIN
                                    ins = pe.matmul(o[w * WIN:(w + 1) * WIN, :], q16[sl, par, g, lo:lo + WIN],
                                                    k16[par][sl, g, lo:lo + P], start=False, stop=True,
                                                    skip_group_check=True)
                        ins.then_inc(s["s"], 1)

                    def scores_turned(i, par, r):
                        qt, kb, c = rounds[r]
                        if (qt, kb, c) in ((0, 0, 0), (1, 0, 0)):
                            pe.wait_ge(s["qm"], i * 2 + (qt + 1))
                        if positive(i * NR + (r - 1)):
                            pe.wait_ge(s["pf"], i * NR + (r - 1))
                        diagonal = not causal or qt == kb
                        if diagonal:
                            masked(2 + r % 2, 1 if causal else 3)
                        sl = slice(SL * c, SL * (c + 1))
                        for g in range(G):
                            o = PS[:, 2 + r % 2, g * P:(g + 1) * P]
                            if causal:
                                ins = pe.matmul(o, k16[par][sl, g, PAD + kb * P:PAD + (kb + 1) * P],
                                                q16[sl, par, g, qt * P:(qt + 1) * P],
                                                start=not diagonal, stop=True, skip_group_check=True)
                            else:
                                for w in range(2):
                                    lo = (2 * qt + w) * WIN
                                    ins = pe.matmul(o[:, w * WIN:(w + 1) * WIN], k16[par][sl, g, lo:lo + P],
                                                    q16[sl, par, g, lo:lo + WIN], start=False, stop=True,
                                                    skip_group_check=True)
                        ins.then_inc(s["st"], 1)

                    def weighted(i, par, qt, c):
                        if (qt, c) == (0, 0):
                            pe.wait_ge(s["vl"], i + 1)
                            if positive(i):
                                pe.wait_ge(s["at"], i)
                        last = rounds.index((qt, qt if causal else 0, c))
                        pe.wait_ge(s["pl"], i * NR + (last + 1))
                        for g in range(G):
                            at = (qt * H + 4 * g + c) * (HD + 1)
                            o = PS[:, 7, at:at + HD + 1]
                            for kb in range(qt + 1 if causal else 1):
                                at_r = (NR * par + rounds.index((qt, kb, c))) % 8
                                for n_, (hp, hv) in enumerate(((0, 0), (1, 0), (0, 1))):
                                    pr = prob16[hp][:, at_r, g, :]
                                    if causal:
                                        ins = pe.matmul(o, pr, vaug[par][:, hv, kb, 4 * g + c, :],
                                                        start=kb == 0 and n_ == 0, stop=kb == qt and n_ == 2)
                                    else:
                                        for w in range(2):
                                            ins = pe.matmul(o[w * WIN:(w + 1) * WIN, :], pr[:, w * WIN:(w + 1) * WIN],
                                                            vaug[par][:, hv, 2 * qt + w, 4 * g + c, :],
                                                            start=n_ == 0, stop=n_ == 2, skip_group_check=True)
                        ins.then_inc(s["pv"], 1)

                    def turn_maxima(i, qt):
                        if qt == 1:
                            if causal:
                                pe.wait_ge(s["mn"], i + 1)
                            else:
                                pe.wait_ge(s["mx"], (i + 1) * NR)
                            pe.wait_ge(s["qm"], i * 2 + 1)
                        else:
                            pe.wait_ge(s["mx"], i * NR + 4)
                            if positive(i - 1):
                                pe.wait_ge(s["atS"], i - 1)
                        for g in range(G):
                            ins = pe.matmul(PS[:, 4, g * P:(g + 1) * P],
                                            mpad[:, qt, g, :, :].rearrange("p j s -> p (j s)"), ident16[:],
                                            start=True, stop=True)
                        ins.then_inc(s["mt"], 1)

                    after = ({1: (0, 0), 2: (0, 1), 3: (0, 2), 4: (0, 3), 6: (1, 0), 8: (1, 1), 10: (1, 2)} if causal else
                             {1: (0, 0), 2: (0, 1), 3: (0, 2), 4: (0, 3), 5: (1, 0), 6: (1, 1), 7: (1, 2)})

                    def step(item):
                        prev, now, nxt, nn = (item(ahead) for ahead in (-1, 0, 1, 2))
                        for r in range(2):
                            if nxt:
                                queries_keys(*nxt, 2 + r)
                            if now:
                                scores_turned(*now, 2 + r)
                        if nxt:
                            i, _ = nxt
                            pe.wait_ge(s["qk16"], i * 4 + 3)
                            for t in range(NV):
                                lo = PAD + t * P if causal else t * WIN
                                o = PS[:, 5, t * P:(t + 1) * P]
                                pe.matmul(o, xTp[:, lo:lo + P], wv[a][:], start=True, stop=False)
                                ins = pe.matmul(o, valid[:, lo:lo + P], bv[a][:], start=False, stop=True)
                            ins.then_inc(s["v"], 1)
                        if prev:
                            i, _ = prev
                            pe.wait_ge(s["at"], i + 1)
                            if now:
                                pe.wait_ge(s["qm"], (i + 2) * 2)
                            for t in range(2):
                                ins = pe.transpose(PS[:, 4, t * P:(t + 1) * P], att[:, t, :], ident[:])
                            ins.then_inc(s["atT"], 1)
                        if nn:
                            i, par = nn
                            pe.wait_ge(s["xn"], (i + 1) * 2)
                            if positive(i - 1):
                                pe.wait_ge(s["qm"], (i - 1) * 2)
                            for t in range(2):
                                ins = pe.transpose(PS[:, 4, SEQ + t * P:SEQ + (t + 1) * P], xn[:, 2 * par + t, 0:P], ident[:])
                            ins.then_inc(s["tr"], 1)
                        for r in range(NR):
                            if nxt:
                                scores(*nxt, r)
                            if now and r + LEAD < NR:
                                scores_turned(*now, r + LEAD)
                            if now and r in after:
                                weighted(*now, *after[r])
                            if r == place["project"] and prev:
                                i, _ = prev
                                pe.wait_ge(s["atS"], i + 1)
                                for t in range(2):
                                    o = PS[:, 6, t * P:(t + 1) * P]
                                    pe.matmul(o, attT[:, t, :], wp[a][:], start=True, stop=False)
                                    ins = pe.matmul(o, ones1[:], bp[a][:], start=False, stop=True)
                                ins.then_inc(s["pj"], 1)
                            if nn and r in place["products"]:
                                queries_keys(*nn, place["products"].index(r))
                            if r == place["turn"] and nxt:
                                if nn:
                                    pe.wait_ge(s["xt"], nn[0] + 1)
                                turn_maxima(nxt[0], 0)
                        if nxt:
                            scores_turned(*nxt, 0)
                            scores_turned(*nxt, 1)
                            turn_maxima(nxt[0], 1)
                        if now:
                            weighted(*now, 1, 3)

                    sequences(pe, step)
                else:
                    pe.wait_ge(ld["f1"], 16 * len(LOADS["f1"]))
                    logits(s, m, 6, router_w, "xt")
                    pe.wait_ge(s["oh"], m + 1)
                    pe.matmul(PS[:, 2, 0:E], onesb[:], ohsum[:, 0, :], start=True, stop=True)
                    pe.matmul(PS[0:2 * E, 4, 0:1], ohsum[:].rearrange("p a e -> p (a e)"), onesb[:, 0:1],
                              start=True, stop=True)
                    oh = onehot[:].rearrange("p t e -> p (t e)")
                    for back in range(1, NT):
                        pe.matmul(PS[:, 3, back * E:NT * E], onesb[:], oh[:, 0:(NT - back) * E],
                                  start=back == 1, stop=False, skip_group_check=True)
                    pe.matmul(PS[:, 3, 0:NT * E], trib[:], oh, start=False, stop=True,
                              skip_group_check=True).then_inc(s["cnt"], 1)
                    pe.wait_ge(s["ntT"], m + 1)
                    pe.matmul(PS[0:2 * E, 4, 0:1], tri_incl, ntT[:], start=True, stop=True)
                    pe.matmul(PS[0:2 * E, 4, 1:2], tri_excl, ntT[:], start=True, stop=True).then_inc(s["incl"], 1)
                    pe.wait_ge(s["ohT"], m + 1)
                    pe.matmul(PS[0:1, 4, 0:NS], eid_col, ohT[:], start=True, stop=True).then_inc(s["eidp"], 1)
                    pe.wait_ge(s["eid"], m + 1)
                    pe.wait_ge(s_c1, 1)
                    pe.wait_ge(s_stage_l, E)

                    vh = v1h[:].rearrange("p e f -> p (e f)")
                    vl = v1l[:].rearrange("p e f -> p (e f)")
                    v2_ = v2[:].rearrange("p e q c -> p (e q c)")

                    def turn_rows(i, par, k, first):
                        pe.wait_ge(s[f"xld{par}"], (NTP[par] * m + k + 1) * 16)
                        pe.transpose(PS[:, par, 0:P], xg[:, par, :], ident[:]).then_inc(s["trx"], 1)

                    def up(i, par, k, first):
                        e = pe.value_load(eid[0:1, bass.ds(i, 1)], min_val=0, max_val=E - 1)
                        pe.wait_ge(s["xl"], NS * m + i + 1)
                        pe.wait_ge(s["ohu"], NS * m + i + 1)
                        if not first:
                            pe.wait_ge(s["h"], NS * m + i - 1)
                        for half, bank in ((1, 4 + par), (0, 2 + par)):
                            at = e * (2 * HID) + half * HID
                            o = PS[:, bank, :]
                            pe.matmul(o, oh_up[:, par, :], c1hl[:, half * HID:(half + 1) * HID],
                                      start=True, stop=False)
                            pe.matmul(o, xgh[:, par, :], vh[:, bass.ds(at, HID)], start=False, stop=False)
                            pe.matmul(o, xgl[:, par, :], vh[:, bass.ds(at, HID)], start=False, stop=False)
                            ins = pe.matmul(o, xgh[:, par, :], vl[:, bass.ds(at, HID)], start=False, stop=True)
                        ins.then_inc(s["up"], 1)

                    def turn_hidden(i, par, k, first):
                        pe.wait_ge(s["h"], NS * m + i + 1)
                        if not first or par == 1:
                            pe.wait_ge(s["hT"], NS * m + i)
                        for q in range(4):
                            ins = pe.transpose(PS[:, 6, q * P:(q + 1) * P], hid[:, par, q * P:(q + 1) * P], ident[:])
                        ins.then_inc(s["trh"], 1)

                    def down(i, par, k, first):
                        e = pe.value_load(eid[0:1, bass.ds(i, 1)], min_val=0, max_val=E - 1)
                        pe.wait_ge(s["hT"], NS * m + i + 1)
                        pe.wait_ge(s["ohd"], NS * m + i + 1)
                        if not first or par == 1:
                            pe.wait_ge(s["y"], NS * m + i)
                        for q in range(4):
                            pe.matmul(PS[:, 7, 0:P], hT[:, par, q * P:(q + 1) * P],
                                      v2_[:, bass.ds(e * HID + q * P, P)], start=q == 0, stop=False)
                        pe.matmul(PS[:, 7, 0:P], oh_down[:, par, :], c2[:], start=False, stop=True)\
                          .then_inc(s["dn"], 1)

                    slot_tiles(pe, [(up, 1), (turn_hidden, 0), (turn_rows, 2), (down, -1)])


def _constants():
    import numpy as np
    f = np.float32
    i = np.arange(P)
    c = {"c_ident": np.eye(P, dtype=f)}
    q, k = i[:, None], i[None, :]
    causal = np.where(k > q, NEG, 0.0)
    w = np.where((k >= q % WIN) & (k < q % WIN + WIN), 0.0, NEG)
    c["c_masks"] = np.stack([causal, causal.T, w, w.T], axis=1).astype(f)
    c["c_tri"] = (q < k).astype(f)
    c["c_em8"] = np.broadcast_to(np.arange(E) - float(E), (P, NT, E)).astype(f)
    c["c_k128"] = np.broadcast_to(float(P) * np.arange(NT), (P, E, NT)).astype(f)
    slot = i % SL
    cols = np.zeros((P, 4), f)
    cols[:, 0] = np.where((slot >= HD) & (slot < 2 * HD), -1, 0)
    cols[:, 1] = np.where((slot >= 2 * HD) & (slot < 3 * HD), -1, 0)
    cols[:, 2] = slot == M_SLOT
    cols[1, 3] = -1
    c["c_cols"] = cols
    v = np.zeros((P, SEQ + 2 * PAD), f)
    v[0, PAD:PAD + SEQ] = 1
    c["c_valid"] = v
    c["c_ids"] = (1 + NT * np.arange(P)[:, None] + np.arange(NT)[None, :]).astype(f)
    c["c_rest"] = (1 + NT * P + P * np.arange(NS)[None, :] + np.arange(P)[:, None]).astype(f)
    e = np.arange(2 * E)
    same = (e[:, None] // E) == (e[None, :] // E)
    c["c_small"] = np.concatenate([
        np.broadcast_to(float(P) * np.arange(16), (2 * E, 16)),
        same & (e[:, None] <= e[None, :]), same & (e[:, None] < e[None, :]),
        np.broadcast_to(np.arange(NS), (2 * E, NS)), np.where(e < E, e, 0)[:, None], -(e >= E)[:, None].astype(f)],
        axis=1).astype(f)
    x = np.zeros((P, SEQ), f)
    x[0:3], x[3] = 1, np.arange(SEQ)
    c["c_addx"] = x
    return c


def _laid_out(i):
    import numpy as np

    def slots(w, b, k0):
        n = w.shape[0]
        pw, pb = np.zeros((n, H, SL), w.dtype), np.zeros((H, SL), w.dtype)
        for r in range(3):
            pw[:, :, r * HD:(r + 1) * HD] = w[:, k0:k0 + P].reshape(n, H, HD)
            pb[:, r * HD:(r + 1) * HD] = b[k0:k0 + P].reshape(H, HD)
        return pw.reshape(n, H * SL), pb.reshape(H * SL)

    def padded(rows):
        return np.concatenate([rows, np.zeros((P - rows.shape[0], *rows.shape[1:]), rows.dtype)])

    a = {"x": i["L0_attn_x"].reshape(NT, P, P).transpose(1, 0, 2)}
    w1 = np.concatenate([i["L0_ffn_rw1"], i["L0_ffn_sw1"]])
    a["w1_0"] = w1.transpose(1, 0, 2).reshape(P, E0 * 2 * P)
    b1 = np.concatenate([i["L0_ffn_rb1"], i["L0_ffn_sb1"]])
    a["b1_0"] = b1.reshape(E0, 2, P).transpose(2, 0, 1)
    a["w2_0"] = np.concatenate([i["L0_ffn_rw2"], i["L0_ffn_sw2"]]).transpose(1, 0, 2)
    a["b2_0"] = np.concatenate([i["L0_ffn_rb2"], i["L0_ffn_sb2"]])
    a["gate_w"], a["gate_b"] = i["L0_ffn_gate_w"], np.broadcast_to(i["L0_ffn_gate_b"], (P, E))
    for n, (w, b, wp, bp) in enumerate([
            (i["L0_attn_W_attn"], i["L0_attn_b_attn"], i["L0_attn_W_proj"], i["L0_attn_b_proj"]),
            (i["L1_attn_Wqkv"].T, i["L1_attn_bqkv"], i["L1_attn_Wout"].T, i["L1_attn_bout"])]):
        qw, qb = slots(w, b, 0)
        kw, kb = slots(w, b, P)
        a[f"wqk_{n}"] = np.stack([qw, kw], axis=1)
        const, slope = np.zeros((2, H, SL), w.dtype), np.zeros((2, H, SL), w.dtype)
        const[1, :, M_SLOT] = 1
        if n == 0:
            const[0, :, 24] = const[1, :, 25] = 1
            slope[1, :, 24] = 2.0 ** -np.arange(1, H + 1)
            slope[0, :, 25] = -slope[1, :, 24]
        b2 = np.stack([qb, kb])
        a[f"add_{n}"] = padded(np.stack([b2, b2, const.reshape(2, -1), slope.reshape(2, -1)]))
        a[f"wv_{n}"], a[f"bv_{n}"] = w[:, 2 * P:], padded(b[None, 2 * P:])
        a[f"wp_{n}"], a[f"bp_{n}"] = wp, padded(bp[None])
    a["router_w"], a["router_b"] = i["L1_ffn_router_w"], np.broadcast_to(i["L1_ffn_router_b"], (P, E))
    a["w1_1"] = i["L1_ffn_w1"].transpose(1, 0, 2)
    a["b1_1"] = i["L1_ffn_b1"]
    a["w2_1"] = i["L1_ffn_w2"].reshape(E, HID // P, P, P).transpose(2, 0, 1, 3)
    a["b2_1"] = i["L1_ffn_b2"]
    return a


def kernel(**inputs):
    import numpy as np
    import concourse.bacc as bacc
    from concourse.bass_utils import run_bass_kernel_spmd

    nc = bacc.Bacc("TRN2", target_bir_lowering=False, num_devices=1)
    arrays, d = {}, {}
    for name, a in {**_laid_out({k: np.asarray(v) for k, v in inputs.items()}), **_constants()}.items():
        a = np.ascontiguousarray(a)
        arrays[f"in_{name}"] = a
        d[name] = nc.dram_tensor(f"in_{name}", a.shape, mybir.dt.from_np(a.dtype), kind="ExternalInput").ap()
    out = nc.dram_tensor("out_x", (P, NT, P), F32, kind="ExternalOutput").ap()
    macaron(nc, d, out)
    r = run_bass_kernel_spmd(nc, [arrays], core_ids=[0])
    got = r.results[0]["out_x"]
    return got.transpose(1, 0, 2).reshape(NB, SEQ, P)
```
